# Optimizing a Trainium2 kernel written in Bass

```python
import numpy as np
import jax
import jax.numpy as jnp

def _softmax(x, axis=-1):
    return jax.nn.softmax(x, axis=axis)

def _gelu(x):
    return jax.nn.gelu(x, approximate=True)

def _silu(x):
    return jax.nn.silu(x)

def _sigmoid(x):
    return jax.nn.sigmoid(x)

def _layernorm(x, axis=-1, eps=1e-05):
    m = jnp.mean(x, axis=axis, keepdims=True)
    v = jnp.var(x, axis=axis, keepdims=True)
    return (x - m) / jnp.sqrt(v + eps)

def _scatter_add(tgt, idx, src, axis=0):
    return tgt.at[idx].add(src)

def _segment_sum(src, seg, n):
    return jax.ops.segment_sum(src, seg, n)
kernel_name = 'mk_perceiver_d2_seqx_r4_fcc7f2'

def setup_inputs(seed: int=0):
    np.random.seed(seed)
    _w = jnp.asarray

    def _rec_inputs():
        import jax
        import jax.numpy as jnp
        _rk = jax.random.key(seed)
        x = 7.22e-05 + 1 * jax.random.normal(jax.random.fold_in(_rk, 1), (32, 64, 256), jnp.float32)
        _lenS = 64 - jax.random.randint(jax.random.fold_in(_rk, 7), (32,), 0, max(1, 64 // 4) + 1, jnp.int32)
        _lenS2 = 256 - jax.random.randint(jax.random.fold_in(_rk, 8), (32,), 0, max(1, 256 // 4) + 1, jnp.int32)
        _ctx_1024P = jax.random.normal(jax.random.fold_in(_rk, 11), (32, 16, 256), jnp.float32)
        _ctx_1024c = jax.random.dirichlet(jax.random.fold_in(_rk, 511), 0.3 * jnp.ones((16,), jnp.float32), (32, 256))
        _ctx_1024t = jnp.einsum('bsk,bkd->bsd', _ctx_1024c, _ctx_1024P)
        _ctx_1024t = _ctx_1024t * jax.lax.rsqrt(jnp.mean(jnp.square(_ctx_1024t)) + 1e-12) * 0.953939
        ctx_1024 = -0.000514642 + 1.00011 * (_ctx_1024t + 0.3 * jax.random.normal(jax.random.fold_in(_rk, 611), (32, 256, 256), jnp.float32))
        itok_BxS_0_511 = jax.random.randint(jax.random.fold_in(_rk, 12), (32, 64), 0, 128, jnp.int32)
        fside_SxS2_0 = 0.000376506 + 0.999991 * jax.random.normal(jax.random.fold_in(_rk, 13), (64, 256), jnp.float32)
        return (x, ctx_1024, itok_BxS_0_511, fside_SxS2_0)
    x, ctx_1024, itok_BxS_0_511, fside_SxS2_0 = _rec_inputs()

    def _L0_xattn_setup():
        import jax, jax.numpy as jnp
        import numpy as np
        Q_DIM, KV_DIM = (256, 256)
        H, HD, KVC, QC, R = (16, 64, 64, 96, 64)
        LOOKBACK = 2
        B, LQ, LK = (4, 512, 128)

        def _rope(x, pos):
            r = x.shape[-1]
            half = r // 2
            inv = 1.0 / 10000.0 ** (jnp.arange(half, dtype=jnp.float32) / half)
            ang = pos[..., None].astype(jnp.float32) * inv
            cos, sin = (jnp.cos(ang), jnp.sin(ang))
            x1, x2 = (x[..., :half], x[..., half:])
            return jnp.concatenate([x1 * cos - x2 * sin, x1 * sin + x2 * cos], axis=-1)
        key = jax.random.key(seed)
        ks = jax.random.split(key, 11)
        w = lambda k, shape: jax.random.normal(k, shape, jnp.float32) / np.sqrt(shape[0]).astype(np.float32)
        return {'q': jax.random.normal(ks[0], (B, LQ, Q_DIM), jnp.float32), 'kv': jax.random.normal(ks[1], (B, LK, KV_DIM), jnp.float32), 'seg_id': jnp.sort(jax.random.randint(ks[2], (B, LQ), 0, LK), axis=-1), 'w_kv_comp': w(ks[3], (KV_DIM, KVC)), 'w_q_down': w(ks[4], (Q_DIM, QC)), 'w_q_up': w(ks[5], (QC, H * HD)), 'w_q_rope': w(ks[6], (QC, H * R)), 'w_k_up': w(ks[7], (KVC, H * HD)), 'w_k_rope': w(ks[8], (KVC, R)), 'w_v_up': w(ks[9], (KVC, H * HD)), 'w_out': w(ks[10], (H * HD, Q_DIM))}
    _L0_xattn_all = _L0_xattn_setup()
    _L0_xattn_in = {k: v for k, v in _L0_xattn_all.items() if k in ('w_kv_comp', 'w_q_down', 'w_q_up', 'w_q_rope', 'w_k_up', 'w_k_rope', 'w_v_up', 'w_out')}
    del _L0_xattn_all

    def _L0_attn_setup():
        import jax, jax.numpy as jnp
        import numpy as np
        B, L, D_MODEL, D_INNER, D_STATE, DT_RANK, K = (2, 256, 256, 512, 16, 64, 4)
        key = jax.random.key(seed)
        ks = jax.random.split(key, 8)
        sc = lambda n: 1.0 / np.sqrt(n)
        return {'x': jax.random.normal(ks[0], (B, L, D_MODEL), jnp.float32), 'W_in': jax.random.normal(ks[1], (2 * D_INNER, D_MODEL), jnp.float32) * sc(D_MODEL), 'conv_w': jax.random.normal(ks[2], (D_INNER, K), jnp.float32) * sc(K), 'conv_b': jax.random.normal(ks[3], (D_INNER,), jnp.float32) * 0.1, 'W_x': jax.random.normal(ks[4], (DT_RANK + 2 * D_STATE, D_INNER), jnp.float32) * sc(D_INNER), 'W_dt': jax.random.normal(ks[5], (D_INNER, DT_RANK), jnp.float32) * sc(DT_RANK), 'b_dt': jax.random.normal(ks[6], (D_INNER,), jnp.float32) * 0.1, 'A_log': jnp.log(jnp.tile(jnp.arange(1.0, D_STATE + 1.0, dtype=jnp.float32)[None, :], (D_INNER, 1))), 'Dp': jnp.ones((D_INNER,), jnp.float32), 'W_out': jax.random.normal(ks[7], (D_MODEL, D_INNER), jnp.float32) * sc(D_INNER)}
    _L0_attn_all = _L0_attn_setup()
    _L0_attn_in = {k: v for k, v in _L0_attn_all.items() if k in ('W_in', 'conv_w', 'conv_b', 'W_x', 'W_dt', 'b_dt', 'A_log', 'Dp', 'W_out')}
    del _L0_attn_all

    def _L0_ffn_setup():
        import jax, jax.numpy as jnp
        import numpy as np
        E = 64
        K = 6
        CAP = 128
        ROUTE_SCALE = 1.0
        key = jax.random.key(seed)
        ks = jax.random.split(key, 9)
        B, S, D, I = (2, 256, 256, 176)
        SI = 2 * I
        s = 0.02
        return {'x': jax.random.normal(ks[0], (B, S, D), jnp.float32), 'gate_w': jax.random.normal(ks[1], (E, D), jnp.float32) * s, 'gate_b': jnp.zeros((E,), jnp.float32), 'w1': jax.random.normal(ks[2], (E, I, D), jnp.float32) * s, 'w2': jax.random.normal(ks[3], (E, D, I), jnp.float32) * s, 'w3': jax.random.normal(ks[4], (E, I, D), jnp.float32) * s, 'ws1': jax.random.normal(ks[5], (SI, D), jnp.float32) * s, 'ws2': jax.random.normal(ks[6], (D, SI), jnp.float32) * s, 'ws3': jax.random.normal(ks[7], (SI, D), jnp.float32) * s}
    _L0_ffn_all = _L0_ffn_setup()
    _L0_ffn_in = {k: v for k, v in _L0_ffn_all.items() if k in ('gate_w', 'gate_b', 'w1', 'w2', 'w3', 'ws1', 'ws2', 'ws3')}
    del _L0_ffn_all

    def _L1_xattn_setup():
        import jax, jax.numpy as jnp
        import numpy as np
        D_MODEL = 256
        N_HEAD = 16
        D_QKV = D_MODEL // N_HEAD
        key = jax.random.key(seed)
        ks = jax.random.split(key, 12)
        B, S = (2, 512)
        scale = 1.0 / np.sqrt(D_MODEL)
        inp = {'src': jax.random.normal(ks[0], (B, S, D_MODEL), jnp.float32), 'tgt': jax.random.normal(ks[1], (B, S, D_MODEL), jnp.float32), 'mask': jax.random.normal(ks[2], (S, S), jnp.float32), 'Wq': jax.random.normal(ks[3], (N_HEAD, D_MODEL, D_QKV), jnp.float32) * scale, 'bq': jax.random.normal(ks[4], (N_HEAD, D_QKV), jnp.float32) * scale, 'Wk': jax.random.normal(ks[5], (N_HEAD, D_MODEL, D_QKV), jnp.float32) * scale, 'bk': jax.random.normal(ks[6], (N_HEAD, D_QKV), jnp.float32) * scale, 'Wv': jax.random.normal(ks[7], (N_HEAD, D_MODEL, D_QKV), jnp.float32) * scale, 'bv': jax.random.normal(ks[8], (N_HEAD, D_QKV), jnp.float32) * scale, 'Wo': jax.random.normal(ks[9], (D_MODEL, D_MODEL), jnp.float32) * scale, 'bo': jax.random.normal(ks[10], (D_MODEL,), jnp.float32) * scale}
        return inp
    _L1_xattn_all = _L1_xattn_setup()
    _L1_xattn_in = {k: v for k, v in _L1_xattn_all.items() if k in ('Wq', 'bq', 'Wk', 'bk', 'Wv', 'bv', 'Wo', 'bo')}
    del _L1_xattn_all

    def _L1_attn_setup():
        import jax, jax.numpy as jnp
        import numpy as np
        D_MODEL = 256
        N_HEADS = 16
        HEAD_DIM = D_MODEL // N_HEADS
        ROPE_BASE = 10000.0

        def _rope(q, k):
            S, Dh = (q.shape[1], q.shape[-1])
            inv_freq = 1.0 / ROPE_BASE ** (jnp.arange(0, Dh, 2, dtype=jnp.float32) / Dh)
            t = jnp.arange(S, dtype=jnp.float32)
            freqs = jnp.outer(t, inv_freq)
            emb = jnp.concatenate([freqs, freqs], axis=-1)
            cos = jnp.cos(emb)[None, :, None, :]
            sin = jnp.sin(emb)[None, :, None, :]

            def rotate_half(v):
                v1, v2 = (v[..., :Dh // 2], v[..., Dh // 2:])
                return jnp.concatenate([-v2, v1], axis=-1)
            return (q * cos + rotate_half(q) * sin, k * cos + rotate_half(k) * sin)
        key = jax.random.key(seed)
        ks = jax.random.split(key, 5)
        B, S = (1, 1024)
        scale = 1.0 / np.sqrt(D_MODEL)
        x = jax.random.normal(ks[0], (B, S, D_MODEL), dtype=jnp.float32)
        Wq = jax.random.normal(ks[1], (D_MODEL, D_MODEL), dtype=jnp.float32) * scale
        Wk = jax.random.normal(ks[2], (D_MODEL, D_MODEL), dtype=jnp.float32) * scale
        Wv = jax.random.normal(ks[3], (D_MODEL, D_MODEL), dtype=jnp.float32) * scale
        Wo = jax.random.normal(ks[4], (D_MODEL, D_MODEL), dtype=jnp.float32) * scale
        return {'x': x, 'Wq': Wq, 'Wk': Wk, 'Wv': Wv, 'Wo': Wo}
    _L1_attn_all = _L1_attn_setup()
    _L1_attn_in = {k: v for k, v in _L1_attn_all.items() if k in ('Wq', 'Wk', 'Wv', 'Wo')}
    del _L1_attn_all

    def _L1_ffn_setup():
        import jax, jax.numpy as jnp
        import numpy as np
        N_GROUP = 8
        TOPK_GROUP = 4
        TOPK = 8
        ROUTED_SCALE = 2.5
        B, S, D, F, E = (4, 512, 256, 128, 64)

        def _route(x, w_router, b_router):
            scores = jax.nn.sigmoid(jnp.einsum('bsd,de->bse', x, w_router)).astype(jnp.float32)
            swb = scores + b_router
            e = scores.shape[-1]
            group_scores = jnp.sum(jax.lax.top_k(swb.reshape(swb.shape[:-1] + (N_GROUP, -1)), 2)[0], axis=-1)
            group_idx = jax.lax.top_k(group_scores, TOPK_GROUP)[1]
            mask = jnp.any(jnp.arange(N_GROUP)[:, None] == group_idx[..., None, :], axis=-1)
            mask = jnp.repeat(mask, e // N_GROUP, axis=-1)
            masked_scores = jnp.where(mask, swb, 0.0)
            topk_idx = jax.lax.top_k(masked_scores, TOPK)[1]
            topk_w = jnp.take_along_axis(scores, topk_idx, axis=-1).astype(jnp.float32)
            topk_w = ROUTED_SCALE * topk_w / (jnp.sum(topk_w, axis=-1)[..., None] + 1e-20)
            return (topk_w, topk_idx)

        def _moe_forward(x, w_router, b_router, we_gate, we_up, we_down, ws_gate, ws_up, ws_down):
            b, s, d = x.shape
            e = we_gate.shape[0]
            topk_w, topk_idx = _route(x, w_router, b_router)
            x_flat = x.reshape(-1, d)
            idx_flat = topk_idx.reshape(-1)
            sort = jnp.argsort(idx_flat)
            tok = sort // TOPK
            x_sorted = x_flat[tok]
            group_sizes = jnp.bincount(idx_flat, length=e).astype(jnp.int32)
            g = jax.lax.ragged_dot(x_sorted, we_gate, group_sizes)
            u = jax.lax.ragged_dot(x_sorted, we_up, group_sizes)
            o = jax.lax.ragged_dot(jax.nn.silu(g) * u, we_down, group_sizes)
            w_sorted = topk_w.reshape(-1)[sort].astype(o.dtype)
            y = jnp.zeros_like(x_flat).at[tok].add(o * w_sorted[:, None])
            y = y.reshape(b, s, d)
            shared = jnp.einsum('btf,fd->btd', jax.nn.silu(jnp.einsum('btd,df->btf', x, ws_gate)) * jnp.einsum('btd,df->btf', x, ws_up), ws_down)
            return y + shared
        key = jax.random.key(seed)
        ks = jax.random.split(key, 10)
        sd = 1.0 / np.sqrt(D)
        sf = 1.0 / np.sqrt(F)
        return {'x': jax.random.normal(ks[0], (B, S, D), jnp.float32), 'w_router': jax.random.normal(ks[1], (D, E), jnp.float32) * sd, 'b_router': jax.random.normal(ks[2], (E,), jnp.float32) * 0.1, 'we_gate': jax.random.normal(ks[3], (E, D, F), jnp.float32) * sd, 'we_up': jax.random.normal(ks[4], (E, D, F), jnp.float32) * sd, 'we_down': jax.random.normal(ks[5], (E, F, D), jnp.float32) * sf, 'ws_gate': jax.random.normal(ks[6], (D, F), jnp.float32) * sd, 'ws_up': jax.random.normal(ks[7], (D, F), jnp.float32) * sd, 'ws_down': jax.random.normal(ks[8], (F, D), jnp.float32) * sf}
    _L1_ffn_all = _L1_ffn_setup()
    _L1_ffn_in = {k: v for k, v in _L1_ffn_all.items() if k in ('w_router', 'b_router', 'we_gate', 'we_up', 'we_down', 'ws_gate', 'ws_up', 'ws_down')}
    del _L1_ffn_all
    return {'x': x, 'ctx_1024': ctx_1024, 'itok_BxS_0_511': itok_BxS_0_511, 'fside_SxS2_0': fside_SxS2_0, 'L0_xattn_w_kv_comp': _L0_xattn_in['w_kv_comp'], 'L0_xattn_w_q_down': _L0_xattn_in['w_q_down'], 'L0_xattn_w_q_up': _L0_xattn_in['w_q_up'], 'L0_xattn_w_q_rope': _L0_xattn_in['w_q_rope'], 'L0_xattn_w_k_up': _L0_xattn_in['w_k_up'], 'L0_xattn_w_k_rope': _L0_xattn_in['w_k_rope'], 'L0_xattn_w_v_up': _L0_xattn_in['w_v_up'], 'L0_xattn_w_out': _L0_xattn_in['w_out'], 'L0_attn_W_in': _L0_attn_in['W_in'], 'L0_attn_conv_w': _L0_attn_in['conv_w'], 'L0_attn_conv_b': _L0_attn_in['conv_b'], 'L0_attn_W_x': _L0_attn_in['W_x'], 'L0_attn_W_dt': _L0_attn_in['W_dt'], 'L0_attn_b_dt': _L0_attn_in['b_dt'], 'L0_attn_A_log': _L0_attn_in['A_log'], 'L0_attn_Dp': _L0_attn_in['Dp'], 'L0_attn_W_out': _L0_attn_in['W_out'], 'L0_ffn_gate_w': _L0_ffn_in['gate_w'], 'L0_ffn_gate_b': _L0_ffn_in['gate_b'], 'L0_ffn_w1': _L0_ffn_in['w1'], 'L0_ffn_w2': _L0_ffn_in['w2'], 'L0_ffn_w3': _L0_ffn_in['w3'], 'L0_ffn_ws1': _L0_ffn_in['ws1'], 'L0_ffn_ws2': _L0_ffn_in['ws2'], 'L0_ffn_ws3': _L0_ffn_in['ws3'], 'L1_xattn_Wq': _L1_xattn_in['Wq'], 'L1_xattn_bq': _L1_xattn_in['bq'], 'L1_xattn_Wk': _L1_xattn_in['Wk'], 'L1_xattn_bk': _L1_xattn_in['bk'], 'L1_xattn_Wv': _L1_xattn_in['Wv'], 'L1_xattn_bv': _L1_xattn_in['bv'], 'L1_xattn_Wo': _L1_xattn_in['Wo'], 'L1_xattn_bo': _L1_xattn_in['bo'], 'L1_attn_Wq': _L1_attn_in['Wq'], 'L1_attn_Wk': _L1_attn_in['Wk'], 'L1_attn_Wv': _L1_attn_in['Wv'], 'L1_attn_Wo': _L1_attn_in['Wo'], 'L1_ffn_w_router': _L1_ffn_in['w_router'], 'L1_ffn_b_router': _L1_ffn_in['b_router'], 'L1_ffn_we_gate': _L1_ffn_in['we_gate'], 'L1_ffn_we_up': _L1_ffn_in['we_up'], 'L1_ffn_we_down': _L1_ffn_in['we_down'], 'L1_ffn_ws_gate': _L1_ffn_in['ws_gate'], 'L1_ffn_ws_up': _L1_ffn_in['ws_up'], 'L1_ffn_ws_down': _L1_ffn_in['ws_down']}

def reference(x, ctx_1024, itok_BxS_0_511, fside_SxS2_0, L0_xattn_w_kv_comp, L0_xattn_w_q_down, L0_xattn_w_q_up, L0_xattn_w_q_rope, L0_xattn_w_k_up, L0_xattn_w_k_rope, L0_xattn_w_v_up, L0_xattn_w_out, L0_attn_W_in, L0_attn_conv_w, L0_attn_conv_b, L0_attn_W_x, L0_attn_W_dt, L0_attn_b_dt, L0_attn_A_log, L0_attn_Dp, L0_attn_W_out, L0_ffn_gate_w, L0_ffn_gate_b, L0_ffn_w1, L0_ffn_w2, L0_ffn_w3, L0_ffn_ws1, L0_ffn_ws2, L0_ffn_ws3, L1_xattn_Wq, L1_xattn_bq, L1_xattn_Wk, L1_xattn_bk, L1_xattn_Wv, L1_xattn_bv, L1_xattn_Wo, L1_xattn_bo, L1_attn_Wq, L1_attn_Wk, L1_attn_Wv, L1_attn_Wo, L1_ffn_w_router, L1_ffn_b_router, L1_ffn_we_gate, L1_ffn_we_up, L1_ffn_we_down, L1_ffn_ws_gate, L1_ffn_ws_up, L1_ffn_ws_down):
    import jax
    import jax.numpy as jnp

    def _L0_xattn_ref(q, kv, seg_id, w_kv_comp, w_q_down, w_q_up, w_q_rope, w_k_up, w_k_rope, w_v_up, w_out):
        import jax, jax.numpy as jnp
        import numpy as np
        Q_DIM, KV_DIM = (256, 256)
        H, HD, KVC, QC, R = (16, 64, 64, 96, 64)
        LOOKBACK = 2
        B, LQ, LK = (4, 512, 128)

        def _rope(x, pos):
            r = x.shape[-1]
            half = r // 2
            inv = 1.0 / 10000.0 ** (jnp.arange(half, dtype=jnp.float32) / half)
            ang = pos[..., None].astype(jnp.float32) * inv
            cos, sin = (jnp.cos(ang), jnp.sin(ang))
            x1, x2 = (x[..., :half], x[..., half:])
            return jnp.concatenate([x1 * cos - x2 * sin, x1 * sin + x2 * cos], axis=-1)
        b, lq, _ = q.shape
        lk = kv.shape[1]
        kv_c = kv @ w_kv_comp
        qc = q @ w_q_down
        q_nope = (qc @ w_q_up).reshape(b, lq, H, HD)
        q_rope = (qc @ w_q_rope).reshape(b, lq, H, R)
        q_rope = _rope(q_rope, jnp.arange(lq)[None, :, None])
        k_nope = (kv_c @ w_k_up).reshape(b, lk, H, HD)
        k_rope = _rope(kv_c @ w_k_rope, jnp.arange(lk)[None, :])
        v = (kv_c @ w_v_up).reshape(b, lk, H, HD)
        scale = 1.0 / np.sqrt(HD + R).astype(np.float32)
        scores = (jnp.einsum('bqhd,bkhd->bhqk', q_nope, k_nope) + jnp.einsum('bqhr,bkr->bhqk', q_rope, k_rope)) * scale
        k_idx = jnp.arange(lk)[None, None, :]
        q_seg = seg_id[:, :, None]
        good = (k_idx <= q_seg) & (k_idx >= q_seg - LOOKBACK)
        neg = jnp.finfo(scores.dtype).min
        scores = jnp.where(good[:, None, :, :], scores, neg)
        attn = jax.nn.softmax(scores, axis=-1)
        out = jnp.einsum('bhqk,bkhd->bqhd', attn, v).reshape(b, lq, H * HD)
        return out @ w_out

    def _L0_attn_ref(x, W_in, conv_w, conv_b, W_x, W_dt, b_dt, A_log, Dp, W_out):
        import jax, jax.numpy as jnp
        import numpy as np
        B, L, D_MODEL, D_INNER, D_STATE, DT_RANK, K = (2, 256, 256, 512, 16, 64, 4)
        xz = x @ W_in.T
        xc, z = jnp.split(xz, 2, axis=-1)
        d_inner = xc.shape[-1]
        k = conv_w.shape[1]
        xt = xc.transpose(0, 2, 1)
        yt = jax.lax.conv_general_dilated(xt, conv_w[:, None, :], window_strides=(1,), padding=[(k - 1, 0)], dimension_numbers=('NCH', 'OIH', 'NCH'), feature_group_count=d_inner)
        xc = yt.transpose(0, 2, 1) + conv_b
        xc = jax.nn.silu(xc)
        dBC = xc @ W_x.T
        dt_rank = W_dt.shape[1]
        d_state = A_log.shape[1]
        delta = dBC[..., :dt_rank]
        Bm = dBC[..., dt_rank:dt_rank + d_state]
        Cm = dBC[..., dt_rank + d_state:]
        delta = jax.nn.softplus(delta @ W_dt.T + b_dt)
        A = -jnp.exp(A_log)
        deltaA = jnp.exp(delta[..., None] * A)
        BX = delta[..., None] * Bm[:, :, None, :] * xc[..., None]

        def combine(e1, e2):
            a1, x1 = e1
            a2, x2 = e2
            return (a1 * a2, a2 * x1 + x2)
        _, hs = jax.lax.associative_scan(combine, (deltaA, BX), axis=1)
        y = jnp.einsum('bldn,bln->bld', hs, Cm) + Dp * xc
        out = y * jax.nn.silu(z) @ W_out.T
        return out

    def _L0_ffn_ref(x, gate_w, gate_b, w1, w2, w3, ws1, ws2, ws3):
        import jax, jax.numpy as jnp
        import numpy as np
        E = 64
        K = 6
        CAP = 128
        ROUTE_SCALE = 1.0
        shape = x.shape
        D = shape[-1]
        xf = x.reshape(-1, D)
        T = xf.shape[0]
        scores = jax.nn.softmax(xf @ gate_w.T, axis=-1)
        _, idx = jax.lax.top_k(scores + gate_b, K)
        weights = jnp.take_along_axis(scores, idx, axis=1) * ROUTE_SCALE
        flat_e = idx.reshape(-1)
        order = jnp.argsort(flat_e)
        se = flat_e[order]
        counts = jnp.bincount(flat_e, length=E)
        starts = jnp.cumsum(counts) - counts
        pos = jnp.arange(T * K) - starts[se]
        tok = order // K
        xb = jnp.zeros((E, CAP, D), xf.dtype).at[se, pos].set(xf[tok], mode='drop')
        h = jax.nn.silu(jnp.einsum('ecd,eid->eci', xb, w1)) * jnp.einsum('ecd,eid->eci', xb, w3)
        yb = jnp.einsum('eci,edi->ecd', h, w2)
        valid = (pos < CAP).astype(xf.dtype)
        contrib = yb[se, jnp.minimum(pos, CAP - 1)]
        wf = weights.reshape(-1)[order] * valid
        y = jnp.zeros_like(xf).at[tok].add(contrib * wf[:, None])
        z = jax.nn.silu(xf @ ws1.T) * (xf @ ws3.T) @ ws2.T
        return (y + z).reshape(shape)

    def _L1_xattn_ref(src, tgt, mask, Wq, bq, Wk, bk, Wv, bv, Wo, bo):
        import jax, jax.numpy as jnp
        import numpy as np
        D_MODEL = 256
        N_HEAD = 16
        D_QKV = D_MODEL // N_HEAD
        q = jnp.einsum('bsd,hdk->bhsk', tgt, Wq) + bq[None, :, None, :]
        k = jnp.einsum('bsd,hdk->bhsk', src, Wk) + bk[None, :, None, :]
        v = jnp.einsum('bsd,hdk->bhsk', src, Wv) + bv[None, :, None, :]
        scores = jnp.einsum('bhtk,bhsk->bhts', q, k) + mask[None, None, :, :]
        attn = jax.nn.softmax(scores * D_QKV ** (-0.5), axis=-1)
        out = jnp.einsum('bhts,bhsk->bhtk', attn, v)
        B, H, T, K = out.shape
        out = out.transpose(0, 2, 1, 3).reshape(B, T, H * K)
        return out @ Wo.T if False else jnp.einsum('btd,ed->bte', out, Wo) + bo

    def _L1_attn_ref(x, Wq, Wk, Wv, Wo):
        import jax, jax.numpy as jnp
        import numpy as np
        D_MODEL = 256
        N_HEADS = 16
        HEAD_DIM = D_MODEL // N_HEADS
        ROPE_BASE = 10000.0

        def _rope(q, k):
            S, Dh = (q.shape[1], q.shape[-1])
            inv_freq = 1.0 / ROPE_BASE ** (jnp.arange(0, Dh, 2, dtype=jnp.float32) / Dh)
            t = jnp.arange(S, dtype=jnp.float32)
            freqs = jnp.outer(t, inv_freq)
            emb = jnp.concatenate([freqs, freqs], axis=-1)
            cos = jnp.cos(emb)[None, :, None, :]
            sin = jnp.sin(emb)[None, :, None, :]

            def rotate_half(v):
                v1, v2 = (v[..., :Dh // 2], v[..., Dh // 2:])
                return jnp.concatenate([-v2, v1], axis=-1)
            return (q * cos + rotate_half(q) * sin, k * cos + rotate_half(k) * sin)
        B, S, _ = x.shape
        H, Dh = (N_HEADS, HEAD_DIM)
        q = (x @ Wq.T).reshape(B, S, H, Dh)
        k = (x @ Wk.T).reshape(B, S, H, Dh)
        v = (x @ Wv.T).reshape(B, S, H, Dh)
        q, k = _rope(q, k)
        scale = 1.0 / np.sqrt(Dh)
        scores = jnp.einsum('bqhd,bkhd->bhqk', q, k) * scale
        causal = jnp.triu(jnp.ones((S, S), dtype=bool), k=1)
        scores = jnp.where(causal, -jnp.inf, scores)
        attn = jax.nn.softmax(scores, axis=-1)
        out = jnp.einsum('bhqk,bkhd->bqhd', attn, v).reshape(B, S, H * Dh)
        return out @ Wo.T

    def _L1_ffn_ref(x, w_router, b_router, we_gate, we_up, we_down, ws_gate, ws_up, ws_down):
        import jax, jax.numpy as jnp
        import numpy as np
        N_GROUP = 8
        TOPK_GROUP = 4
        TOPK = 8
        ROUTED_SCALE = 2.5
        B, S, D, F, E = (4, 512, 256, 128, 64)

        def _route(x, w_router, b_router):
            scores = jax.nn.sigmoid(jnp.einsum('bsd,de->bse', x, w_router)).astype(jnp.float32)
            swb = scores + b_router
            e = scores.shape[-1]
            group_scores = jnp.sum(jax.lax.top_k(swb.reshape(swb.shape[:-1] + (N_GROUP, -1)), 2)[0], axis=-1)
            group_idx = jax.lax.top_k(group_scores, TOPK_GROUP)[1]
            mask = jnp.any(jnp.arange(N_GROUP)[:, None] == group_idx[..., None, :], axis=-1)
            mask = jnp.repeat(mask, e // N_GROUP, axis=-1)
            masked_scores = jnp.where(mask, swb, 0.0)
            topk_idx = jax.lax.top_k(masked_scores, TOPK)[1]
            topk_w = jnp.take_along_axis(scores, topk_idx, axis=-1).astype(jnp.float32)
            topk_w = ROUTED_SCALE * topk_w / (jnp.sum(topk_w, axis=-1)[..., None] + 1e-20)
            return (topk_w, topk_idx)

        def _moe_forward(x, w_router, b_router, we_gate, we_up, we_down, ws_gate, ws_up, ws_down):
            b, s, d = x.shape
            e = we_gate.shape[0]
            topk_w, topk_idx = _route(x, w_router, b_router)
            x_flat = x.reshape(-1, d)
            idx_flat = topk_idx.reshape(-1)
            sort = jnp.argsort(idx_flat)
            tok = sort // TOPK
            x_sorted = x_flat[tok]
            group_sizes = jnp.bincount(idx_flat, length=e).astype(jnp.int32)
            g = jax.lax.ragged_dot(x_sorted, we_gate, group_sizes)
            u = jax.lax.ragged_dot(x_sorted, we_up, group_sizes)
            o = jax.lax.ragged_dot(jax.nn.silu(g) * u, we_down, group_sizes)
            w_sorted = topk_w.reshape(-1)[sort].astype(o.dtype)
            y = jnp.zeros_like(x_flat).at[tok].add(o * w_sorted[:, None])
            y = y.reshape(b, s, d)
            shared = jnp.einsum('btf,fd->btd', jax.nn.silu(jnp.einsum('btd,df->btf', x, ws_gate)) * jnp.einsum('btd,df->btf', x, ws_up), ws_down)
            return y + shared
        return _moe_forward(x, w_router, b_router, we_gate, we_up, we_down, ws_gate, ws_up, ws_down)
    x = x + _L0_xattn_ref(_layernorm(x, axis=-1), ctx_1024, itok_BxS_0_511, L0_xattn_w_kv_comp, L0_xattn_w_q_down, L0_xattn_w_q_up, L0_xattn_w_q_rope, L0_xattn_w_k_up, L0_xattn_w_k_rope, L0_xattn_w_v_up, L0_xattn_w_out)
    x = x + _L0_attn_ref(_layernorm(x, axis=-1), L0_attn_W_in, L0_attn_conv_w, L0_attn_conv_b, L0_attn_W_x, L0_attn_W_dt, L0_attn_b_dt, L0_attn_A_log, L0_attn_Dp, L0_attn_W_out)
    x = x + _L0_ffn_ref(_layernorm(x, axis=-1), L0_ffn_gate_w, L0_ffn_gate_b, L0_ffn_w1, L0_ffn_w2, L0_ffn_w3, L0_ffn_ws1, L0_ffn_ws2, L0_ffn_ws3)
    x = x + _L1_xattn_ref(ctx_1024, _layernorm(x, axis=-1), fside_SxS2_0, L1_xattn_Wq, L1_xattn_bq, L1_xattn_Wk, L1_xattn_bk, L1_xattn_Wv, L1_xattn_bv, L1_xattn_Wo, L1_xattn_bo)
    x = x + _L1_attn_ref(_layernorm(x, axis=-1), L1_attn_Wq, L1_attn_Wk, L1_attn_Wv, L1_attn_Wo)
    x = x + _L1_ffn_ref(_layernorm(x, axis=-1), L1_ffn_w_router, L1_ffn_b_router, L1_ffn_we_gate, L1_ffn_we_up, L1_ffn_we_down, L1_ffn_ws_gate, L1_ffn_ws_up, L1_ffn_ws_down)
    return x

_drawn_inputs = setup_inputs


def setup_inputs(seed=0):
    import zlib

    import numpy as np

    out = dict(_drawn_inputs(seed))
    spreads = {'L0_attn_Dp': (1.0, 0.2), 'L0_ffn_gate_b': (0.0, 0.8)}
    factors = {'L0_ffn_gate_w': 8.0,
     'L0_ffn_w1': 8.0,
     'L0_ffn_w2': 8.0,
     'L0_ffn_w3': 8.0,
     'L1_xattn_bk': 64.0,
     'L1_xattn_bq': 2.899}
    for name, (base, spread) in spreads.items():
        noise = np.random.default_rng([zlib.crc32(name.encode()), seed]).standard_normal(out[name].shape)
        drawn = base * np.exp(spread * noise) if base else spread * noise
        out[name] = jnp.asarray(drawn.astype(out[name].dtype))
    for name, factor in factors.items():
        out[name] = (out[name] * factor).astype(out[name].dtype)
    return out
```

```python
from contextlib import ExitStack

import numpy as np

import concourse.bass as bass
from concourse import mybir

F32 = mybir.dt.float32
I32 = mybir.dt.int32
U32 = mybir.dt.uint32
ALU = mybir.AluOpType
ACT = mybir.ActivationFunctionType
AX_X = mybir.AxisListType.X

P = 128
B, S, D = 32, 64, 256
SK = 256
T = B * S
NT = T // P
KD = D // P
H = 16
LN_EPS = 1e-5
NEG = -1.0e30

HD, KVC, QC, RD = 64, 64, 96, 64
LOOK = 3
KROWS = B * SK

DI, NST, DTR, KC = 512, 16, 64, 4
NCH = DI // P
GT = 512
NG = T // GT

E = 64
CAP0, K0, I0, SI0 = 128, 6, 176, 352
K1, F1, NGR, TOPG, RSCALE = 8, 128, 8, 4, 2.5
IH = I0 // 2
SB0 = SI0 // IH
SLOTS0 = E * CAP0
NB1 = T * K1 // P + E
SLOTS1 = NB1 * P
DROPPED = 1.0e6

HK = 16


class Stage:

    def __init__(self, nc, name):
        self.nc, self.name, self.ctx, self.sems = nc, name, ExitStack(), {}

    def sb(self, name, shape, dt=F32):
        return self.ctx.enter_context(self.nc.sbuf_tensor(f"{self.name}_{name}", shape, dt))

    def ps(self, name, shape):
        return self.ctx.enter_context(self.nc.psum_tensor(f"{self.name}_{name}", shape, F32))

    def sem(self, name, u=0):
        if (name, u) not in self.sems:
            self.sems[name, u] = self.nc.alloc_semaphore(f"{self.name}_{name}{u}")
        return self.sems[name, u]


def bc(ap, shape):
    return ap.broadcast_to(shape)


class LayerNorm:

    def __init__(self, st, e):
        self.st, self.e = st, e
        self.stats = st.sb("stats", [P, NT, 6])
        self.mean = st.sb("mean", [P, NT])
        self.rstd = st.sb("rstd", [P, NT])
        self.tmp = st.sb("lntmp", [P, 2, NT])
        self.xs = st.sb("xs", [P, 2, D])
        self.psT = st.ps("psT", [P, 512])

    def vector_stats(self, v):
        st, X = self.st, self.e["X"]
        for t in range(NT):
            v.bn_stats(self.stats[:, t, :], X[:, t, :]).then_inc(st.sem("bn"), 1)
        v.wait_ge(st.sem("bn"), NT)
        s = self.stats
        v.tensor_tensor(self.tmp[:, 0, :], s[:, :, 1], s[:, :, 4], ALU.add).then_inc(st.sem("ln"), 1)
        v.tensor_tensor(self.tmp[:, 1, :], s[:, :, 1], s[:, :, 4], ALU.subtract).then_inc(st.sem("ln"), 1)
        v.tensor_tensor(self.rstd[:, :], s[:, :, 2], s[:, :, 5], ALU.add).then_inc(st.sem("ln"), 1)
        v.wait_ge(st.sem("ln"), 3)
        v.tensor_scalar(self.mean[:, :], self.tmp[:, 0, :], 0.5, None, ALU.mult).then_inc(st.sem("ln"), 1)
        v.scalar_tensor_tensor(self.tmp[:, 1, :], self.tmp[:, 1, :], 0.25, self.tmp[:, 1, :],
                               ALU.mult, ALU.mult).then_inc(st.sem("ln"), 1)
        v.tensor_scalar(self.rstd[:, :], self.rstd[:, :], 1.0 / D, LN_EPS, ALU.mult, ALU.add).then_inc(st.sem("ln"), 1)
        v.wait_ge(st.sem("ln"), 6)
        v.tensor_tensor(self.tmp[:, 0, :], self.rstd[:, :], self.tmp[:, 1, :], ALU.add).then_inc(st.sem("ln_var"), 1)
        v.wait_ge(st.sem("ln_std"), 1)
        v.reciprocal(self.rstd[:, :], self.tmp[:, 1, :]).then_inc(st.sem("ln_rstd"), 1)
        v.wait_ge(st.sem("ln_rstd"), 1)

    def scalar_std(self, a):
        st = self.st
        a.wait_ge(st.sem("ln_var"), 1)
        a.activation(self.tmp[:, 1, :], self.tmp[:, 0, :], ACT.Sqrt).then_inc(st.sem("ln_std"), 1)

    def vector_tile(self, v, p, u):
        st, X, t = self.st, self.e["X"], 2 * p + u
        v.wait_ge(st.sem("xs_free", u), p)
        v.tensor_scalar(self.xs[:, u, :], X[:, t, :], self.mean[:, bass.ds(t, 1)],
                        self.rstd[:, bass.ds(t, 1)], ALU.subtract, ALU.mult).then_inc(st.sem("xs_ready", u), 1)

    def tensor_tile(self, pe, p, u):
        st = self.st
        pe.wait_ge(st.sem("xs_ready", u), p + 1)
        pe.wait_ge(st.sem("xnT_ready", 1 - u), p + u)
        for k in range(KD):
            mm = pe.transpose(self.psT[:, k * P:(k + 1) * P], self.xs[:, u, k * P:(k + 1) * P], self.e["ident"][:, :])
        mm.then_inc(st.sem("xs_free", u), 1)

    def scalar_tile(self, a, p, u, out):
        st = self.st
        a.wait_ge(st.sem("xs_free", u), p + 1)
        carry_waits(a, st.sem("passed_act"))
        a.activation(out, self.psT[:, 0:D].rearrange("p (k n) -> p k n", k=KD), ACT.Copy).then_inc(st.sem("xnT_ready", u), 1)


def pipelined(eng, front, back, n=NT // 2):
    front(0, 0)
    with eng.Fori(0, n - 1) as p:
        front(p, 1)
        back(p, 0)
        front(p + 1, 0)
        back(p, 1)
    front(n - 1, 1)
    back(n - 1, 0)
    back(n - 1, 1)


def carry_waits(eng, passed):
    eng.sem_inc(passed, 1)


def stage_mla(nc, e, d):
    st = Stage(nc, "a")
    sb, ps, sem = st.sb, st.ps, st.sem
    X, ident = e["X"], e["ident"]
    table = d["key_table"]
    W2 = KVC + RD

    with st.ctx:
        kcompT, krope = sb("kcompT", [KVC, D]), sb("krope", [KVC, RD])
        qup, kup, vup, wout = (sb("qup", [HD, H, QC]), sb("kup", [HD, H, KVC]),
                               sb("vup", [HD, H, KVC]), sb("wout", [HD, H, D]))
        wqd = sb("wqd", [P, KD, QC])
        wk = sb("wk", [P, KD, W2])
        wq = sb("wq", [QC, H, W2])
        wo = sb("wo", [P, H // 2, D])
        cosk, sink = sb("cosk", [P, 4, RD]), sb("sink", [P, 4, RD])
        cosq, sinq = sb("cosq", [P, RD]), sb("sinq", [P, RD])
        segi, segf = sb("segi", [P, NT], I32), sb("segf", [P, NT])
        rows = sb("rows", [P, 2, NT])
        key = sb("key", [P, LOOK, NT])
        good = sb("good", [P, LOOK, NT])
        none = sb("none", [P, 2, NT])
        idx = sb("idx", [P, LOOK, NT])
        meanw = sb("meanw", [P, 1])
        c = sb("c", [P, 2, 2, KD, SK])
        tab = sb("tab", [P, 2, 4, W2])
        ra = sb("ra", [P, 2, 2, 4, RD])
        mrow = sb("mrow", [1, 2, 2, W2])
        ln = LayerNorm(st, e)
        xts = sb("xts", [P, 2, KD, P])
        qc = sb("qc", [QC, 2, P])
        q = sb("q", [P, 2, H, W2])
        kg = sb("kg", [P, 2, LOOK, W2])
        kra = sb("kra", [P, 2, 2, LOOK, RD])
        idxt = sb("idxt", [P, 2, 4], U32)
        prod = sb("prod", [P, H, W2])
        prod2 = sb("prod2", [P, H, W2])
        sc = sb("sc", [P, 2, H, 4])
        mx = sb("mx", [P, 2, 4, H])
        ol = sb("ol", [P, 2, 3, H, KVC])
        oT = sb("oT", [P, 2, 8, P])
        seen = sb("seen", [P, NT, LOOK])
        psk = ps("psk", [P, 4, 512])
        psm = ps("psm", [P, 2, 512])
        aux = ps("aux", [P, 512])

        LOADS = [(kcompT[:, :], d["kcompT"]), (krope[:, :], d["krope"]), (qup[:, :, :], d["qup"]),
                 (kup[:, :, :], d["kup"]), (vup[:, :, :], d["vup"]), (wout[:, :, :], d["wout"]),
                 (wqd[:, :, :], d["wqd"]), (wk[:, :, 0:KVC], d["kcomp"]), (wq[:, :, KVC:W2], d["qrope"]),
                 (cosk[:, :, :], d["cosk"]), (sink[:, :, :], d["sink"]), (cosq[:, :], d["cosq"]),
                 (sinq[:, :], d["sinq"]), (segi[:, :], d["seg"]), (rows[:, :, :], d["rows"]),
                 (meanw[:, :], d["meanw"])]
        W_ALL = 16 * len(LOADS)
        ctx_v = d["ctxT"].rearrange("(g b) p k n -> g p b k n", b=2)
        tab_v = table[0:KROWS, :].rearrange("(g j p) c -> g p j c", p=P, j=4)
        mean_v = table[KROWS:KROWS + B, :].rearrange("(g b) c -> g (b c)", b=2)

        with nc.Block() as block:
            @block.sync
            def _(sp):
                for dst, src in LOADS:
                    sp.dma_start(dst, src).then_inc(sem("weights"), 16)
                with sp.Fori(0, NT // 2) as p:
                    for u in range(2):
                        sp.wait_ge(sem("keys_done", u), p)
                        sp.dma_start(c[:, u], ctx_v[2 * p + u]).then_inc(sem("ctx", u), 16)

            @block.tensor
            def _(pe):
                pe.wait_ge(sem("weights"), W_ALL)
                for k in range(KD):
                    mm = pe.matmul(psk[:, 0, k * RD:(k + 1) * RD], kcompT[:, k * P:(k + 1) * P], krope[:, :],
                                   start=True, stop=True)
                for h in range(H):
                    mm = pe.matmul(psk[0:QC, 1 + h // 8, (h % 8) * KVC:(h % 8 + 1) * KVC], qup[:, h, :], kup[:, h, :],
                                   start=True, stop=True)
                mm.then_inc(sem("prep"), 1)
                for r in range(4):
                    if r:
                        pe.wait_ge(sem("wo_copied"), r)
                    else:
                        pe.wait_ge(sem("prep_copied"), 2 + KD)
                    for i in range(4):
                        h = 4 * r + i
                        mm = pe.matmul(psm[64 * (h % 2):64 * (h % 2) + KVC, i // 2, 0:D], vup[:, h, :], wout[:, h, :],
                                       start=True, stop=True)
                    mm.then_inc(sem("wo_prod"), 1)
                pe.wait_ge(sem("wo_copied"), 4)
                with pe.Fori(0, NT // 2) as p:
                    for u in range(2):
                        pe.wait_ge(sem("ctx", u), 16 * (p + 1))
                        pe.wait_ge(sem("rope", u), p)
                        pe.wait_ge(sem("nope", u), p)
                        for j in range(4):
                            for k in range(KD):
                                mm = pe.matmul(psk[:, u, j * P:(j + 1) * P], c[:, u, j // 2, k, (j % 2) * P:(j % 2 + 1) * P],
                                               wk[:, k, :], start=(k == 0), stop=(k == KD - 1))
                        mm.then_inc(sem("keys_done", u), 1)
                        pe.wait_ge(sem("rope", u), p + 1)
                        pe.wait_ge(sem("nope", u), p + 1)
                        pe.wait_ge(sem("mean_copied", u), p)
                        for j in range(4):
                            mm = pe.matmul(psm[0:1, u, (j // 2) * W2:(j // 2 + 1) * W2], meanw[:, :], tab[:, u, j, :],
                                           start=(j % 2 == 0), stop=(j % 2 == 1))
                        mm.then_inc(sem("mean_done", u), 1)

            @block.scalar
            def _(a):
                a.wait_ge(sem("prep"), 1)
                for k in range(KD):
                    a.activation(wk[:, k, KVC:W2], psk[:, 0, k * RD:(k + 1) * RD], ACT.Copy).then_inc(sem("prep_copied"), 1)
                for k in range(2):
                    a.activation(wq[:, 8 * k:8 * k + 8, 0:KVC], psk[0:QC, 1 + k, :].rearrange("p (h c) -> p h c", h=8),
                                 ACT.Copy).then_inc(sem("prep_copied"), 1)
                for r in range(4):
                    a.wait_ge(sem("wo_prod"), r + 1)
                    a.activation(wo[:, 2 * r:2 * r + 2, :], psm[:, 0:2, 0:D], ACT.Copy).then_inc(sem("wo_copied"), 1)
                with a.Fori(0, NT // 2) as p:
                    for u in range(2):
                        a.wait_ge(sem("keys_done", u), p + 1)
                        a.wait_ge(sem("tab_stored", u), 16 * p)
                        a.activation(tab[:, u, :, 0:KVC], psk[:, u, :].rearrange("p (j c) -> p j c", j=4)[:, :, 0:KVC],
                                     ACT.Copy).then_inc(sem("nope", u), 1)
                        a.wait_ge(sem("mean_done", u), p + 1)
                        a.wait_ge(sem("mean_stored", u), 16 * p)
                        a.activation(mrow[:, u, :, :].rearrange("p b c -> p (b c)"), psm[0:1, u, 0:2 * W2],
                                     ACT.Copy).then_inc(sem("mean_copied", u), 1)
                        a.wait_ge(sem("mean_copied", u), p + 1)
                        a.dma_start(mean_v[bass.ds(2 * p + u, 1), :], mrow[:, u, :, :].rearrange("p b c -> p (b c)")).then_inc(sem("mean_stored", u), 16)

            @block.gpsimd
            def _(g):
                with g.Fori(0, NT // 2) as p:
                    for u in range(2):
                        g.wait_ge(sem("rope", u), p + 1)
                        g.wait_ge(sem("nope", u), p + 1)
                        g.dma_start(tab_v[2 * p + u], tab[:, u]).then_inc(sem("tab_stored", u), 16)
                for u in range(2):
                    g.wait_ge(sem("tab_stored", u), 16 * (NT // 2))
                    g.wait_ge(sem("mean_stored", u), 16 * (NT // 2))

            @block.vector
            def _(v):
                v.wait_ge(sem("weights"), W_ALL)
                v.tensor_copy(segf[:, :], segi[:, :]).then_inc(sem("seg"), 1)
                v.wait_ge(sem("seg"), 1)
                for j in range(LOOK):
                    v.tensor_scalar(key[:, j, :], segf[:, :], float(-j), None, ALU.add).then_inc(sem("seg"), 1)
                v.tensor_scalar(none[:, 0, :], segf[:, :], 0.0, None, ALU.is_lt).then_inc(sem("seg"), 1)
                v.tensor_scalar(none[:, 1, :], segf[:, :], float(SK + LOOK - 1), None, ALU.is_ge).then_inc(sem("seg"), 1)
                v.wait_ge(sem("seg"), 6)
                v.tensor_scalar(good[:, :, :], key[:, :, :], 0.0, None, ALU.is_ge).then_inc(sem("seg"), 1)
                v.tensor_scalar(idx[:, :, :], key[:, :, :], float(SK), None, ALU.is_lt).then_inc(sem("seg"), 1)
                v.tensor_tensor(none[:, 0, :], none[:, 0, :], none[:, 1, :], ALU.add).then_inc(sem("seg"), 1)
                v.wait_ge(sem("seg"), 9)
                v.tensor_tensor(good[:, :, :], good[:, :, :], idx[:, :, :], ALU.mult).then_inc(sem("seg"), 1)
                v.wait_ge(sem("seg"), 10)
                v.tensor_scalar(idx[:, :, :], key[:, :, :], 0.0, float(SK - 1), ALU.max, ALU.min).then_inc(sem("seg"), 1)
                v.wait_ge(sem("seg"), 11)
                v.tensor_tensor(idx[:, :, :], idx[:, :, :], bc(rows[:, 0, None, :], [P, LOOK, NT]), ALU.add).then_inc(sem("seg"), 1)
                v.tensor_tensor(good[:, 0, :], good[:, 0, :], none[:, 0, :], ALU.add).then_inc(sem("seg"), 1)
                v.wait_ge(sem("seg"), 13)
                v.tensor_tensor(none[:, 1, :], rows[:, 1, :], idx[:, 0, :], ALU.subtract).then_inc(sem("seg"), 1)
                v.wait_ge(sem("seg"), 14)
                v.tensor_tensor(none[:, 1, :], none[:, 1, :], none[:, 0, :], ALU.mult).then_inc(sem("seg"), 1)
                v.wait_ge(sem("seg"), 15)
                v.tensor_tensor(idx[:, 0, :], idx[:, 0, :], none[:, 1, :], ALU.add).then_inc(sem("seg"), 1)
                v.tensor_scalar(seen[:, :, :].rearrange("p t j -> p j t"), good[:, :, :], -1.0, -NEG, ALU.add, ALU.mult).then_inc(sem("seg"), 1)
                v.wait_ge(sem("seg"), 17)
                with v.Fori(0, NT // 2) as p:
                    for u in range(2):
                        v.wait_ge(sem("nope", u), p + 1)
                        v.wait_ge(sem("tab_stored", u), 16 * p)
                        kr = psk[:, u, :].rearrange("p (j c) -> p j c", j=4)[:, :, KVC:W2]
                        hf = RD // 2
                        v.tensor_tensor(ra[:, u, 0], kr, cosk[:, :, :], ALU.mult).then_inc(sem("ra", u), 1)
                        v.tensor_tensor(ra[:, u, 1, :, 0:hf], kr[:, :, hf:RD], sink[:, :, 0:hf], ALU.mult).then_inc(sem("ra", u), 1)
                        v.tensor_tensor(ra[:, u, 1, :, hf:RD], kr[:, :, 0:hf], sink[:, :, hf:RD], ALU.mult).then_inc(sem("ra", u), 1)
                        v.wait_ge(sem("ra", u), 3 * p + 3)
                        v.tensor_tensor(tab[:, u, :, KVC:W2], ra[:, u, 0], ra[:, u, 1], ALU.add).then_inc(sem("rope", u), 1)

        SCALE = float(1.0 / np.sqrt(np.float32(HD + RD)))
        hf = RD // 2
        with nc.Block() as block:
            @block.gpsimd
            def _(g):
                def front(p, u):
                    g.wait_ge(sem("idxt", u), p + 1)
                    g.wait_ge(sem("o_lat", u), p)
                    carry_waits(g, sem("passed_pool"))
                    for j in range(LOOK):
                        g.indirect_dma_start(out=kg[:, u, j, :], out_offset=None, in_=table[:, :],
                                             in_offset=bass.IndirectOffsetOnAxis(ap=idxt[:, u, j:j + 1], axis=0)
                                             ).then_inc(sem("kg", u), 16)

                def back(p, u):
                    g.wait_ge(sem("q", u), p + 1)
                    g.wait_ge(sem("kr", u), p + 1)
                    g.wait_ge(sem("prod2_used", 1 - u), p + u)
                    g.tensor_tensor(prod2[:, :, :], q[:, u], bc(kg[:, u, 2:3, :], [P, H, W2]), ALU.mult).then_inc(sem("prod2", u), 1)
                    g.wait_ge(sem("probs", u), p + 1)
                    g.wait_ge(sem("ol_free", u), p)
                    for j in range(LOOK):
                        g.tensor_tensor(ol[:, u, j], bc(sc[:, u, :, j:j + 1], [P, H, KVC]),
                                        bc(kg[:, u, j:j + 1, 0:KVC], [P, H, KVC]), ALU.mult).then_inc(sem("ol", u), 1)

                pipelined(g, front, back)

            @block.tensor
            def _(pe):
                def front(p, u):
                    t = 2 * p + u
                    pe.wait_ge(sem("qc"), t)
                    ln.tensor_tile(pe, p, u)
                    pe.wait_ge(sem("xnT_ready", u), p + 1)
                    for k in range(KD):
                        mm = pe.matmul(ln.psT[0:QC, D:D + P], wqd[:, k, :], xts[:, u, k, :], start=(k == 0), stop=(k == KD - 1))
                    mm.then_inc(sem("qc_done"), 1)
                    pe.wait_ge(sem("qc"), t + 1)
                    pe.wait_ge(sem("q", 1 - u), p + u)
                    for n in range(4):
                        mm = pe.matmul(psk[:, n, :], qc[:, u, :], wq[:, 4 * n:4 * n + 4, :].rearrange("p h c -> p (h c)"),
                                       start=True, stop=True)
                    mm.then_inc(sem("q_done"), 1)

                def back(p, u):
                    t = 2 * p + u
                    pe.wait_ge(sem("o_lat", u), p + 1)
                    pe.wait_ge(sem("oT"), t)
                    for n in range(8):
                        mm = pe.transpose(psm[:, n // 4, (n % 4) * P:(n % 4 + 1) * P],
                                          ol[:, u, 0].rearrange("p h c -> p (h c)")[:, n * P:(n + 1) * P], ident[:, :])
                    mm.then_inc(sem("ol_free", u), 1)
                    pe.wait_ge(sem("oT"), t + 1)
                    pe.wait_ge(sem("x_added"), t)
                    for n in range(8):
                        mm = pe.matmul(aux[:, 0:D], oT[:, u, n, :], wo[:, n, :], start=(n == 0), stop=(n == 7))
                    mm.then_inc(sem("y_done"), 1)

                pipelined(pe, front, back)

            @block.scalar
            def _(a):
                def front(p, u):
                    t = 2 * p + u
                    a.wait_ge(sem("qc_done"), 2 * p)
                    ln.scalar_tile(a, p, u, xts[:, u])
                    a.wait_ge(sem("qc_done"), t + 1)
                    a.activation(qc[:, u, :], ln.psT[0:QC, D:D + P], ACT.Copy).then_inc(sem("qc"), 1)
                    a.wait_ge(sem("q_done"), t + 1)
                    a.wait_ge(sem("scores", u), p)
                    a.activation(q[:, u].rearrange("p h c -> p (h c)"), psk[:, :, :].rearrange("p n c -> p (n c)"), ACT.Copy).then_inc(sem("q", u), 1)

                def back(p, u):
                    a.wait_ge(sem("shifted", u), p + 1)
                    a.activation(sc[:, u, :, 0:LOOK], sc[:, u, :, 0:LOOK], ACT.Exp).then_inc(sem("exp", u), 1)
                    a.wait_ge(sem("ol_free", u), p + 1)
                    a.activation(oT[:, u].rearrange("p n c -> p (n c)"), psm[:, :, :].rearrange("p n c -> p (n c)"), ACT.Copy).then_inc(sem("oT"), 1)

                ln.scalar_std(a)
                pipelined(a, front, back)

            @block.vector
            def _(v):
                def front(p, u):
                    v.wait_ge(sem("kg", u), 48 * p)
                    v.tensor_copy(idxt[:, u, 0:LOOK], idx[:, :, bass.ds(2 * p + u, 1)].rearrange("p j o -> p (j o)")).then_inc(sem("idxt", u), 1)
                    ln.vector_tile(v, p, u)

                def back(p, u):
                    t = 2 * p + u
                    v.wait_ge(sem("kg", u), 48 * (p + 1))
                    kk = kg[:, u, :, KVC:W2]
                    v.tensor_tensor(kra[:, u, 0], kk, bc(cosq[:, None, :], [P, LOOK, RD]), ALU.mult).then_inc(sem("kra", u), 1)
                    v.tensor_tensor(kra[:, u, 1, :, 0:hf], kk[:, :, hf:RD], bc(sinq[:, None, 0:hf], [P, LOOK, hf]), ALU.mult).then_inc(sem("kra", u), 1)
                    v.tensor_tensor(kra[:, u, 1, :, hf:RD], kk[:, :, 0:hf], bc(sinq[:, None, hf:RD], [P, LOOK, hf]), ALU.mult).then_inc(sem("kra", u), 1)
                    v.wait_ge(sem("kra", u), 3 * p + 3)
                    v.tensor_tensor(kk, kra[:, u, 0], kra[:, u, 1], ALU.add).then_inc(sem("kr", u), 1)
                    v.wait_ge(sem("kr", u), p + 1)
                    v.wait_ge(sem("q", u), p + 1)
                    for j in range(LOOK - 1):
                        v.tensor_tensor(prod[:, :, :], q[:, u], bc(kg[:, u, j:j + 1, :], [P, H, W2]), ALU.mult).then_inc(sem("prod"), 1)
                        v.wait_ge(sem("prod"), 2 * t + j + 1)
                        v.tensor_reduce(sc[:, u, :, j], prod[:, :, :], AX_X, ALU.add).then_inc(sem("sdot", u), 1)
                        v.wait_ge(sem("sdot", u), 2 * p + j + 1)
                    v.wait_ge(sem("prod2", u), p + 1)
                    v.tensor_reduce(sc[:, u, :, 2], prod2[:, :, :], AX_X, ALU.add).then_inc(sem("prod2_used", u), 1)
                    v.wait_ge(sem("prod2_used", u), p + 1)
                    s3 = sc[:, u, :, 0:LOOK]
                    v.scalar_tensor_tensor(s3, s3, SCALE, bc(seen[:, bass.ds(t, 1), :], [P, H, LOOK]),
                                           ALU.mult, ALU.add).then_inc(sem("scores", u), 1)
                    v.wait_ge(sem("scores", u), p + 1)
                    v.tensor_reduce(mx[:, u, 0, :], s3, AX_X, ALU.max).then_inc(sem("smax", u), 1)
                    v.wait_ge(sem("smax", u), p + 1)
                    v.tensor_tensor(s3, s3, bc(mx[:, u, 0, :, None], [P, H, LOOK]), ALU.subtract).then_inc(sem("shifted", u), 1)
                    v.wait_ge(sem("exp", u), p + 1)
                    v.tensor_reduce(mx[:, u, 1, :], s3, AX_X, ALU.add).then_inc(sem("ssum", u), 1)
                    v.wait_ge(sem("ssum", u), p + 1)
                    v.reciprocal(mx[:, u, 2, :], mx[:, u, 1, :]).then_inc(sem("srec", u), 1)
                    v.wait_ge(sem("srec", u), p + 1)
                    v.tensor_tensor(s3, s3, bc(mx[:, u, 2, :, None], [P, H, LOOK]), ALU.mult).then_inc(sem("probs", u), 1)
                    v.wait_ge(sem("ol", u), 3 * p + 3)
                    v.tensor_tensor(ol[:, u, 0], ol[:, u, 0], ol[:, u, 1], ALU.add).then_inc(sem("osum", u), 1)
                    v.wait_ge(sem("osum", u), p + 1)
                    v.tensor_tensor(ol[:, u, 0], ol[:, u, 0], ol[:, u, 2], ALU.add).then_inc(sem("o_lat", u), 1)
                    v.wait_ge(sem("y_done"), t + 1)
                    v.tensor_tensor(X[:, bass.ds(t, 1), :].rearrange("p o d -> p (o d)"), X[:, bass.ds(t, 1), :].rearrange("p o d -> p (o d)"),
                                    aux[:, 0:D], ALU.add).then_inc(sem("x_added"), 1)

                ln.vector_stats(v)
                pipelined(v, front, back)


def stage_mamba(nc, e, d):
    st = Stage(nc, "b")
    sb, ps, sem = st.sb, st.ps, st.sem
    X, ident = e["X"], e["ident"]
    NB, CQ = GT // S, 4
    NQ = NST // CQ
    LP = S + KC - 1

    with st.ctx:
        win = sb("win", [P, KD, 2 * DI])
        convw, convb = sb("convw", [P, NCH, KC]), sb("convb", [P, NCH])
        wx = sb("wx", [P, NCH, DTR + 2 * NST])
        wdt, bdt = sb("wdt", [DTR, DI]), sb("bdt", [P, NCH])
        A, Dp = sb("A", [P, NCH, NST]), sb("Dp", [P, NCH])
        wout = sb("wout", [P, NCH, D])
        ln = LayerNorm(st, e)
        xnT = sb("xnT", [P, KD, T])
        xcp = sb("xcp", [P, NCH, NB, LP])
        xz = sb("xz", [P, 2, 2 * NCH, GT])
        th = sb("th", [P, NCH, GT])
        delta, dx = sb("delta", [P, 2, NCH, GT]), sb("dx", [P, 2, NCH, GT])
        dbc = sb("dbc", [DTR + 2 * NST, GT])
        bcb = sb("bcb", [P, 2, 2, CQ, GT])
        dA = sb("dA", [P, 2, CQ, GT])
        h = sb("h", [P, 2, CQ, GT])
        yz = sb("yz", [P, NCH, GT])
        psy = ps("psy", [P, NCH, GT])
        psw = ps("psw", [P, 2, GT])
        pso = ps("pso", [P, 512])

        LOADS = [(win[:, :, :], d["b_win"]), (convw[:, :, :], d["b_convw"]), (convb[:, :], d["b_convb"]),
                 (wx[:, :, :], d["b_wx"]), (wdt[:, :], d["b_wdt"]), (bdt[:, :], d["b_bdt"]),
                 (A[:, :, :], d["b_alog"]), (Dp[:, :], d["b_dp"]), (wout[:, :, :], d["b_wout"])]
        W_ALL = 16 * len(LOADS)
        rows = d["bc_rows"]
        PER = (7, 6)

        def buf(t, g):
            v = t[:, bass.ds(g % 2, 1)]
            return v.rearrange("p o c n -> p (o c) n")

        def wait_bank(eng, name, g, r, more):
            eng.wait_ge(sem(name, r % 2), PER[r % 2] * g + r // 2 + more)

        def interleave(eng, piece, step, pieces):
            for r in range(pieces):
                piece(0, r)
            with eng.Fori(0, NG - 1) as g:
                for i in range(NQ * NCH):
                    step(g, i)
                    if i < pieces:
                        piece(g + 1, i)
            for i in range(NQ * NCH):
                step(NG - 1, i)

        NP = 15

        with nc.Block() as block:
            @block.sync
            def _(sp):
                for dst, src in LOADS:
                    sp.dma_start(dst, src).then_inc(sem("weights"), 16)

                def load(g, nq, first=False):
                    if nq == 0:
                        sp.wait_ge(sem("rows_stored"), 16 * (g + 1))
                    if not first:
                        sp.wait_ge(sem("hc", 1), 8 * g + 2 * nq - 2)
                    for k in range(2):
                        src = rows[bass.ds(g, 1), k * NST + CQ * nq:k * NST + CQ * nq + CQ, :].rearrange("o n t -> (o n t)")
                        sp.dma_start(bcb[:, nq % 2, k].rearrange("p n t -> p (n t)"), src.partition_broadcast(P)).then_inc(sem("bcast", nq % 2), 16)

                load(0, 0, True)
                load(0, 1, True)
                with sp.Fori(0, NG - 1) as g:
                    load(g, 2)
                    load(g, 3)
                    load(g + 1, 0)
                    load(g + 1, 1)
                load(NG - 1, 2)
                load(NG - 1, 3)

            @block.tensor
            def _(pe):
                with pe.Fori(0, NT // 2) as p:
                    for u in range(2):
                        ln.tensor_tile(pe, p, u)
                for u in range(2):
                    pe.wait_ge(sem("xnT_ready", u), NT // 2)
                pe.wait_ge(sem("weights"), W_ALL)

                def piece(g, r):
                    if r < 8:
                        wait_bank(pe, "psw_free", g, r, 0)
                        for k in range(KD):
                            mm = pe.matmul(psw[:, r % 2, :], win[:, k, r * P:(r + 1) * P], xnT[:, k, bass.ds(GT * g, GT)],
                                           start=(k == 0), stop=(k == KD - 1))
                        mm.then_inc(sem("psw_ready", r % 2), 1)
                    elif r == 9:
                        pe.wait_ge(sem("silu"), g + 1)
                        wait_bank(pe, "psw_free", g, 8, 0)
                        for c in range(NCH):
                            mm = pe.matmul(psw[0:DTR + 2 * NST, 0, :], wx[:, c, :], buf(xz, g)[:, c, :], start=(c == 0), stop=(c == NCH - 1))
                        mm.then_inc(sem("psw_ready", 0), 1)
                    elif 10 <= r < 14:
                        c = r - 10
                        pe.wait_ge(sem("dbc"), g + 1)
                        wait_bank(pe, "psw_free", g, 9 + c, 0)
                        pe.matmul(psw[:, (9 + c) % 2, :], wdt[:, c * P:(c + 1) * P], dbc[0:DTR, :], start=True, stop=True
                                  ).then_inc(sem("psw_ready", (9 + c) % 2), 1)

                def step(g, i):
                    s, c, nq = i % 2, i % NCH, i // NCH
                    if nq == 0:
                        pe.wait_ge(sem("y", c), g)
                    pe.wait_ge(sem("hc", s), 8 * g + i // 2 + 1)
                    for j in range(CQ):
                        mm = pe.matmul(psy[:, c, :], ident[:, :], h[:, s, j, :], start=(nq == 0 and j == 0),
                                       stop=(nq == NQ - 1 and j == CQ - 1))
                    mm.then_inc(sem("h_free", s), 1)
                    if i == NQ * NCH - 1:
                        pe.wait_ge(sem("yz"), NCH * (g + 1))
                        for t in range(GT // P):
                            out = [pso, ln.psT][t % 2]
                            pe.wait_ge(sem("x_added", t % 2), 2 * g + t // 2)
                            for cc in range(NCH):
                                mm = pe.matmul(out[:, 0:D], yz[:, cc, t * P:(t + 1) * P], wout[:, cc, :], start=(cc == 0), stop=(cc == NCH - 1))
                            mm.then_inc(sem("out", t % 2), 1)

                interleave(pe, piece, step, NP)

            @block.scalar
            def _(a):
                ln.scalar_std(a)
                a.wait_ge(sem("weights"), W_ALL)
                a.activation(A[:, :, :], A[:, :, :], ACT.Exp).then_inc(sem("A_exp"), 1)
                with a.Fori(0, NT // 2) as p:
                    for u in range(2):
                        ln.scalar_tile(a, p, u, xnT[:, :, bass.ds(P * (2 * p + u), P)])
                a.wait_ge(sem("pads"), 2)

                def piece(g, r):
                    if r < 8:
                        wait_bank(a, "psw_ready", g, r, 1)
                        if r < NCH:
                            a.wait_ge(sem("conv", r), g)
                            out = xcp[:, r, :, KC - 1:LP]
                        else:
                            out = buf(xz, g)[:, r, :].rearrange("p (b l) -> p b l", b=NB)
                        carry_waits(a, sem("passed_act"))
                        a.activation(out, psw[:, r % 2, :].rearrange("p (b l) -> p b l", b=NB), ACT.Copy).then_inc(sem("psw_free", r % 2), 1)
                    elif r == 8:
                        for c in range(NCH):
                            a.wait_ge(sem("conv", c), g + 1)
                        a.wait_ge(sem("delta"), g)
                        carry_waits(a, sem("passed_act"))
                        for k in range(2):
                            a.activation(th[:, :, :], buf(xz, g)[:, NCH * k:NCH * k + NCH, :], ACT.Tanh, scale=0.5).then_inc(sem("tanh"), 1)
                            a.wait_ge(sem("gated"), 2 * g + k + 1)
                            carry_waits(a, sem("passed_act"))
                        a.activation(buf(xz, g), buf(xz, g), ACT.Copy, scale=0.5).then_inc(sem("silu"), 1)
                    elif r == 9:
                        wait_bank(a, "psw_ready", g, 8, 1)
                        a.wait_ge(sem("rows_stored"), 16 * g)
                        a.activation(dbc[:, :], psw[0:DTR + 2 * NST, 0, :], ACT.Copy).then_inc(sem("psw_free", 0), 1)
                        wait_bank(a, "psw_free", g, 8, 1)
                        a.activation(th[0:1, 0, 0:1], th[0:1, 0, 0:1], ACT.Copy).then_inc(sem("dbc"), 1)
                        a.dma_start(rows[bass.ds(g, 1)].rearrange("o n t -> (o n) t"), dbc[DTR:DTR + 2 * NST, :]).then_inc(sem("rows_stored"), 16)
                    elif 10 <= r < 14:
                        c = r - 10
                        wait_bank(a, "psw_ready", g, 9 + c, 1)
                        src = psw[:, (9 + c) % 2, :]
                        carry_waits(a, sem("passed_act"))
                        a.activation(buf(delta, g)[:, c, :], src, ACT.Relu, bias=bdt[:, c:c + 1])
                        a.activation(th[:, c, :], src, ACT.Abs, bias=bdt[:, c:c + 1]).then_inc(sem("psw_free", (9 + c) % 2), 1)
                    elif r == 14:
                        a.wait_ge(sem("psw_free", 0), 7 * g + 7)
                        a.wait_ge(sem("psw_free", 1), 6 * g + 6)
                        a.activation(th[:, :, :], th[:, :, :], ACT.Exp, scale=-1.0).then_inc(sem("sp_exp"), 1)
                        a.wait_ge(sem("sp_exp"), g + 1)
                        a.activation(th[:, :, :], th[:, :, :], ACT.Ln, bias=1.0).then_inc(sem("sp_ln"), 1)

                def step(g, i):
                    s, c, nq = i % 2, i % NCH, i // NCH
                    if i == 0:
                        a.wait_ge(sem("delta"), g + 1)
                        a.wait_ge(sem("A_neg"), 1)
                    a.wait_ge(sem("scan", s), 8 * g + i // 2)
                    carry_waits(a, sem("passed_act"))
                    dv = buf(delta, g)[:, c, :].rearrange("p (b l) -> p b l", b=NB)[:, :, 1:S]
                    for j in range(CQ):
                        n = CQ * nq + j
                        ins = a.activation(dA[:, s, j, :].rearrange("p (b l) -> p b l", b=NB)[:, :, 1:S], dv, ACT.Exp,
                                           scale=A[:, c, n:n + 1])
                    ins.then_inc(sem("dA", s), 1)

                interleave(a, piece, step, NP)
                a.wait_ge(sem("rows_stored"), 16 * NG)

            @block.gpsimd
            def _(g_):
                g_.memset(dA[:, :, :, :], 0.0).then_inc(sem("pads"), 1)
                g_.memset(xcp[:, :, :, 0:KC - 1], 0.0).then_inc(sem("pads"), 1)

                def piece(g, r):
                    if r == 14:
                        g_.wait_ge(sem("sp_ln"), g + 1)
                        carry_waits(g_, sem("passed_pool"))
                        g_.tensor_tensor(buf(delta, g), buf(delta, g), th[:, :, :], ALU.add).then_inc(sem("delta"), 1)
                        g_.wait_ge(sem("delta"), g + 1)
                        carry_waits(g_, sem("passed_pool"))
                        g_.tensor_tensor(buf(dx, g), buf(delta, g), buf(xz, g)[:, 0:NCH, :], ALU.mult).then_inc(sem("dx"), 1)
                        g_.wait_ge(sem("dx"), g + 1)

                def step(g, i):
                    s, c, nq = i % 2, i % NCH, i // NCH
                    g_.wait_ge(sem("h_free", s), 8 * g + i // 2)
                    if c == 0:
                        g_.wait_ge(sem("bcast", nq % 2), 32 * (2 * g + nq // 2 + 1))
                    carry_waits(g_, sem("passed_pool"))
                    g_.tensor_tensor(h[:, s], bc(buf(dx, g)[:, c:c + 1, :], [P, CQ, GT]), bcb[:, nq % 2, 0], ALU.mult).then_inc(sem("bx", s), 1)

                interleave(g_, piece, step, NP)

            @block.vector
            def _(v):
                ln.vector_stats(v)
                with v.Fori(0, NT // 2) as p:
                    for u in range(2):
                        ln.vector_tile(v, p, u)
                v.wait_ge(sem("weights"), W_ALL)
                v.wait_ge(sem("A_exp"), 1)
                v.tensor_scalar(A[:, :, :], A[:, :, :], -1.0, None, ALU.mult).then_inc(sem("A_neg"), 1)
                v.wait_ge(sem("pads"), 2)

                def piece(g, r):
                    if r < NCH:
                        wait_bank(v, "psw_free", g, r, 1)
                        acc = buf(xz, g)[:, r, :].rearrange("p (b l) -> p b l", b=NB)
                        v.tensor_scalar(acc, xcp[:, r, :, 0:S], convw[:, r, 0:1], convb[:, r:r + 1], ALU.mult, ALU.add).then_inc(sem("cv", r), 1)
                        for k in range(1, KC):
                            v.wait_ge(sem("cv", r), 3 * g + k)
                            v.scalar_tensor_tensor(acc, xcp[:, r, :, k:k + S], convw[:, r, k:k + 1], acc, ALU.mult, ALU.add
                                                   ).then_inc(sem("cv" if k < KC - 1 else "conv", r), 1)
                    elif r == 8:
                        for k in range(2):
                            half = buf(xz, g)[:, NCH * k:NCH * k + NCH, :]
                            v.wait_ge(sem("tanh"), 2 * g + k + 1)
                            v.scalar_tensor_tensor(half, th[:, :, :], 1.0, half, ALU.add, ALU.mult).then_inc(sem("gated"), 1)

                def step(g, i):
                    s, c, nq = i % 2, i % NCH, i // NCH
                    k = 8 * g + i // 2
                    v.wait_ge(sem("dA", s), k + 1)
                    v.wait_ge(sem("bx", s), k + 1)
                    hs = h[:, s].rearrange("p j n -> p (j n)")
                    v.tensor_tensor_scan(hs, dA[:, s].rearrange("p j n -> p (j n)"), hs, 0.0, ALU.mult, ALU.add).then_inc(sem("scan", s), 1)
                    v.wait_ge(sem("scan", s), k + 1)
                    v.tensor_tensor(h[:, s], h[:, s], bcb[:, nq % 2, 1], ALU.mult).then_inc(sem("hc", s), 1)
                    if nq == NQ - 1:
                        v.wait_ge(sem("h_free", s), k + 1)
                        if c < 2:
                            v.wait_ge(sem("out", c), 2 * g)
                        v.scalar_tensor_tensor(yz[:, c, :], buf(xz, g)[:, c, :], Dp[:, c:c + 1], psy[:, c, :], ALU.mult, ALU.add).then_inc(sem("y", c), 1)
                        v.wait_ge(sem("y", c), g + 1)
                        v.tensor_tensor(yz[:, c, :], yz[:, c, :], buf(xz, g)[:, NCH + c, :], ALU.mult).then_inc(sem("yz"), 1)
                    if i == NQ * NCH - 1:
                        for t in range(GT // P):
                            out = [pso, ln.psT][t % 2]
                            v.wait_ge(sem("out", t % 2), 2 * g + t // 2 + 1)
                            xt = X[:, bass.ds(4 * g + t, 1), :].rearrange("p o d -> p (o d)")
                            v.tensor_tensor(xt, xt, out[:, 0:D], ALU.add).then_inc(sem("x_added", t % 2), 1)

                interleave(v, piece, step, NP)


def stage_moe(nc, e, d, layer):
    st = Stage(nc, f"m{layer}")
    sb, ps, sem = st.sb, st.ps, st.sem
    X, ident = e["X"], e["ident"]
    capped = layer == 0
    K = K0 if capped else K1
    NB_ = E if capped else NB1
    BW, NBW = (IH, 2) if capped else (F1, 1)
    NSB = SB0 if capped else 1
    slot_tok, xn, y = d[f"slot_tok{layer}"], d[f"xn{layer}"], d[f"y{layer}"]
    TR = NB_ // 2 if not capped else E
    NTR = NB_ // TR

    with st.ctx:
        xnT = sb("xnT", [P, KD, T])
        gslot = sb("gslot", [P, NT, K], U32)
        wts = sb("wts", [P, NT, K])
        ebrow = sb("ebrow", [1, NB_], U32)

        r = Stage(nc, f"m{layer}r")
        rs = r.sem
        with r.ctx:
            gw, gb = r.sb("gw", [P, KD, E]), r.sb("gb", [P, E])
            iota, ltri, ones = r.sb("iota", [P, E]), r.sb("ltri", [P, P]), r.sb("ones", [P, P])
            base, iotab = r.sb("base", [P, E]), r.sb("iotab", [P, 2])
            tokid = r.sb("tokid", [P, NT], I32)
            ln = LayerNorm(r, e)
            xts = r.sb("xts", [P, 2, KD, P])
            sc, sel = r.sb("sc", [P, NT, E]), r.sb("sel", [P, NT, E])
            ex = r.sb("ex", [P, NT, E])
            row = r.sb("row", [P, 4, NT])
            top, topi, topf = r.sb("top", [P, NT, 8]), r.sb("topi", [P, NT, 8], U32), r.sb("topf", [P, NT, 8])
            oh, pr = r.sb("oh", [P, NT, K, E]), r.sb("pr", [P, NT, K, E])
            mask = r.sb("mask", [P, NT, E])
            before = r.sb("before", [P, NT + 1, E])
            slotf = r.sb("slotf", [P, NT, K])
            sloti = r.sb("sloti", [P, NT, K], U32)
            ids, idt = r.sb("ids", [P, 2, K], U32), r.sb("idt", [P, 2], I32)
            zero = r.sb("zero", [P, NB_], I32)
            nb = r.sb("nb", [P, 4, E])
            nbi = r.sb("nbi", [P, 2, E], I32)
            ebc = r.sb("ebc", [P, 2])
            ebr = r.sb("ebr", [1, 2, P])
            gt8, gs = r.sb("gt8", [P, NT, NGR, 8]), r.sb("gs", [P, NT, NGR])
            gm = r.sb("gm", [P, NT, NGR])
            psl = r.ps("psl", [P, NT, E])
            psc = r.ps("psc", [P, NT, E])
            pst = r.ps("pst", [P, NT, E])

            LOADS = [(gw[:, :, :], d[f"m{layer}_gw"]), (gb[:, :], d[f"m{layer}_gb"].partition_broadcast(P)),
                     (iota[:, :], d["iota_e"].partition_broadcast(P)), (ltri[:, :], d["ltri"]), (ones[:, :], d["ones"]),
                     (base[:, :], d["slot_base"].partition_broadcast(P)), (iotab[:, :], d["iota_b"]), (tokid[:, :], d["tokid"])]
            W_ALL = 16 * len(LOADS)

            with nc.Block() as block:
                @block.sync
                def _(sp):
                    for dst, src in LOADS:
                        sp.dma_start(dst, src).then_inc(rs("weights"), 16)
                    sp.wait_ge(rs("zero"), 1)
                    sp.dma_start(slot_tok.rearrange("(p n) o -> p (n o)", p=P), zero[:, :]).then_inc(rs("table_clear"), 16)
                    with sp.Fori(0, NT // 2) as p:
                        for u in range(2):
                            sp.wait_ge(rs("xs_ready", u), p + 1)
                            sp.dma_start(xn.rearrange("(t p) d -> t p d", p=P)[2 * p + u], ln.xs[:, u, :]).then_inc(rs("xs_stored", u), 16)
                    for u in range(2):
                        sp.wait_ge(rs("xs_stored", u), 16 * (NT // 2))
                    sp.wait_ge(rs("table_clear"), 16)

                @block.tensor
                def _(pe):
                    pe.wait_ge(rs("weights"), W_ALL)
                    with pe.Fori(0, NT // 2) as p:
                        for u in range(2):
                            t = 2 * p + u
                            ln.tensor_tile(pe, p, u)
                            pe.wait_ge(rs("xts", u), p + 1)
                            pe.wait_ge(rs("logits_out", 1 - u), p + u)
                            for k in range(KD):
                                mm = pe.matmul(psc[:, 8 * u, :], xts[:, u, k, :], gw[:, k, :], start=(k == 0), stop=(k == KD - 1))
                            mm.then_inc(rs("logits", u), 1)
                    pe.wait_ge(rs("mask"), 1)
                    for u in range(2):
                        pe.wait_ge(rs("logits_out", u), NT // 2)
                    for n in range(2):
                        pe.matmul(psl[:, 8 * n:8 * n + 8, :].rearrange("p t e -> p (t e)"), ltri[:, :],
                                  mask[:, 8 * n:8 * n + 8, :].rearrange("p t e -> p (t e)"), start=True, stop=True)
                    for n in range(2):
                        mm = pe.matmul(pst[:, 8 * n:8 * n + 8, :].rearrange("p t e -> p (t e)"), ones[:, :],
                                       mask[:, 8 * n:8 * n + 8, :].rearrange("p t e -> p (t e)"), start=True, stop=True)
                    mm.then_inc(rs("ranks"), 1)
                    if not capped:
                        pe.wait_ge(rs("ebc"), 1)
                        for n in range(2):
                            mm = pe.matmul(psc[0:1, 0:2, :].rearrange("p a b -> p (a b)") if n == 0 else psc[0:1, 2:4, :].rearrange("p a b -> p (a b)"),
                                           ebc[:, n:n + 1], ident[:, :], start=True, stop=True)
                        mm.then_inc(rs("ebt"), 1)

                @block.scalar
                def _(a):
                    ln.scalar_std(a)
                    with a.Fori(0, NT // 2) as p:
                        for u in range(2):
                            t = 2 * p + u
                            a.wait_ge(rs("logits", u), p)
                            ln.scalar_tile(a, p, u, xnT[:, :, bass.ds(P * t, P)])
                            a.activation(xts[:, u], ln.psT[:, 0:D].rearrange("p (k n) -> p k n", k=KD), ACT.Copy).then_inc(rs("xts", u), 1)
                            a.wait_ge(rs("logits", u), p + 1)
                            carry_waits(a, rs("passed_act"))
                            a.activation(sc[:, bass.ds(t, 1), :].rearrange("p o e -> p (o e)"), psc[:, 8 * u, :], ACT.Copy).then_inc(rs("logits_out", u), 1)
                    if capped:
                        a.wait_ge(rs("shifted"), 1)
                        a.activation(ex[:, :, :], sc[:, :, :], ACT.Exp).then_inc(rs("exp"), 1)
                    else:
                        for u in range(2):
                            a.wait_ge(rs("logits_out", u), NT // 2)
                        a.activation(ex[:, :, :], sc[:, :, :], ACT.Exp, scale=-1.0).then_inc(rs("exp"), 1)

                @block.gpsimd
                def _(g):
                    g.memset(zero[:, :], 0).then_inc(rs("zero"), 1)
                    g.wait_ge(rs("weights"), W_ALL)
                    g.wait_ge(rs("table_clear"), 16)
                    g.wait_ge(rs("sloti"), 1)
                    with g.Fori(0, NT // 2) as p:
                        for u in range(2):
                            t = 2 * p + u
                            g.wait_ge(rs("scattered", u), 16 * K * p)
                            carry_waits(g, rs("passed_pool"))
                            g.tensor_copy(ids[:, u, :], sloti[:, bass.ds(t, 1), :].rearrange("p o k -> p (o k)")).then_inc(rs("ids"), 1)
                            g.tensor_copy(idt[:, u:u + 1], tokid[:, bass.ds(t, 1)]).then_inc(rs("ids"), 1)
                            g.wait_ge(rs("ids"), 2 * t + 2)
                            carry_waits(g, rs("passed_pool"))
                            for k in range(K):
                                g.indirect_dma_start(out=slot_tok, out_offset=bass.IndirectOffsetOnAxis(ap=ids[:, u, k:k + 1], axis=0),
                                                     in_=idt[:, u:u + 1], in_offset=None, bounds_check=NB_ * P - 1, oob_is_err=False
                                                     ).then_inc(rs("scattered", u), 16)
                    for u in range(2):
                        g.wait_ge(rs("scattered", u), 16 * K * (NT // 2))

                @block.vector
                def _(v):
                    v.wait_ge(rs("weights"), W_ALL)
                    n_step = [0]

                    def step(ins):
                        n_step[0] += 1
                        ins.then_inc(rs("chain"), 1)
                        v.wait_ge(rs("chain"), n_step[0])

                    ln.vector_stats(v)
                    with v.Fori(0, NT // 2) as p:
                        for u in range(2):
                            v.wait_ge(rs("xs_stored", u), 16 * p)
                            carry_waits(v, rs("passed_dve"))
                            ln.vector_tile(v, p, u)
                    for u in range(2):
                        v.wait_ge(rs("logits_out", u), NT // 2)
                    NE = [P, NT, E]
                    if capped:
                        step(v.tensor_reduce(row[:, 0, :], sc[:, :, :], AX_X, ALU.max))
                        v.tensor_tensor(sc[:, :, :], sc[:, :, :], bc(row[:, 0, :, None], NE), ALU.subtract).then_inc(rs("shifted"), 1)
                        v.wait_ge(rs("exp"), 1)
                        step(v.tensor_reduce(row[:, 1, :], ex[:, :, :], AX_X, ALU.add))
                        step(v.reciprocal(row[:, 2, :], row[:, 1, :]))
                        step(v.tensor_tensor(sc[:, :, :], ex[:, :, :], bc(row[:, 2, :, None], NE), ALU.mult))
                        step(v.tensor_tensor(sel[:, :, :], sc[:, :, :], bc(gb[:, None, :], NE), ALU.add))
                    else:
                        v.wait_ge(rs("exp"), 1)
                        step(v.tensor_scalar(ex[:, :, :], ex[:, :, :], 1.0, None, ALU.add))
                        step(v.reciprocal(sc[:, :, :], ex[:, :, :]))
                        step(v.tensor_tensor(sel[:, :, :], sc[:, :, :], bc(gb[:, None, :], NE), ALU.add))
                        for t in range(NT):
                            for k in range(NGR):
                                ins = v.max(gt8[:, t, k, :], sel[:, t, 8 * k:8 * k + 8])
                        step(ins)
                        step(v.tensor_tensor(gs[:, :, :], gt8[:, :, :, 0], gt8[:, :, :, 1], ALU.add))
                        for t in range(NT):
                            ins = v.max(top[:, t, :], gs[:, t, :])
                        step(ins)
                        for t in range(NT):
                            ins = v.max_index(topi[:, t, :], top[:, t, :], gs[:, t, :])
                        step(ins)
                        step(v.tensor_copy(topf[:, :, 0:TOPG], topi[:, :, 0:TOPG]))
                        g4 = pr[:, :, 0:TOPG, 0:NGR]
                        step(v.tensor_tensor(pr[:, :, 0, 0:NGR], bc(iota[:, None, 0:NGR], [P, NT, NGR]), bc(topf[:, :, 0:1], [P, NT, NGR]), ALU.is_equal))
                        for k in range(1, TOPG):
                            step(v.tensor_tensor(pr[:, :, k, 0:NGR], bc(iota[:, None, 0:NGR], [P, NT, NGR]), bc(topf[:, :, k:k + 1], [P, NT, NGR]), ALU.is_equal))
                        step(v.tensor_reduce(gm[:, :, :], g4.rearrange("p t k g -> p t g k"), AX_X, ALU.add))
                        step(v.tensor_tensor(sel[:, :, :].rearrange("p t (g k) -> p t g k", k=8), sel[:, :, :].rearrange("p t (g k) -> p t g k", k=8),
                                             bc(gm[:, :, :, None], [P, NT, NGR, 8]), ALU.mult))
                    for t in range(NT):
                        ins = v.max(top[:, t, :], sel[:, t, :])
                    step(ins)
                    for t in range(NT):
                        ins = v.max_index(topi[:, t, :], top[:, t, :], sel[:, t, :])
                    step(ins)
                    step(v.tensor_copy(topf[:, :, :], topi[:, :, :]))
                    for k in range(K):
                        ins = v.tensor_tensor(oh[:, :, k, :], bc(iota[:, None, :], NE), bc(topf[:, :, k:k + 1], NE), ALU.is_equal)
                    step(ins)
                    v.tensor_reduce(mask[:, :, :], oh[:, :, :, :].rearrange("p t k e -> p t e k"), AX_X, ALU.add).then_inc(rs("mask"), 1)
                    for k in range(K):
                        ins = v.tensor_tensor(pr[:, :, k, :], oh[:, :, k, :], sc[:, :, :], ALU.mult)
                    step(ins)
                    step(v.tensor_reduce(wts[:, :, :], pr[:, :, :, :], AX_X, ALU.add))
                    if not capped:
                        step(v.tensor_reduce(row[:, 0, :], wts[:, :, :], AX_X, ALU.add))
                        step(v.tensor_scalar(row[:, 0, :], row[:, 0, :], 1e-20, None, ALU.add))
                        step(v.reciprocal(row[:, 1, :], row[:, 0, :]))
                        step(v.tensor_scalar(wts[:, :, :], wts[:, :, :], RSCALE, None, ALU.mult))
                        step(v.tensor_tensor(wts[:, :, :], wts[:, :, :], bc(row[:, 1, :, None], [P, NT, K]), ALU.mult))
                    v.wait_ge(rs("ranks"), 1)
                    step(v.memset(before[:, 0, :], 0.0))
                    for t in range(NT):
                        step(v.tensor_tensor(before[:, t + 1, :], before[:, t, :], pst[:, t, :], ALU.add))
                    step(v.tensor_tensor(sel[:, :, :], before[:, 0:NT, :], psl[:, :, :], ALU.add))
                    if capped:
                        step(v.tensor_scalar(ex[:, :, :], sel[:, :, :], float(CAP0), DROPPED, ALU.is_ge, ALU.mult))
                        step(v.tensor_tensor(sel[:, :, :], sel[:, :, :], ex[:, :, :], ALU.add))
                        step(v.tensor_tensor(sel[:, :, :], sel[:, :, :], bc(base[:, None, :], NE), ALU.add))
                    else:
                        step(v.tensor_scalar(nb[:, 0, :], before[:, NT, :], float(P - 1), None, ALU.add))
                        step(v.tensor_copy(nbi[:, 0, :], nb[:, 0, :]))
                        step(v.tensor_single_scalar(nbi[:, 1, :], nbi[:, 0, :], 7, ALU.arith_shift_right))
                        step(v.tensor_copy(nb[:, 1, :], nbi[:, 1, :]))
                        step(v.tensor_tensor_scan(nb[:, 2, :], ones[:, 0:E], nb[:, 1, :], 0.0, ALU.mult, ALU.add))
                        step(v.tensor_tensor(nb[:, 3, :], nb[:, 2, :], nb[:, 1, :], ALU.subtract))
                        step(v.tensor_scalar(nb[:, 3, :], nb[:, 3, :], float(P), None, ALU.mult))
                        step(v.tensor_tensor(sel[:, :, :], sel[:, :, :], bc(nb[:, 3:4, :], NE), ALU.add))
                        for n in range(2):
                            step(v.tensor_scalar(ex[:, n, :], nb[:, 2, :], iotab[:, n:n + 1], None, ALU.is_le))
                        step(v.tensor_reduce(ebc[:, :], ex[:, 0:2, :], AX_X, ALU.add))
                        v.tensor_scalar(ebc[:, :], ebc[:, :], float(E - 1), None, ALU.min).then_inc(rs("ebc"), 1)
                        v.wait_ge(rs("ebt"), 1)
                        step(v.tensor_copy(ebrow[:, :], psc[0:1, 0:4, :].rearrange("p a b -> p (a b)")[:, 0:NB_]))
                    for k in range(K):
                        ins = v.tensor_tensor(pr[:, :, k, :], oh[:, :, k, :], sel[:, :, :], ALU.mult)
                    step(ins)
                    step(v.tensor_reduce(slotf[:, :, :], pr[:, :, :, :], AX_X, ALU.add))
                    v.tensor_copy(sloti[:, :, :], slotf[:, :, :]).then_inc(rs("sloti"), 1)
                    if capped:
                        step(v.tensor_scalar(top[:, :, 0:K], slotf[:, :, :], float(SLOTS0), None, ALU.is_lt))
                        step(v.tensor_tensor(wts[:, :, :], wts[:, :, :], top[:, :, 0:K], ALU.mult))
                        step(v.tensor_scalar(slotf[:, :, :], slotf[:, :, :], float(SLOTS0 - 1), None, ALU.min))
                    step(v.tensor_copy(gslot[:, :, :], slotf[:, :, :]))

        x = Stage(nc, f"m{layer}x")
        xs = x.sem
        with x.ctx:
            tabi, tabf = x.sb("tabi", [TR, NTR, P], I32), x.sb("tabf", [TR, NTR, P])
            tok = x.sb("tok", [P, NB_], U32)
            tokb = x.sb("tokb", [P, 2], U32)
            xb = x.sb("xb", [P, 2, D])
            xe = x.sb("xe", [P, 2, KD, P])
            w13 = x.sb("w13", [P, 2, KD, 2, NBW, BW])
            w2 = x.sb("w2", [BW, 2, NBW, D])
            sg, hT = x.sb("sg", [BW, 2, NBW, P]), x.sb("hT", [BW, 2, NBW, P])
            yb = x.sb("yb", [P, 2, D])
            psx = [x.ps(f"psx{u}", [P, 512]) for u in range(2)]
            psh = [x.ps(f"psh{u}", [P, 2, NBW, P] if capped else [P, 4, NBW, P]) for u in range(2)]
            psyy = [x.ps(f"psy{u}", [P, 512]) for u in range(2)]
            NP2 = NB_ // 2

            with nc.Block() as block:
                @block.sync
                def _(sp):
                    sp.dma_start(tabi[:, :, :], slot_tok.rearrange("(n r p) o -> r n (p o)", p=P, r=TR)).then_inc(xs("table"), 16)
                    with sp.Fori(0, NP2) as p:
                        for u in range(2):
                            b = 2 * p + u
                            if not capped:
                                b = sp.value_load(ebrow[0:1, bass.ds(b, 1)], min_val=0, max_val=E - 1)
                            sp.wait_ge(xs("y_done", u), p)
                            sp.dma_start(w13[:, u].rearrange("p k g n i -> p (k g n i)"), d[f"m{layer}_w13"][bass.ds(b, 1)].rearrange("o p n -> (o p) n")).then_inc(xs("w", u), 16)
                            sp.dma_start(w2[:, u].rearrange("p n d -> p (n d)"), d[f"m{layer}_w2"][bass.ds(b, 1)].rearrange("o p n -> (o p) n")).then_inc(xs("w", u), 16)

                @block.gpsimd
                def _(g):
                    g.wait_ge(xs("tok"), NTR)
                    with g.Fori(0, NP2) as p:
                        for u in range(2):
                            g.wait_ge(xs("xb", u), 16 * p)
                            g.wait_ge(xs("xb_used", u), p)
                            carry_waits(g, xs("passed_pool"))
                            g.tensor_copy(tokb[:, u:u + 1], tok[:, bass.ds(2 * p + u, 1)]).then_inc(xs("tokb", u), 1)
                            g.wait_ge(xs("tokb", u), p + 1)
                            carry_waits(g, xs("passed_pool"))
                            g.indirect_dma_start(out=xb[:, u, :], out_offset=None, in_=xn,
                                                 in_offset=bass.IndirectOffsetOnAxis(ap=tokb[:, u:u + 1], axis=0)).then_inc(xs("xb", u), 16)

                @block.tensor
                def _(pe):
                    pe.wait_ge(xs("tabf"), 1)
                    for n in range(NTR):
                        pe.transpose(psx[n][:, 0:TR], tabf[:, n, :], ident[0:TR, 0:TR]).then_inc(xs("tok_turned"), 1)
                    pe.wait_ge(xs("tok"), NTR)

                    def front(p, u):
                        pe.wait_ge(xs("xb", u), 16 * (p + 1))
                        pe.wait_ge(xs("xe", u), p)
                        for k in range(KD):
                            mm = pe.transpose(psx[u][:, k * P:(k + 1) * P], xb[:, u, k * P:(k + 1) * P], ident[:, :])
                        mm.then_inc(xs("xb_used", u), 1)
                        pe.wait_ge(xs("w", u), 32 * (p + 1))
                        pe.wait_ge(xs("xe", u), p + 1)
                        pe.wait_ge(xs("hT", u), p)
                        for k2 in range(2):
                            for n in range(NBW):
                                for k in range(KD):
                                    mm = pe.matmul(psh[u][0:BW, k2, n, :], w13[:, u, k, k2, n, :], xe[:, u, k, :],
                                                   start=(k == 0), stop=(k == KD - 1))
                        mm.then_inc(xs("h_done", u), 1)

                    def back(p, u):
                        pe.wait_ge(xs("hT", u), p + 1)
                        pe.wait_ge(xs("yb", u), p)
                        for n in range(NBW):
                            mm = pe.matmul(psyy[u][:, 0:D], hT[:, u, n, :], w2[:, u, n, :], start=(n == 0), stop=(n == NBW - 1))
                        mm.then_inc(xs("y_done", u), 1)

                    pipelined(pe, front, back, NP2)

                @block.scalar
                def _(a):
                    def front(p, u):
                        a.wait_ge(xs("xb_used", u), p + 1)
                        a.wait_ge(xs("h_done", u), p)
                        a.activation(xe[:, u].rearrange("p k n -> p (k n)"), psx[u][:, 0:D], ACT.Copy).then_inc(xs("xe", u), 1)
                        a.wait_ge(xs("h_done", u), p + 1)
                        a.wait_ge(xs("hT", u), p)
                        a.activation(sg[:, u], psh[u][0:BW, 0], ACT.Silu).then_inc(xs("sg", u), 1)

                    def back(p, u):
                        a.wait_ge(xs("y_stored", u), 16 * p)
                        a.wait_ge(xs("y_done", u), p + 1)
                        a.activation(yb[:, u, :], psyy[u][:, 0:D], ACT.Copy).then_inc(xs("yb", u), 1)
                        a.wait_ge(xs("yb", u), p + 1)
                        a.dma_start(y.rearrange("(b p) d -> b p d", p=P)[bass.ds(2 * p + u, 1)].rearrange("o p d -> (o p) d"), yb[:, u, :]).then_inc(xs("y_stored", u), 16)

                    pipelined(a, front, back, NP2)
                    for u in range(2):
                        a.wait_ge(xs("y_stored", u), 16 * NP2)

                @block.vector
                def _(v):
                    v.wait_ge(xs("table"), 16)
                    v.tensor_copy(tabf[:, :, :], tabi[:, :, :]).then_inc(xs("tabf"), 1)
                    for n in range(NTR):
                        v.wait_ge(xs("tok_turned"), n + 1)
                        v.tensor_copy(tok[:, n * TR:(n + 1) * TR], psx[n][:, 0:TR]).then_inc(xs("tok"), 1)
                    with v.Fori(0, NP2) as p:
                        for u in range(2):
                            v.wait_ge(xs("sg", u), p + 1)
                            v.wait_ge(xs("y_done", u), p)
                            v.tensor_tensor(hT[:, u], sg[:, u], psh[u][0:BW, 1], ALU.mult).then_inc(xs("hT", u), 1)

        c = Stage(nc, f"m{layer}c")
        cs = c.sem
        with c.ctx:
            ws13, ws2 = c.sb("ws13", [P, KD, 2, NSB, BW]), c.sb("ws2", [BW, NSB, D])
            sgs, hs = c.sb("sgs", [BW, 2, GT]), c.sb("hs", [BW, NSB, GT])
            gi = c.sb("gi", [P, 2, K], U32)
            yg = c.sb("yg", [P, 2, K, D])
            pgu = [c.ps(f"pgu{n}", [P, 2, GT]) for n in range(2)]
            pso = [c.ps(f"pso{n}", [P, 512]) for n in range(2)]
            UPG = NSB

            with nc.Block() as block:
                @block.sync
                def _(sp):
                    sp.dma_start(ws13[:, :, :, :, :], d[f"m{layer}_ws13"]).then_inc(cs("weights"), 16)
                    sp.dma_start(ws2[:, :, :], d[f"m{layer}_ws2"]).then_inc(cs("weights"), 16)

                @block.gpsimd
                def _(g):
                    with g.Fori(0, NT // 2) as p:
                        for u in range(2):
                            g.wait_ge(cs("yg", u), 16 * K * p)
                            g.wait_ge(cs("yg_used", u), p)
                            carry_waits(g, cs("passed_pool"))
                            g.tensor_copy(gi[:, u, :], gslot[:, bass.ds(2 * p + u, 1), :].rearrange("p o k -> p (o k)")).then_inc(cs("gi", u), 1)
                            g.wait_ge(cs("gi", u), p + 1)
                            carry_waits(g, cs("passed_pool"))
                            for k in range(K):
                                g.indirect_dma_start(out=yg[:, u, k, :], out_offset=None, in_=y,
                                                     in_offset=bass.IndirectOffsetOnAxis(ap=gi[:, u, k:k + 1], axis=0)).then_inc(cs("yg", u), 16)

                @block.tensor
                def _(pe):
                    pe.wait_ge(cs("weights"), 32)
                    with pe.Fori(0, NG) as g:
                        for n in range(NSB):
                            s = n % 2
                            nth = (NSB + 1 - s) // 2
                            pe.wait_ge(cs("hs", s), nth * g + n // 2)
                            for k2 in range(2):
                                for k in range(KD):
                                    mm = pe.matmul(pgu[s][0:BW, k2, :], ws13[:, k, k2, n, :], xnT[:, k, bass.ds(GT * g, GT)],
                                                   start=(k == 0), stop=(k == KD - 1))
                            mm.then_inc(cs("gu", s), 1)
                        for s in range(min(2, NSB)):
                            nth = (NSB + 1 - s) // 2
                            pe.wait_ge(cs("hs", s), nth * (g + 1))
                        for t in range(4):
                            pe.wait_ge(cs("x_added", t % 2), 2 * g + t // 2)
                            for n in range(NSB):
                                mm = pe.matmul(pso[t % 2][:, 0:D], hs[:, n, t * P:(t + 1) * P], ws2[:, n, :], start=(n == 0), stop=(n == NSB - 1))
                            mm.then_inc(cs("out", t % 2), 1)

                @block.scalar
                def _(a):
                    with a.Fori(0, NG) as g:
                        for n in range(NSB):
                            s = n % 2
                            nth = (NSB + 1 - s) // 2
                            a.wait_ge(cs("hs", s), nth * g + n // 2)
                            a.wait_ge(cs("gu", s), nth * g + n // 2 + 1)
                            a.activation(sgs[:, s, :], pgu[s][0:BW, 0, :], ACT.Silu).then_inc(cs("sgs", s), 1)

                @block.vector
                def _(v):
                    with v.Fori(0, NG) as g:
                        if NSB:
                            for n in range(NSB):
                                s = n % 2
                                nth = (NSB + 1 - s) // 2
                                if n == 0:
                                    for q in range(2):
                                        v.wait_ge(cs("out", q), 2 * g)
                                v.wait_ge(cs("sgs", s), nth * g + n // 2 + 1)
                                v.tensor_tensor(hs[:, n, :], sgs[:, s, :], pgu[s][0:BW, 1, :], ALU.mult).then_inc(cs("hs", s), 1)
                        for t in range(4):
                            u = t % 2
                            k_ = 2 * g + t // 2
                            xt = X[:, bass.ds(4 * g + t, 1), :].rearrange("p o d -> p (o d)")
                            v.wait_ge(cs("out", u), k_ + 1)
                            v.tensor_tensor(xt, xt, pso[u][:, 0:D], ALU.add).then_inc(cs("x_added", u), 1)
                            v.wait_ge(cs("x_added", u), k_ + 1)
                            v.wait_ge(cs("yg", u), 16 * K * (k_ + 1))
                            carry_waits(v, cs("passed_dve"))
                            for k in range(K):
                                ins = v.scalar_tensor_tensor(xt, yg[:, u, k, :], wts[:, bass.ds(4 * g + t, 1), k:k + 1].rearrange("p o k -> p (o k)"),
                                                             xt, ALU.mult, ALU.add)
                                if k < K - 1:
                                    ins.then_inc(cs("acc", u), 1)
                                    v.wait_ge(cs("acc", u), (K - 1) * k_ + k + 1)
                                    carry_waits(v, cs("passed_dve"))
                            ins.then_inc(cs("yg_used", u), 1)


def stage_moe0(nc, e, d):
    stage_moe(nc, e, d, 0)


def stage_moe1(nc, e, d):
    stage_moe(nc, e, d, 1)


def stage_cross(nc, e, d):
    st = Stage(nc, "x")
    sb, ps, sem = st.sb, st.ps, st.sem
    X, ident = e["X"], e["ident"]
    F2, HP, NR = 2, H // 2, 4
    ISC = float(HK) ** -0.5

    with st.ctx:
        wq, wk, wv, wo = (sb(n, [P, KD, D]) for n in ("wq", "wk", "wv", "wo"))
        bq, bk, bv = (sb(n, [P, F2]) for n in ("bq", "bk", "bv"))
        bo, one = sb("bo", [1, D]), sb("one", [1, P])
        maskr, bm = sb("maskr", [P, SK]), sb("bm", [P, 2])
        xnT, qT = sb("xnT", [P, KD, T]), sb("qT", [P, F2, T])
        c = sb("c", [P, 2, KD, SK])
        kT = sb("kT", [P, 2, F2, SK])
        val = sb("val", [P, 2, 2, D])
        qblk = sb("qblk", [P, 2, F2, 2, S])
        s = sb("s", [P, 2, HP, SK])
        mx, nm, sm, rs_ = (sb(n, [P, 2, HP]) for n in ("mx", "nm", "sm", "rs"))
        pT = sb("pT", [P, 2, HP, 2, P])
        oc, oT = sb("oc", [P, D]), sb("oT", [P, F2, P])

        LOADS = [(wq[:, :, :], d["x_wq"]), (wk[:, :, :], d["x_wk"]), (wv[:, :, :], d["x_wv"]), (wo[:, :, :], d["x_wo"]),
                 (bq[:, :], d["x_bq"]), (bk[:, :], d["x_bk"]), (bv[:, :], d["x_bv"]), (bo[:, :], d["x_bo"]),
                 (one[:, :], d["ones"][0:1, :]), (maskr[0:S, :], d["x_mask"]), (maskr[S:P, :], d["x_mask"]), (bm[:, :], d["pair_mask"])]
        W_ALL = 16 * len(LOADS)

        q = Stage(nc, "xq")
        qs = q.sem
        with q.ctx:
            ln = LayerNorm(q, e)
            pq = [q.ps(f"pq{n}", [P, GT]) for n in range(2)]
            with nc.Block() as block:
                @block.sync
                def _(sp):
                    for dst, src in LOADS:
                        sp.dma_start(dst, src).then_inc(qs("weights"), 16)
                    sp.wait_ge(qs("weights"), W_ALL)

                @block.tensor
                def _(pe):
                    pe.wait_ge(qs("weights"), W_ALL)
                    with pe.Fori(0, NT // 2) as p:
                        for u in range(2):
                            ln.tensor_tile(pe, p, u)
                    for u in range(2):
                        pe.wait_ge(qs("xnT_ready", u), NT // 2)
                    with pe.Fori(0, NG) as g:
                        for f in range(F2):
                            pe.wait_ge(qs("q_out", f), g)
                            for k in range(KD):
                                mm = pe.matmul(pq[f][:, :], wq[:, k, f * P:(f + 1) * P], xnT[:, k, bass.ds(GT * g, GT)], start=(k == 0), stop=(k == KD - 1))
                            mm.then_inc(qs("q_done", f), 1)

                @block.scalar
                def _(a):
                    ln.scalar_std(a)
                    with a.Fori(0, NT // 2) as p:
                        for u in range(2):
                            ln.scalar_tile(a, p, u, xnT[:, :, bass.ds(P * (2 * p + u), P)])
                    a.wait_ge(qs("weights"), W_ALL)
                    with a.Fori(0, NG) as g:
                        for f in range(F2):
                            a.wait_ge(qs("q_done", f), g + 1)
                            carry_waits(a, qs("passed_act"))
                            a.activation(qT[:, f, bass.ds(GT * g, GT)], pq[f][:, :], ACT.Identity, bias=bq[:, f:f + 1]).then_inc(qs("q_out", f), 1)

                @block.vector
                def _(v):
                    ln.vector_stats(v)
                    with v.Fori(0, NT // 2) as p:
                        for u in range(2):
                            ln.vector_tile(v, p, u)

        psS = ps("psS", [P, NR, F2, SK])
        psP = [ps(f"psP{n}", [P, 512]) for n in range(2)]
        psK = ps("psK", [P, 2, D])
        psO = ps("psO", [P, 512])

        def schedule(eng, front, back, finish, n=NT):
            front(0, 0)
            front(0, 1)
            back(0, 0)
            front(1, 0)
            back(0, 1)
            with eng.Fori(1, n - 1) as p:
                front(p, 1)
                finish(p - 1)
                back(p, 0)
                front(p + 1, 0)
                back(p, 1)
            front(n - 1, 1)
            finish(n - 2)
            back(n - 1, 0)
            back(n - 1, 1)
            finish(n - 1)

        with nc.Block() as block:
            @block.sync
            def _(sp):
                ctx_v = d["ctxT"].rearrange("(g b) p k n -> g b p k n", b=2)
                with sp.Fori(0, NT) as p:
                    for u in range(2):
                        sp.wait_ge(sem("v_done", u), p)
                        sp.dma_start(c[:, u], ctx_v[bass.ds(p, 1), u].rearrange("o p k n -> (o p) k n")
                                     ).then_inc(sem("ctx", u), 16)

            @block.gpsimd
            def _(g):
                with g.Fori(0, NT) as p:
                    for u in range(2):
                        g.wait_ge(sem("s_done", u), p)
                        carry_waits(g, sem("passed_pool"))
                        for f in range(F2):
                            ins = g.tensor_tensor(qblk[:, u, f], bc(qT[:, f, bass.ds(P * p + S * u, S)].rearrange("p (o n) -> p o n", o=1), [P, 2, S]),
                                                  bc(bm[:, :, None], [P, 2, S]), ALU.mult)
                        ins.then_inc(sem("qblk", u), 1)

            @block.tensor
            def _(pe):
                def front(p, u):
                    b = 2 * p + u
                    pe.wait_ge(sem("ctx", u), 16 * (p + 1))
                    pe.wait_ge(sem("v_out"), b)
                    for f in range(F2):
                        for k in range(KD):
                            mm = pe.matmul(psK[:, f, :], wk[:, k, f * P:(f + 1) * P], c[:, u, k, :], start=(k == 0), stop=(k == KD - 1))
                    mm.then_inc(sem("k_done"), 1)
                    pe.wait_ge(sem("k_out"), b + 1)
                    for t in range(2):
                        for k in range(KD):
                            mm = pe.matmul(psK[:, t, :], c[:, u, k, t * P:(t + 1) * P], wv[:, k, :], start=(k == 0), stop=(k == KD - 1))
                    mm.then_inc(sem("v_done", u), 1)
                    pe.wait_ge(sem("qblk", u), p + 1)
                    pe.wait_ge(sem("masked"), b)
                    for f in range(F2):
                        for r in range(NR):
                            mm = pe.matmul(psS[:, r, f, :], qblk[32 * r:32 * r + 32, u, f].rearrange("p a n -> p (a n)"),
                                           kT[32 * r:32 * r + 32, u, f, :], start=True, stop=True)
                    mm.then_inc(sem("s_done", u), 1)

                def back(p, u):
                    b = 2 * p + u
                    pe.wait_ge(sem("exp", u), p + 1)
                    for j in range(4):
                        pe.wait_ge(sem("pT", j % 2), 2 * b + j // 2)
                        for i in range(4):
                            hp, t = 2 * j + i // 2, i % 2
                            mm = pe.transpose(psP[j % 2][:, i * P:(i + 1) * P], s[:, u, hp, t * P:(t + 1) * P], ident[:, :])
                        mm.then_inc(sem("p_turned", j % 2), 1)
                    for n in range(2):
                        pe.wait_ge(sem("pT", n), 2 * b + 2)
                    pe.wait_ge(sem("oc"), b)
                    pe.wait_ge(sem("x_added"), p)
                    for hp in range(HP):
                        r, f = hp // 2, hp % 2
                        for t in range(2):
                            mm = pe.matmul(psO[:, hp * 32:hp * 32 + 32], pT[:, u, hp, t, :], val[:, u, t, f * P + 32 * r:f * P + 32 * r + 32],
                                           start=(t == 0), stop=(t == 1))
                    mm.then_inc(sem("o_done", u), 1)

                def finish(p):
                    pe.wait_ge(sem("oc"), 2 * p + 2)
                    for f in range(F2):
                        mm = pe.transpose(psO[:, f * P:(f + 1) * P], oc[:, f * P:(f + 1) * P], ident[:, :])
                    mm.then_inc(sem("oc_turned"), 1)
                    pe.wait_ge(sem("oT"), p + 1)
                    pe.matmul(psO[:, 0:D], one[:, :], bo[:, :], start=True, stop=False)
                    for f in range(F2):
                        mm = pe.matmul(psO[:, 0:D], oT[:, f, :], wo[:, f, :], start=False, stop=(f == F2 - 1))
                    mm.then_inc(sem("y_done"), 1)

                schedule(pe, front, back, finish)

            @block.scalar
            def _(a):
                def front(p, u):
                    b = 2 * p + u
                    a.wait_ge(sem("s_done", u), p)
                    a.wait_ge(sem("k_done"), b + 1)
                    for f in range(F2):
                        ins = a.activation(kT[:, u, f, :], psK[:, f, :], ACT.Identity, bias=bk[:, f:f + 1])
                    ins.then_inc(sem("k_out"), 1)
                    a.wait_ge(sem("o_done", u), p)
                    a.wait_ge(sem("v_done", u), p + 1)
                    a.activation(val[:, u], psK[:, :, :], ACT.Copy).then_inc(sem("v_out"), 1)

                def back(p, u):
                    b = 2 * p + u
                    a.wait_ge(sem("nm", u), p + 1)
                    for hp in range(HP):
                        ins = a.activation(s[:, u, hp, :], s[:, u, hp, :], ACT.Exp, bias=nm[:, u, hp:hp + 1], scale=ISC,
                                           accum_out=sm[:, u, hp:hp + 1])
                    ins.then_inc(sem("exp", u), 1)
                    for j in range(1, 4, 2):
                        a.wait_ge(sem("p_turned", 1), 2 * b + j // 2 + 1)
                        a.activation(pT[:, u, 2 * j:2 * j + 2].rearrange("p h t n -> p (h t n)"), psP[1][:, :], ACT.Copy).then_inc(sem("pT", 1), 1)

                def finish(p):
                    a.wait_ge(sem("y_done"), p)
                    a.wait_ge(sem("oc_turned"), p + 1)
                    for f in range(F2):
                        ins = a.activation(oT[:, f, :], psO[:, f * P:(f + 1) * P], ACT.Identity, bias=bv[:, f:f + 1])
                    ins.then_inc(sem("oT"), 1)

                schedule(a, front, back, finish)

            @block.vector
            def _(v):
                def front(p, u):
                    b = 2 * p + u
                    v.wait_ge(sem("s_done", u), p + 1)
                    v.wait_ge(sem("o_done", u), p)
                    carry_waits(v, sem("passed_dve"))
                    for hp in range(HP):
                        r, f = hp // 2, hp % 2
                        ins = v.tensor_tensor_reduce(s[:, u, hp, :], psS[:, r, f, :], maskr[:, :], 1.0, -3.0e38, ALU.add, ALU.max,
                                                     mx[:, u, hp:hp + 1])
                    ins.then_inc(sem("masked"), 1)
                    v.wait_ge(sem("masked"), b + 1)
                    v.tensor_scalar(nm[:, u, :], mx[:, u, :], -ISC, None, ALU.mult).then_inc(sem("nm", u), 1)

                def back(p, u):
                    b = 2 * p + u
                    for j in range(0, 4, 2):
                        v.wait_ge(sem("p_turned", 0), 2 * b + j // 2 + 1)
                        v.tensor_copy(pT[:, u, 2 * j:2 * j + 2].rearrange("p h t n -> p (h t n)"), psP[0][:, :]).then_inc(sem("pT", 0), 1)
                    v.wait_ge(sem("exp", u), p + 1)
                    v.reciprocal(rs_[:, u, :], sm[:, u, :]).then_inc(sem("rsum", u), 1)
                    v.wait_ge(sem("rsum", u), p + 1)
                    v.wait_ge(sem("oc_turned"), p)
                    v.wait_ge(sem("o_done", u), p + 1)
                    for h2 in range(2):
                        lo = S * h2
                        src = psO[lo:lo + S, 0:HP * 32].rearrange("p (r f c) -> p r f c", r=NR, f=F2)[:, :, :, HK * h2:HK * h2 + HK]
                        w = bc(rs_[lo:lo + S, u, :].rearrange("p (r f) -> p r f", f=F2)[:, :, :, None], [S, NR, F2, HK])
                        out = oc[S * u:S * u + S, :].rearrange("p (f r c) -> p r f c", f=F2, r=NR)[:, :, :, HK * h2:HK * h2 + HK]
                        ins = v.tensor_tensor(out, src, w, ALU.mult)
                    ins.then_inc(sem("oc"), 1)

                def finish(p):
                    v.wait_ge(sem("y_done"), p + 1)
                    carry_waits(v, sem("passed_dve"))
                    xt = X[:, bass.ds(p, 1), :].rearrange("p o d -> p (o d)")
                    v.tensor_tensor(xt, xt, psO[:, 0:D], ALU.add).then_inc(sem("x_added"), 1)

                schedule(v, front, back, finish)


def stage_self(nc, e, d):
    st = Stage(nc, "s")
    sb, ps, sem = st.sb, st.ps, st.sem
    X, ident = e["X"], e["ident"]
    F2, HP, NR = 2, H // 2, 4
    ISC = float(HK) ** -0.5

    with st.ctx:
        wq, wqs, wk, wks, wv, wo = (sb(n, [P, KD, D]) for n in ("wq", "wqs", "wk", "wks", "wv", "wo"))
        cos, sin = sb("cos", [P, S]), sb("sin", [P, S])
        causal, bm = sb("causal", [P, S]), sb("bm", [P, 2])
        xnT = sb("xnT", [P, KD, T])
        qT, kT = sb("qT", [P, F2, T]), sb("kT", [P, F2, T])
        vall = sb("vall", [P, NT, D])

        q = Stage(nc, "sq")
        qs = q.sem
        with q.ctx:
            ln = LayerNorm(q, e)
            xts = q.sb("xts", [P, 2, KD, P])
            ra = q.sb("ra", [P, 2, 2, GT])
            psv = q.ps("psv", [P, 512])
            pr = [[q.ps(f"pr{n}{m}", [P, GT]) for m in range(2)] for n in range(2)]

            LOADS = [(wq[:, :, :], d["s_wq"]), (wqs[:, :, :], d["s_wqs"]), (wk[:, :, :], d["s_wk"]), (wks[:, :, :], d["s_wks"]),
                     (wv[:, :, :], d["s_wv"]), (wo[:, :, :], d["s_wo"]), (cos[:, :], d["s_cos"]), (sin[:, :], d["s_sin"]),
                     (causal[:, :], d["s_causal"]), (bm[:, :], d["pair_mask"])]
            W_ALL = 16 * len(LOADS)
            UNITS = [(w, ws, out, f) for w, ws, out in ((wq, wqs, qT), (wk, wks, kT)) for f in range(F2)]

            with nc.Block() as block:
                @block.sync
                def _(sp):
                    for dst, src in LOADS:
                        sp.dma_start(dst, src).then_inc(qs("weights"), 16)
                    sp.wait_ge(qs("weights"), W_ALL)

                @block.tensor
                def _(pe):
                    pe.wait_ge(qs("weights"), W_ALL)
                    with pe.Fori(0, NT // 2) as p:
                        for u in range(2):
                            ln.tensor_tile(pe, p, u)
                            pe.wait_ge(qs("xts", u), p + 1)
                            pe.wait_ge(qs("v_out", 1 - u), p + u)
                            for k in range(KD):
                                mm = pe.matmul(psv[:, 0:D], xts[:, u, k, :], wv[:, k, :], start=(k == 0), stop=(k == KD - 1))
                            mm.then_inc(qs("v_done", u), 1)
                    with pe.Fori(0, NG) as g:
                        for i, (w, ws, _, f) in enumerate(UNITS):
                            n = i % 2
                            pe.wait_ge(qs("turned", n), 4 * g + 2 * (i // 2))
                            for m, ww in enumerate((w, ws)):
                                for k in range(KD):
                                    mm = pe.matmul(pr[n][m][:, :], ww[:, k, f * P:(f + 1) * P], xnT[:, k, bass.ds(GT * g, GT)], start=(k == 0), stop=(k == KD - 1))
                            mm.then_inc(qs("qk", n), 1)

                @block.scalar
                def _(a):
                    ln.scalar_std(a)
                    with a.Fori(0, NT // 2) as p:
                        for u in range(2):
                            t = 2 * p + u
                            a.wait_ge(qs("v_done", u), p)
                            ln.scalar_tile(a, p, u, xnT[:, :, bass.ds(P * t, P)])
                            a.activation(xts[:, u], ln.psT[:, 0:D].rearrange("p (k n) -> p k n", k=KD), ACT.Copy).then_inc(qs("xts", u), 1)
                            a.wait_ge(qs("v_done", u), p + 1)
                            carry_waits(a, qs("passed_act"))
                            a.activation(vall[:, bass.ds(t, 1), :].rearrange("p o d -> p (o d)"), psv[:, 0:D], ACT.Copy).then_inc(qs("v_out", u), 1)

                @block.vector
                def _(v):
                    ln.vector_stats(v)
                    with v.Fori(0, NT // 2) as p:
                        for u in range(2):
                            ln.vector_tile(v, p, u)
                    v.wait_ge(qs("weights"), W_ALL)
                    with v.Fori(0, NG) as g:
                        for i, (_, _, out, f) in enumerate(UNITS):
                            n = i % 2
                            v.wait_ge(qs("qk", n), 2 * g + i // 2 + 1)
                            shape = [P, GT // S, S]
                            for m, tab in enumerate((cos, sin)):
                                v.tensor_tensor(ra[:, n, m, :].rearrange("p (b s) -> p b s", s=S), pr[n][m][:, :].rearrange("p (b s) -> p b s", s=S),
                                                bc(tab[:, None, :], shape), ALU.mult).then_inc(qs("turned", n), 1)
                            v.wait_ge(qs("turned", n), 4 * g + 2 * (i // 2) + 2)
                            carry_waits(v, qs("passed_dve"))
                            v.tensor_tensor(out[:, f, bass.ds(GT * g, GT)], ra[:, n, 0, :], ra[:, n, 1, :], ALU.add).then_inc(qs("rotated", n), 1)

        kb, vb = sb("kb", [P, 2, F2, P]), sb("vb", [P, 2, D])
        qblk = sb("qblk", [P, 2, F2, 2, 2, S])
        s = sb("s", [P, 2, NR, F2, 2, S])
        mx = sb("mx", [P, 2, 4, 4 * NR])
        pT = sb("pT", [P, 2, HP, P])
        oc, oT = sb("oc", [P, D]), sb("oT", [P, F2, P])
        psS = ps("psS", [P, NR, 512])
        psP = ps("psP", [P, 2, 512])
        psO = ps("psO", [P, 2, 512])
        NP2 = NT // 2

        def schedule(eng, front, back, finish):
            front(0, 0)
            front(0, 1)
            back(0, 0)
            with eng.Fori(1, NP2) as p:
                front(p, 0)
                finish(p - 1, 0)
                back(p - 1, 1)
                front(p, 1)
                finish(p - 1, 1)
                back(p, 0)
            finish(NP2 - 1, 0)
            back(NP2 - 1, 1)
            finish(NP2 - 1, 1)

        with nc.Block() as block:
            @block.gpsimd
            def _(g):
                with g.Fori(0, NP2) as p:
                    for u in range(2):
                        t = 2 * p + u
                        g.wait_ge(sem("s_done", u), p)
                        g.wait_ge(sem("o_done", u), p)
                        carry_waits(g, sem("passed_pool"))
                        for f in range(F2):
                            for b in range(2):
                                g.tensor_tensor(qblk[:, u, f, b], bc(qT[:, f, bass.ds(P * t + S * b, S)].rearrange("p (o n) -> p o n", o=1), [P, 2, S]),
                                                bc(bm[:, :, None], [P, 2, S]), ALU.mult)
                        g.tensor_copy(kb[:, u], kT[:, :, bass.ds(P * t, P)])
                        g.tensor_copy(vb[:, u, :], vall[:, bass.ds(t, 1), :].rearrange("p o d -> p (o d)")).then_inc(sem("ready", u), 1)

            @block.tensor
            def _(pe):
                def front(p, u):
                    pe.wait_ge(sem("ready", u), p + 1)
                    pe.wait_ge(sem("masked", 1 - u), p + u)
                    for f in range(F2):
                        for b in range(2):
                            for r in range(NR):
                                o = (2 * f + b) * S
                                mm = pe.matmul(psS[:, r, o:o + S], qblk[32 * r:32 * r + 32, u, f, b].rearrange("p a n -> p (a n)"),
                                               kb[32 * r:32 * r + 32, u, f, S * b:S * b + S], start=True, stop=True)
                    mm.then_inc(sem("s_done", u), 1)

                def back(p, u):
                    pe.wait_ge(sem("exp", u), p + 1)
                    pe.wait_ge(sem("pT", 1 - u), p + u)
                    for hp in range(HP):
                        mm = pe.transpose(psP[:, hp // 4, (hp % 4) * P:(hp % 4 + 1) * P], s[:, u, hp // 2, hp % 2].rearrange("p b k -> p (b k)"), ident[:, :])
                    mm.then_inc(sem("p_turned", u), 1)
                    pe.wait_ge(sem("pT", u), p + 1)
                    for hp in range(HP):
                        r, f = hp // 2, hp % 2
                        for b in range(2):
                            mm = pe.matmul(psO[:, b, hp * 32:hp * 32 + 32], pT[S * b:S * b + S, u, hp, :],
                                           vb[S * b:S * b + S, u, f * P + 32 * r:f * P + 32 * r + 32], start=True, stop=True)
                    mm.then_inc(sem("o_done", u), 1)

                def finish(p, u):
                    t = 2 * p + u
                    pe.wait_ge(sem("oc"), t + 1)
                    for f in range(F2):
                        mm = pe.transpose(psO[:, 0, f * P:(f + 1) * P], oc[:, f * P:(f + 1) * P], ident[:, :])
                    mm.then_inc(sem("oc_turned"), 1)
                    pe.wait_ge(sem("oT"), t + 1)
                    for f in range(F2):
                        mm = pe.matmul(psO[:, 1, 0:D], oT[:, f, :], wo[:, f, :], start=(f == 0), stop=(f == F2 - 1))
                    mm.then_inc(sem("y_done"), 1)
                    pe.wait_ge(sem("x_added"), t + 1)

                schedule(pe, front, back, finish)

            @block.scalar
            def _(a):
                def front(p, u):
                    pass

                def back(p, u):
                    a.wait_ge(sem("shifted", u), p + 1)
                    a.activation(s[:, u], s[:, u], ACT.Exp, scale=ISC).then_inc(sem("exp", u), 1)
                    a.wait_ge(sem("p_turned", u), p + 1)
                    a.activation(pT[:, u].rearrange("p h n -> p (h n)"), psP[:, :, :].rearrange("p h n -> p (h n)"), ACT.Copy).then_inc(sem("pT", u), 1)

                def finish(p, u):
                    t = 2 * p + u
                    a.wait_ge(sem("y_done"), t)
                    a.wait_ge(sem("oc_turned"), t + 1)
                    a.activation(oT[:, :, :].rearrange("p f n -> p (f n)"), psO[:, 0, 0:D], ACT.Copy).then_inc(sem("oT"), 1)

                schedule(a, front, back, finish)

            @block.vector
            def _(v):
                def front(p, u):
                    v.wait_ge(sem("s_done", u), p + 1)
                    v.wait_ge(sem("o_done", u), p)
                    carry_waits(v, sem("passed_dve"))
                    sv = s[:, u].rearrange("p r f b k -> p r (f b) k")
                    flat = s[:, u].rearrange("p r f b k -> p (r f b) k")
                    v.tensor_tensor(sv, psS[:, :, 0:4 * S].rearrange("p r (o k) -> p r o k", k=S), bc(causal[:, None, None, :], [P, NR, 4, S]),
                                    ALU.add).then_inc(sem("masked", u), 1)
                    v.wait_ge(sem("masked", u), p + 1)
                    v.tensor_reduce(mx[:, u, 0, :], flat, AX_X, ALU.max).then_inc(sem("max", u), 1)
                    v.wait_ge(sem("max", u), p + 1)
                    v.tensor_tensor(flat, flat, bc(mx[:, u, 0, :, None], [P, 4 * NR, S]), ALU.subtract).then_inc(sem("shifted", u), 1)

                def back(p, u):
                    t = 2 * p + u
                    v.wait_ge(sem("exp", u), p + 1)
                    v.tensor_reduce(mx[:, u, 1, :], s[:, u].rearrange("p r f b k -> p (r f b) k"), AX_X, ALU.add).then_inc(sem("sum", u), 1)
                    v.wait_ge(sem("sum", u), p + 1)
                    v.reciprocal(mx[:, u, 2, :], mx[:, u, 1, :]).then_inc(sem("rsum", u), 1)
                    v.wait_ge(sem("rsum", u), p + 1)
                    v.wait_ge(sem("oc_turned"), t)
                    v.wait_ge(sem("o_done", u), p + 1)
                    for b in range(2):
                        for h2 in range(2):
                            lo = S * h2
                            src = psO[lo:lo + S, b, 0:HP * 32].rearrange("p (r f c) -> p r f c", r=NR, f=F2)[:, :, :, HK * h2:HK * h2 + HK]
                            w = bc(mx[lo:lo + S, u, 2, :].rearrange("p (r f b) -> p r f b", f=F2, b=2)[:, :, :, b:b + 1], [S, NR, F2, HK])
                            out = oc[S * b:S * b + S, :].rearrange("p (f r c) -> p r f c", f=F2, r=NR)[:, :, :, HK * h2:HK * h2 + HK]
                            ins = v.tensor_tensor(out, src, w, ALU.mult)
                    ins.then_inc(sem("oc"), 1)

                def finish(p, u):
                    t = 2 * p + u
                    v.wait_ge(sem("y_done"), t + 1)
                    carry_waits(v, sem("passed_dve"))
                    xt = X[:, bass.ds(t, 1), :].rearrange("p o d -> p (o d)")
                    v.tensor_tensor(xt, xt, psO[:, 1, 0:D], ALU.add).then_inc(sem("x_added"), 1)

                schedule(v, front, back, finish)


def build(nc, d, out, stages):
    ctx = ExitStack()
    with ctx:
        X = ctx.enter_context(nc.sbuf_tensor("X", [P, NT, D], F32))
        ident = ctx.enter_context(nc.sbuf_tensor("ident", [P, P], F32))
        loaded = ctx.enter_context(nc.semaphore("x_loaded"))
        stored = ctx.enter_context(nc.semaphore("x_stored"))
        e = {"X": X, "ident": ident}
        with nc.Block() as block:
            @block.sync
            def _(sp):
                sp.dma_start(X[:, :, :], d["x"].rearrange("(t p) d -> p t d", p=P)).then_inc(loaded, 16)
                sp.dma_start(ident[:, :], d["ident"]).then_inc(loaded, 16)
                sp.wait_ge(loaded, 32)
        for s in stages:
            with nc.cleanup_on_exit():
                s(nc, e, d)
        with nc.Block() as block:
            @block.sync
            def _(sp):
                sp.dma_start(out.rearrange("(t p) d -> p t d", p=P), X[:, :, :]).then_inc(stored, 16)
                sp.wait_ge(stored, 16)


def rope_tables(pos, dim, base=10000.0):
    half = dim // 2
    inv = (np.float32(1.0) / np.power(np.float32(base), np.arange(half, dtype=np.float32) / np.float32(half))).astype(np.float32)
    ang = pos.astype(np.float32)[:, None] * inv
    c, s = np.cos(ang).astype(np.float32), np.sin(ang).astype(np.float32)
    return np.concatenate([c, c], 1), np.concatenate([-s, s], 1)


def layout(i):
    f = {}
    c = np.ascontiguousarray
    f["x"] = c(i["x"].reshape(T, D))
    f["ident"] = np.eye(P, dtype=np.float32)
    ctx = i["ctx_1024"]
    f["ctxT"] = c(ctx.reshape(B, SK, KD, P).transpose(0, 3, 2, 1))
    f["seg"] = c(i["itok_BxS_0_511"].reshape(NT, P).T)
    w = i["L0_xattn_w_kv_comp"]
    f["kcompT"] = c(w.T)
    f["kcomp"] = c(w.reshape(KD, P, KVC).transpose(1, 0, 2))
    f["krope"] = c(i["L0_xattn_w_k_rope"])
    f["qup"] = c(i["L0_xattn_w_q_up"].reshape(QC, H, HD).transpose(2, 1, 0))
    f["kup"] = c(i["L0_xattn_w_k_up"].reshape(KVC, H, HD).transpose(2, 1, 0))
    f["vup"] = c(i["L0_xattn_w_v_up"].reshape(KVC, H, HD).transpose(2, 1, 0))
    f["wout"] = c(i["L0_xattn_w_out"].reshape(H, HD, D).transpose(1, 0, 2))
    f["wqd"] = c(i["L0_xattn_w_q_down"].reshape(KD, P, QC).transpose(1, 0, 2))
    f["qrope"] = c(i["L0_xattn_w_q_rope"].reshape(QC, H, RD))
    ck, sk = rope_tables(np.arange(SK), RD)
    f["cosk"] = c(np.tile(ck.reshape(2, P, RD), (2, 1, 1)).transpose(1, 0, 2))
    f["sink"] = c(np.tile(sk.reshape(2, P, RD), (2, 1, 1)).transpose(1, 0, 2))
    cq, sq = rope_tables(np.arange(P) % S, RD)
    f["cosq"], f["sinq"] = cq, -sq
    b = np.arange(T).reshape(NT, P).T // S
    f["rows"] = c(np.stack([b * SK, KROWS + b], 1).astype(np.float32))
    f["meanw"] = np.full((P, 1), 1.0 / SK, np.float32)
    f["b_win"] = c(i["L0_attn_W_in"].T.reshape(KD, P, 2 * DI).transpose(1, 0, 2))
    f["b_convw"] = c(i["L0_attn_conv_w"].reshape(NCH, P, KC).transpose(1, 0, 2))
    f["b_convb"] = c(i["L0_attn_conv_b"].reshape(NCH, P).T)
    f["b_wx"] = c(i["L0_attn_W_x"].T.reshape(NCH, P, DTR + 2 * NST).transpose(1, 0, 2))
    f["b_wdt"] = c(i["L0_attn_W_dt"].T)
    f["b_bdt"] = c(i["L0_attn_b_dt"].reshape(NCH, P).T)
    f["b_alog"] = c(i["L0_attn_A_log"].reshape(NCH, P, NST).transpose(1, 0, 2))
    f["b_dp"] = c(i["L0_attn_Dp"].reshape(NCH, P).T)
    f["b_wout"] = c(i["L0_attn_W_out"].T.reshape(NCH, P, D).transpose(1, 0, 2))
    f["iota_e"] = np.arange(E, dtype=np.float32)
    f["slot_base"] = np.arange(E, dtype=np.float32) * CAP0
    f["iota_b"] = c(np.arange(2 * P, dtype=np.float32).reshape(2, P).T)
    f["tokid"] = c(np.arange(T, dtype=np.int32).reshape(NT, P).T)
    f["ltri"] = np.triu(np.ones((P, P), np.float32), 1)
    f["ones"] = np.ones((P, P), np.float32)

    def by_row(w):
        return w.reshape(KD, P, -1).transpose(1, 0, 2)

    f["m0_gw"], f["m0_gb"] = c(by_row(i["L0_ffn_gate_w"].T)), c(i["L0_ffn_gate_b"])
    w1, w3 = (i[f"L0_ffn_{n}"].reshape(E, 2, IH, KD, P) for n in ("w1", "w3"))
    f["m0_w13"] = c(np.stack([w1, w3], 1).transpose(0, 5, 4, 1, 2, 3).reshape(E, P, -1))
    f["m0_w2"] = c(i["L0_ffn_w2"].reshape(E, D, 2, IH).transpose(0, 3, 2, 1).reshape(E, IH, -1))
    w1, w3 = (i[f"L0_ffn_{n}"].reshape(SB0, IH, KD, P) for n in ("ws1", "ws3"))
    f["m0_ws13"] = c(np.stack([w1, w3], 0).transpose(4, 3, 0, 1, 2))
    f["m0_ws2"] = c(i["L0_ffn_ws2"].reshape(D, SB0, IH).transpose(2, 1, 0))
    f["m1_gw"], f["m1_gb"] = c(by_row(i["L1_ffn_w_router"])), c(i["L1_ffn_b_router"])
    w1, w3 = (i[f"L1_ffn_{n}"].reshape(E, KD, P, F1) for n in ("we_gate", "we_up"))
    f["m1_w13"] = c(np.stack([w1, w3], 1).transpose(0, 3, 2, 1, 4).reshape(E, P, -1))
    f["m1_w2"] = c(i["L1_ffn_we_down"])
    w1, w3 = (i[f"L1_ffn_{n}"].reshape(KD, P, F1) for n in ("ws_gate", "ws_up"))
    f["m1_ws13"] = c(np.stack([w1, w3], 0).transpose(2, 1, 0, 3).reshape(P, KD, 2, 1, F1))
    f["m1_ws2"] = c(i["L1_ffn_ws_down"].reshape(F1, 1, D))
    for n in "qkv":
        f[f"x_w{n}"] = c(by_row(i[f"L1_xattn_W{n}"].transpose(1, 0, 2).reshape(D, D)))
        f[f"x_b{n}"] = c(i[f"L1_xattn_b{n}"].reshape(2, P).T)
    f["x_wo"] = c(by_row(i["L1_xattn_Wo"].T))
    f["x_bo"] = c(i["L1_xattn_bo"].reshape(1, D))
    f["x_mask"] = c(i["fside_SxS2_0"])
    f["pair_mask"] = (np.arange(P)[:, None] // HK % 2 == np.arange(2)).astype(np.float32)
    swap = np.arange(D).reshape(H, 2, HK // 2)[:, ::-1].reshape(D)
    for n in "qk":
        w = i[f"L1_attn_W{n}"]
        f[f"s_w{n}"], f[f"s_w{n}s"] = c(by_row(w.T)), c(by_row(w[swap].T))
    f["s_wv"], f["s_wo"] = c(by_row(i["L1_attn_Wv"].T)), c(by_row(i["L1_attn_Wo"].T))
    cs, sn = rope_tables(np.arange(S), HK)
    f["s_cos"], f["s_sin"] = c(np.tile(cs.T, (P // HK, 1))), c(np.tile(sn.T, (P // HK, 1)))
    f["s_causal"] = np.where(np.arange(S)[None, :] > np.arange(P)[:, None] % S, NEG, 0.0).astype(np.float32)
    return f


STAGES = [stage_mla, stage_mamba, stage_moe0, stage_cross, stage_self, stage_moe1]
SCRATCH = {"key_table": ([KROWS + B, KVC + RD], F32), "bc_rows": ([NG, 2 * NST, GT], F32),
           "slot_tok0": ([SLOTS0, 1], I32), "slot_tok1": ([SLOTS1, 1], I32), "xn0": ([T, D], F32), "xn1": ([T, D], F32),
           "y0": ([SLOTS0, D], F32), "y1": ([SLOTS1, D], F32)}


def kernel(**inputs):
    import concourse.bacc as bacc
    from concourse.bass_utils import run_bass_kernel_spmd

    nc = bacc.Bacc("TRN2", target_bir_lowering=False, num_devices=1)
    arrays = layout({k: np.asarray(v) for k, v in inputs.items()})
    d = {n: nc.dram_tensor(f"in_{n}", a.shape, mybir.dt.from_np(a.dtype), kind="ExternalInput").ap()
         for n, a in arrays.items()}
    for n, (shape, dt) in SCRATCH.items():
        d[n] = nc.dram_tensor(f"scratch_{n}", shape, dt).ap()
    out = nc.dram_tensor("out_x", [T, D], F32, kind="ExternalOutput").ap()
    build(nc, d, out, STAGES)
    r = run_bass_kernel_spmd(nc, [{f"in_{n}": a for n, a in arrays.items()}], core_ids=[0])
    return r.results[0]["out_x"].reshape(B, S, D)
```

```python
from contextlib import ExitStack

import numpy as np

import concourse.bass as bass
from concourse import mybir

F32 = mybir.dt.float32
I32 = mybir.dt.int32
U32 = mybir.dt.uint32
ALU = mybir.AluOpType
ACT = mybir.ActivationFunctionType
AX_X = mybir.AxisListType.X

P = 128
B, S, D = 32, 64, 256
SK = 256
T = B * S
NT = T // P
KD = D // P
H = 16
LN_EPS = 1e-5
NEG = -1.0e30

HD, KVC, QC, RD = 64, 64, 96, 64
LOOK = 3
KROWS = B * SK

DI, NST, DTR, KC = 512, 16, 64, 4
NCH = DI // P
GT = 512
NG = T // GT

E = 64
CAP0, K0, I0, SI0 = 128, 6, 176, 352
K1, F1, NGR, TOPG, RSCALE = 8, 128, 8, 4, 2.5
IH = I0 // 2
SB0 = SI0 // IH
SLOTS0 = E * CAP0
NB1 = T * K1 // P + E
SLOTS1 = NB1 * P
DROPPED = 1.0e6

HK = 16


class Stage:

    def __init__(self, nc, name):
        self.nc, self.name, self.ctx, self.sems = nc, name, ExitStack(), {}

    def sb(self, name, shape, dt=F32):
        return self.ctx.enter_context(self.nc.sbuf_tensor(f"{self.name}_{name}", shape, dt))

    def ps(self, name, shape):
        return self.ctx.enter_context(self.nc.psum_tensor(f"{self.name}_{name}", shape, F32))

    def sem(self, name, u=0):
        if (name, u) not in self.sems:
            self.sems[name, u] = self.nc.alloc_semaphore(f"{self.name}_{name}{u}")
        return self.sems[name, u]


def bc(ap, shape):
    return ap.broadcast_to(shape)


class LayerNorm:

    def __init__(self, st, e):
        self.st, self.e = st, e
        self.stats = st.sb("stats", [P, NT, 6])
        self.mean = st.sb("mean", [P, NT])
        self.rstd = st.sb("rstd", [P, NT])
        self.tmp = st.sb("lntmp", [P, 2, NT])
        self.xs = st.sb("xs", [P, 2, D])
        self.psT = st.ps("psT", [P, 512])

    def vector_stats(self, v):
        st, X = self.st, self.e["X"]
        for t in range(NT):
            v.bn_stats(self.stats[:, t, :], X[:, t, :]).then_inc(st.sem("bn"), 1)
        v.wait_ge(st.sem("bn"), NT)
        s = self.stats
        v.tensor_tensor(self.tmp[:, 0, :], s[:, :, 1], s[:, :, 4], ALU.add).then_inc(st.sem("ln"), 1)
        v.tensor_tensor(self.tmp[:, 1, :], s[:, :, 1], s[:, :, 4], ALU.subtract).then_inc(st.sem("ln"), 1)
        v.tensor_tensor(self.rstd[:, :], s[:, :, 2], s[:, :, 5], ALU.add).then_inc(st.sem("ln"), 1)
        v.wait_ge(st.sem("ln"), 3)
        v.tensor_scalar(self.mean[:, :], self.tmp[:, 0, :], 0.5, None, ALU.mult).then_inc(st.sem("ln"), 1)
        v.scalar_tensor_tensor(self.tmp[:, 1, :], self.tmp[:, 1, :], 0.25, self.tmp[:, 1, :],
                               ALU.mult, ALU.mult).then_inc(st.sem("ln"), 1)
        v.tensor_scalar(self.rstd[:, :], self.rstd[:, :], 1.0 / D, LN_EPS, ALU.mult, ALU.add).then_inc(st.sem("ln"), 1)
        v.wait_ge(st.sem("ln"), 6)
        v.tensor_tensor(self.tmp[:, 0, :], self.rstd[:, :], self.tmp[:, 1, :], ALU.add).then_inc(st.sem("ln_var"), 1)
        v.wait_ge(st.sem("ln_std"), 1)
        v.reciprocal(self.rstd[:, :], self.tmp[:, 1, :]).then_inc(st.sem("ln_rstd"), 1)
        v.wait_ge(st.sem("ln_rstd"), 1)

    def scalar_std(self, a):
        st = self.st
        a.wait_ge(st.sem("ln_var"), 1)
        a.activation(self.tmp[:, 1, :], self.tmp[:, 0, :], ACT.Sqrt).then_inc(st.sem("ln_std"), 1)

    def vector_tile(self, v, p, u):
        st, X, t = self.st, self.e["X"], 2 * p + u
        v.wait_ge(st.sem("xs_free", u), p)
        v.tensor_scalar(self.xs[:, u, :], X[:, t, :], self.mean[:, bass.ds(t, 1)],
                        self.rstd[:, bass.ds(t, 1)], ALU.subtract, ALU.mult).then_inc(st.sem("xs_ready", u), 1)

    def tensor_tile(self, pe, p, u):
        st = self.st
        pe.wait_ge(st.sem("xs_ready", u), p + 1)
        pe.wait_ge(st.sem("xnT_ready", 1 - u), p + u)
        for k in range(KD):
            mm = pe.transpose(self.psT[:, k * P:(k + 1) * P], self.xs[:, u, k * P:(k + 1) * P], self.e["ident"][:, :])
        mm.then_inc(st.sem("xs_free", u), 1)

    def scalar_tile(self, a, p, u, out):
        st = self.st
        a.wait_ge(st.sem("xs_free", u), p + 1)
        carry_waits(a, st.sem("passed_act"))
        a.activation(out, self.psT[:, 0:D].rearrange("p (k n) -> p k n", k=KD), ACT.Copy).then_inc(st.sem("xnT_ready", u), 1)


def pipelined(eng, front, back, n=NT // 2):
    front(0, 0)
    with eng.Fori(0, n - 1) as p:
        front(p, 1)
        back(p, 0)
        front(p + 1, 0)
        back(p, 1)
    front(n - 1, 1)
    back(n - 1, 0)
    back(n - 1, 1)


def in_steps(eng, parts, n, R, order=None):
    lag = len(parts) - 1
    assert n > lag // R

    def step(p, j, begun=lag + 1, over=0):
        for i in order or range(lag + 1):
            a = j + lag - i
            if parts[i] and over <= i < begun:
                parts[i](p + a // R, a % R)

    for j in range(-lag, 0):
        step(0, j, begun=lag + j + 1)
    rounds = n - 1 - (lag - 1) // R if lag else n
    with eng.Fori(0, rounds) as p:
        for j in range(R):
            step(p, j)
    for b in range(R * rounds, R * n):
        step(b // R, b % R, over=lag + b - R * n + 1)


def carry_waits(eng, passed):
    eng.sem_inc(passed, 1)


def stage_mla(nc, e, d):
    st = Stage(nc, "a")
    sb, ps, sem = st.sb, st.ps, st.sem
    X, ident = e["X"], e["ident"]
    table = d["key_table"]
    W2 = KVC + RD

    with st.ctx:
        kcompT, krope = sb("kcompT", [KVC, D]), sb("krope", [KVC, RD])
        qup, kup, vup, wout = (sb("qup", [HD, H, QC]), sb("kup", [HD, H, KVC]),
                               sb("vup", [HD, H, KVC]), sb("wout", [HD, H, D]))
        wqd = sb("wqd", [P, KD, QC])
        wk = sb("wk", [P, KD, W2])
        wq = sb("wq", [QC, H, W2])
        wo = sb("wo", [P, H // 2, D])
        cosk, sink = sb("cosk", [P, 4, RD]), sb("sink", [P, 4, RD])
        cosq, sinq = sb("cosq", [P, RD]), sb("sinq", [P, RD])
        segi, segf = sb("segi", [P, NT], I32), sb("segf", [P, NT])
        rows = sb("rows", [P, 2, NT])
        key = sb("key", [P, LOOK, NT])
        good = sb("good", [P, LOOK, NT])
        none = sb("none", [P, 2, NT])
        idx = sb("idx", [P, LOOK, NT])
        meanw = sb("meanw", [P, 1])
        c = sb("c", [P, 2, 2, KD, SK])
        tab = sb("tab", [P, 2, 4, W2])
        ra = sb("ra", [P, 2, 2, 4, RD])
        mrow = sb("mrow", [1, 2, 2, W2])
        ln = LayerNorm(st, e)
        xts = sb("xts", [P, 2, KD, P])
        qc = sb("qc", [QC, 2, P])
        q = sb("q", [P, 2, H, W2])
        kg = sb("kg", [P, 2, LOOK, W2])
        kra = sb("kra", [P, 2, 2, LOOK, RD])
        idxt = sb("idxt", [P, 2, 4], U32)
        prod = sb("prod", [P, H, W2])
        prod2 = sb("prod2", [P, H, W2])
        sc = sb("sc", [P, 2, H, 4])
        mx = sb("mx", [P, 2, 4, H])
        ol = sb("ol", [P, 2, 3, H, KVC])
        oT = sb("oT", [P, 2, 8, P])
        seen = sb("seen", [P, NT, LOOK])
        psk = ps("psk", [P, 4, 512])
        psm = ps("psm", [P, 2, 512])
        aux = ps("aux", [P, 512])

        LOADS = [(kcompT[:, :], d["kcompT"]), (krope[:, :], d["krope"]), (qup[:, :, :], d["qup"]),
                 (kup[:, :, :], d["kup"]), (vup[:, :, :], d["vup"]), (wout[:, :, :], d["wout"]),
                 (wqd[:, :, :], d["wqd"]), (wk[:, :, 0:KVC], d["kcomp"]), (wq[:, :, KVC:W2], d["qrope"]),
                 (cosk[:, :, :], d["cosk"]), (sink[:, :, :], d["sink"]), (cosq[:, :], d["cosq"]),
                 (sinq[:, :], d["sinq"]), (segi[:, :], d["seg"]), (rows[:, :, :], d["rows"]),
                 (meanw[:, :], d["meanw"])]
        W_ALL = 16 * len(LOADS)
        ctx_v = d["ctxT"].rearrange("(g b) p k n -> g p b k n", b=2)
        tab_v = table[0:KROWS, :].rearrange("(g j p) c -> g p j c", p=P, j=4)
        mean_v = table[KROWS:KROWS + B, :].rearrange("(g b) c -> g (b c)", b=2)

        with nc.Block() as block:
            @block.sync
            def _(sp):
                for dst, src in LOADS:
                    sp.dma_start(dst, src).then_inc(sem("weights"), 16)
                with sp.Fori(0, NT // 2) as p:
                    for u in range(2):
                        sp.wait_ge(sem("keys_done", u), p)
                        sp.dma_start(c[:, u], ctx_v[2 * p + u]).then_inc(sem("ctx", u), 16)

            @block.tensor
            def _(pe):
                pe.wait_ge(sem("weights"), W_ALL)
                for k in range(KD):
                    mm = pe.matmul(psk[:, 0, k * RD:(k + 1) * RD], kcompT[:, k * P:(k + 1) * P], krope[:, :],
                                   start=True, stop=True)
                for h in range(H):
                    mm = pe.matmul(psk[0:QC, 1 + h // 8, (h % 8) * KVC:(h % 8 + 1) * KVC], qup[:, h, :], kup[:, h, :],
                                   start=True, stop=True)
                mm.then_inc(sem("prep"), 1)
                for r in range(4):
                    if r:
                        pe.wait_ge(sem("wo_copied"), r)
                    else:
                        pe.wait_ge(sem("prep_copied"), 2 + KD)
                    for i in range(4):
                        h = 4 * r + i
                        mm = pe.matmul(psm[64 * (h % 2):64 * (h % 2) + KVC, i // 2, 0:D], vup[:, h, :], wout[:, h, :],
                                       start=True, stop=True)
                    mm.then_inc(sem("wo_prod"), 1)
                pe.wait_ge(sem("wo_copied"), 4)

                def keys(p, u):
                    pe.wait_ge(sem("ctx", u), 16 * (p + 1))
                    pe.wait_ge(sem("rope", u), p)
                    pe.wait_ge(sem("nope", u), p)
                    for j in range(4):
                        for k in range(KD):
                            mm = pe.matmul(psk[:, u, j * P:(j + 1) * P], c[:, u, j // 2, k, (j % 2) * P:(j % 2 + 1) * P],
                                           wk[:, k, :], start=(k == 0), stop=(k == KD - 1))
                    mm.then_inc(sem("keys_done", u), 1)

                def mean(p, u):
                    pe.wait_ge(sem("rope", u), p + 1)
                    pe.wait_ge(sem("nope", u), p + 1)
                    pe.wait_ge(sem("mean_copied", u), p)
                    for j in range(4):
                        mm = pe.matmul(psm[0:1, u, (j // 2) * W2:(j // 2 + 1) * W2], meanw[:, :], tab[:, u, j, :],
                                       start=(j % 2 == 0), stop=(j % 2 == 1))
                    mm.then_inc(sem("mean_done", u), 1)

                in_steps(pe, [keys, mean], NT // 2, 2)

            @block.scalar
            def _(a):
                a.wait_ge(sem("prep"), 1)
                for k in range(KD):
                    a.activation(wk[:, k, KVC:W2], psk[:, 0, k * RD:(k + 1) * RD], ACT.Copy).then_inc(sem("prep_copied"), 1)
                for k in range(2):
                    a.activation(wq[:, 8 * k:8 * k + 8, 0:KVC], psk[0:QC, 1 + k, :].rearrange("p (h c) -> p h c", h=8),
                                 ACT.Copy).then_inc(sem("prep_copied"), 1)
                for r in range(4):
                    a.wait_ge(sem("wo_prod"), r + 1)
                    a.activation(wo[:, 2 * r:2 * r + 2, :], psm[:, 0:2, 0:D], ACT.Copy).then_inc(sem("wo_copied"), 1)

                def nope(p, u):
                    a.wait_ge(sem("keys_done", u), p + 1)
                    a.wait_ge(sem("tab_stored", u), 16 * p)
                    a.wait_ge(sem("mean_done", u), p)
                    a.activation(tab[:, u, :, 0:KVC], psk[:, u, :].rearrange("p (j c) -> p j c", j=4)[:, :, 0:KVC],
                                 ACT.Copy).then_inc(sem("nope", u), 1)

                def mean(p, u):
                    a.wait_ge(sem("mean_done", u), p + 1)
                    a.wait_ge(sem("mean_stored", u), 16 * p)
                    a.activation(mrow[:, u, :, :].rearrange("p b c -> p (b c)"), psm[0:1, u, 0:2 * W2],
                                 ACT.Copy).then_inc(sem("mean_copied", u), 1)
                    a.wait_ge(sem("mean_copied", u), p + 1)
                    a.dma_start(mean_v[bass.ds(2 * p + u, 1), :], mrow[:, u, :, :].rearrange("p b c -> p (b c)")).then_inc(sem("mean_stored", u), 16)

                in_steps(a, [nope, mean], NT // 2, 2)

            @block.gpsimd
            def _(g):
                with g.Fori(0, NT // 2) as p:
                    for u in range(2):
                        g.wait_ge(sem("rope", u), p + 1)
                        g.wait_ge(sem("nope", u), p + 1)
                        g.dma_start(tab_v[2 * p + u], tab[:, u]).then_inc(sem("tab_stored", u), 16)
                for u in range(2):
                    g.wait_ge(sem("tab_stored", u), 16 * (NT // 2))
                    g.wait_ge(sem("mean_stored", u), 16 * (NT // 2))

            @block.vector
            def _(v):
                v.wait_ge(sem("weights"), W_ALL)
                v.tensor_copy(segf[:, :], segi[:, :]).then_inc(sem("seg"), 1)
                v.wait_ge(sem("seg"), 1)
                for j in range(LOOK):
                    v.tensor_scalar(key[:, j, :], segf[:, :], float(-j), None, ALU.add).then_inc(sem("seg"), 1)
                v.tensor_scalar(none[:, 0, :], segf[:, :], 0.0, None, ALU.is_lt).then_inc(sem("seg"), 1)
                v.tensor_scalar(none[:, 1, :], segf[:, :], float(SK + LOOK - 1), None, ALU.is_ge).then_inc(sem("seg"), 1)
                v.wait_ge(sem("seg"), 6)
                v.tensor_scalar(good[:, :, :], key[:, :, :], 0.0, None, ALU.is_ge).then_inc(sem("seg"), 1)
                v.tensor_scalar(idx[:, :, :], key[:, :, :], float(SK), None, ALU.is_lt).then_inc(sem("seg"), 1)
                v.tensor_tensor(none[:, 0, :], none[:, 0, :], none[:, 1, :], ALU.add).then_inc(sem("seg"), 1)
                v.wait_ge(sem("seg"), 9)
                v.tensor_tensor(good[:, :, :], good[:, :, :], idx[:, :, :], ALU.mult).then_inc(sem("seg"), 1)
                v.wait_ge(sem("seg"), 10)
                v.tensor_scalar(idx[:, :, :], key[:, :, :], 0.0, float(SK - 1), ALU.max, ALU.min).then_inc(sem("seg"), 1)
                v.wait_ge(sem("seg"), 11)
                v.tensor_tensor(idx[:, :, :], idx[:, :, :], bc(rows[:, 0, None, :], [P, LOOK, NT]), ALU.add).then_inc(sem("seg"), 1)
                v.tensor_tensor(good[:, 0, :], good[:, 0, :], none[:, 0, :], ALU.add).then_inc(sem("seg"), 1)
                v.wait_ge(sem("seg"), 13)
                v.tensor_tensor(none[:, 1, :], rows[:, 1, :], idx[:, 0, :], ALU.subtract).then_inc(sem("seg"), 1)
                v.wait_ge(sem("seg"), 14)
                v.tensor_tensor(none[:, 1, :], none[:, 1, :], none[:, 0, :], ALU.mult).then_inc(sem("seg"), 1)
                v.wait_ge(sem("seg"), 15)
                v.tensor_tensor(idx[:, 0, :], idx[:, 0, :], none[:, 1, :], ALU.add).then_inc(sem("seg"), 1)
                v.tensor_scalar(seen[:, :, :].rearrange("p t j -> p j t"), good[:, :, :], -1.0, -NEG, ALU.add, ALU.mult).then_inc(sem("seg"), 1)
                v.wait_ge(sem("seg"), 17)
                with v.Fori(0, NT // 2) as p:
                    for u in range(2):
                        v.wait_ge(sem("nope", u), p + 1)
                        v.wait_ge(sem("tab_stored", u), 16 * p)
                        kr = psk[:, u, :].rearrange("p (j c) -> p j c", j=4)[:, :, KVC:W2]
                        hf = RD // 2
                        v.tensor_tensor(ra[:, u, 0], kr, cosk[:, :, :], ALU.mult).then_inc(sem("ra", u), 1)
                        v.tensor_tensor(ra[:, u, 1, :, 0:hf], kr[:, :, hf:RD], sink[:, :, 0:hf], ALU.mult).then_inc(sem("ra", u), 1)
                        v.tensor_tensor(ra[:, u, 1, :, hf:RD], kr[:, :, 0:hf], sink[:, :, hf:RD], ALU.mult).then_inc(sem("ra", u), 1)
                        v.wait_ge(sem("ra", u), 3 * p + 3)
                        v.tensor_tensor(tab[:, u, :, KVC:W2], ra[:, u, 0], ra[:, u, 1], ALU.add).then_inc(sem("rope", u), 1)

        SCALE = float(1.0 / np.sqrt(np.float32(HD + RD)))
        hf = RD // 2
        with nc.Block() as block:
            @block.gpsimd
            def _(g):
                def front(p, u):
                    g.wait_ge(sem("idxt", u), p + 1)
                    g.wait_ge(sem("ol", u), 3 * p)
                    carry_waits(g, sem("passed_pool"))
                    for j in range(LOOK):
                        g.indirect_dma_start(out=kg[:, u, j, :], out_offset=None, in_=table[:, :],
                                             in_offset=bass.IndirectOffsetOnAxis(ap=idxt[:, u, j:j + 1], axis=0)
                                             ).then_inc(sem("kg", u), 16)

                def products(p, u):
                    g.wait_ge(sem("q", u), p + 1)
                    g.wait_ge(sem("kr", u), p + 1)
                    g.wait_ge(sem("prod2_used", 1 - u), p + u)
                    g.tensor_tensor(prod2[:, :, :], q[:, u], bc(kg[:, u, 2:3, :], [P, H, W2]), ALU.mult).then_inc(sem("prod2", u), 1)

                def weighted(p, u):
                    g.wait_ge(sem("probs", u), p + 1)
                    g.wait_ge(sem("ol_free", u), p)
                    for j in range(LOOK):
                        g.tensor_tensor(ol[:, u, j], bc(sc[:, u, :, j:j + 1], [P, H, KVC]),
                                        bc(kg[:, u, j:j + 1, 0:KVC], [P, H, KVC]), ALU.mult).then_inc(sem("ol", u), 1)

                in_steps(g, [front, products, weighted], NT // 2, 2, order=(2, 0, 1))

            @block.tensor
            def _(pe):
                def front(p, u):
                    t = 2 * p + u
                    pe.wait_ge(sem("qc"), t)
                    ln.tensor_tile(pe, p, u)
                    pe.wait_ge(sem("xnT_ready", u), p + 1)
                    for k in range(KD):
                        mm = pe.matmul(ln.psT[0:QC, D:D + P], wqd[:, k, :], xts[:, u, k, :], start=(k == 0), stop=(k == KD - 1))
                    mm.then_inc(sem("qc_done"), 1)
                    pe.wait_ge(sem("qc"), t + 1)
                    pe.wait_ge(sem("q", 1 - u), p + u)
                    for n in range(4):
                        mm = pe.matmul(psk[:, n, :], qc[:, u, :], wq[:, 4 * n:4 * n + 4, :].rearrange("p h c -> p (h c)"),
                                       start=True, stop=True)
                    mm.then_inc(sem("q_done"), 1)

                def turn(p, u):
                    t = 2 * p + u
                    pe.wait_ge(sem("o_lat", u), p + 1)
                    pe.wait_ge(sem("oT"), t)
                    for n in range(8):
                        mm = pe.transpose(psm[:, n // 4, (n % 4) * P:(n % 4 + 1) * P],
                                          ol[:, u, 0].rearrange("p h c -> p (h c)")[:, n * P:(n + 1) * P], ident[:, :])
                    mm.then_inc(sem("ol_free", u), 1)

                def output(p, u):
                    t = 2 * p + u
                    pe.wait_ge(sem("oT"), t + 1)
                    pe.wait_ge(sem("x_added"), t)
                    for n in range(8):
                        mm = pe.matmul(aux[:, 0:D], oT[:, u, n, :], wo[:, n, :], start=(n == 0), stop=(n == 7))
                    mm.then_inc(sem("y_done"), 1)

                in_steps(pe, [front, None, turn, output], NT // 2, 2, order=(0, 3, 2))

            @block.scalar
            def _(a):
                def front(p, u):
                    t = 2 * p + u
                    a.wait_ge(sem("qc_done"), 2 * p)
                    ln.scalar_tile(a, p, u, xts[:, u])
                    a.wait_ge(sem("qc_done"), t + 1)
                    a.activation(qc[:, u, :], ln.psT[0:QC, D:D + P], ACT.Copy).then_inc(sem("qc"), 1)
                    a.wait_ge(sem("q_done"), t + 1)
                    a.wait_ge(sem("scores", u), p)
                    a.activation(q[:, u].rearrange("p h c -> p (h c)"), psk[:, :, :].rearrange("p n c -> p (n c)"), ACT.Copy).then_inc(sem("q", u), 1)

                def exps(p, u):
                    a.wait_ge(sem("shifted", u), p + 1)
                    a.activation(sc[:, u, :, 0:LOOK], sc[:, u, :, 0:LOOK], ACT.Exp).then_inc(sem("exp", u), 1)

                def turned(p, u):
                    a.wait_ge(sem("ol_free", u), p + 1)
                    a.activation(oT[:, u].rearrange("p n c -> p (n c)"), psm[:, :, :].rearrange("p n c -> p (n c)"), ACT.Copy).then_inc(sem("oT"), 1)

                ln.scalar_std(a)
                in_steps(a, [front, exps, turned], NT // 2, 2)

            @block.vector
            def _(v):
                def front(p, u):
                    v.wait_ge(sem("kg", u), 48 * p)
                    v.tensor_copy(idxt[:, u, 0:LOOK], idx[:, :, bass.ds(2 * p + u, 1)].rearrange("p j o -> p (j o)")).then_inc(sem("idxt", u), 1)
                    ln.vector_tile(v, p, u)

                def scores(p, u):
                    t = 2 * p + u
                    v.wait_ge(sem("kg", u), 48 * (p + 1))
                    kk = kg[:, u, :, KVC:W2]
                    v.tensor_tensor(kra[:, u, 0], kk, bc(cosq[:, None, :], [P, LOOK, RD]), ALU.mult).then_inc(sem("kra", u), 1)
                    v.tensor_tensor(kra[:, u, 1, :, 0:hf], kk[:, :, hf:RD], bc(sinq[:, None, 0:hf], [P, LOOK, hf]), ALU.mult).then_inc(sem("kra", u), 1)
                    v.tensor_tensor(kra[:, u, 1, :, hf:RD], kk[:, :, 0:hf], bc(sinq[:, None, hf:RD], [P, LOOK, hf]), ALU.mult).then_inc(sem("kra", u), 1)
                    v.wait_ge(sem("kra", u), 3 * p + 3)
                    v.tensor_tensor(kk, kra[:, u, 0], kra[:, u, 1], ALU.add).then_inc(sem("kr", u), 1)
                    v.wait_ge(sem("kr", u), p + 1)
                    v.wait_ge(sem("q", u), p + 1)
                    for j in range(LOOK - 1):
                        v.tensor_tensor(prod[:, :, :], q[:, u], bc(kg[:, u, j:j + 1, :], [P, H, W2]), ALU.mult).then_inc(sem("prod"), 1)
                        v.wait_ge(sem("prod"), 2 * t + j + 1)
                        v.tensor_reduce(sc[:, u, :, j], prod[:, :, :], AX_X, ALU.add).then_inc(sem("sdot", u), 1)
                        v.wait_ge(sem("sdot", u), 2 * p + j + 1)
                    v.wait_ge(sem("prod2", u), p + 1)
                    v.tensor_reduce(sc[:, u, :, 2], prod2[:, :, :], AX_X, ALU.add).then_inc(sem("prod2_used", u), 1)
                    v.wait_ge(sem("prod2_used", u), p + 1)
                    s3 = sc[:, u, :, 0:LOOK]
                    v.scalar_tensor_tensor(s3, s3, SCALE, bc(seen[:, bass.ds(t, 1), :], [P, H, LOOK]),
                                           ALU.mult, ALU.add).then_inc(sem("scores", u), 1)
                    v.wait_ge(sem("scores", u), p + 1)
                    v.tensor_reduce(mx[:, u, 0, :], s3, AX_X, ALU.max).then_inc(sem("smax", u), 1)
                    v.wait_ge(sem("smax", u), p + 1)
                    v.tensor_tensor(s3, s3, bc(mx[:, u, 0, :, None], [P, H, LOOK]), ALU.subtract).then_inc(sem("shifted", u), 1)
                    v.wait_ge(sem("exp", u), p + 1)
                    v.tensor_reduce(mx[:, u, 1, :], s3, AX_X, ALU.add).then_inc(sem("ssum", u), 1)
                    v.wait_ge(sem("ssum", u), p + 1)
                    v.reciprocal(mx[:, u, 2, :], mx[:, u, 1, :]).then_inc(sem("srec", u), 1)
                    v.wait_ge(sem("srec", u), p + 1)
                    v.tensor_tensor(s3, s3, bc(mx[:, u, 2, :, None], [P, H, LOOK]), ALU.mult).then_inc(sem("probs", u), 1)

                def summed(p, u):
                    v.wait_ge(sem("ol", u), 3 * p + 3)
                    v.tensor_tensor(ol[:, u, 0], ol[:, u, 0], ol[:, u, 1], ALU.add).then_inc(sem("osum", u), 1)
                    v.wait_ge(sem("osum", u), p + 1)
                    v.tensor_tensor(ol[:, u, 0], ol[:, u, 0], ol[:, u, 2], ALU.add).then_inc(sem("o_lat", u), 1)

                def added(p, u):
                    t = 2 * p + u
                    v.wait_ge(sem("y_done"), t + 1)
                    v.tensor_tensor(X[:, bass.ds(t, 1), :].rearrange("p o d -> p (o d)"), X[:, bass.ds(t, 1), :].rearrange("p o d -> p (o d)"),
                                    aux[:, 0:D], ALU.add).then_inc(sem("x_added"), 1)

                ln.vector_stats(v)
                in_steps(v, [front, scores, summed, added], NT // 2, 2)


def stage_mamba(nc, e, d):
    st = Stage(nc, "b")
    sb, ps, sem = st.sb, st.ps, st.sem
    X, ident = e["X"], e["ident"]
    NB, CQ = GT // S, 2
    NQ = NST // CQ
    HB, DB = 8, 4
    PG, PD = NQ * NCH // HB, NQ * NCH // DB
    LP = S + KC - 1

    with st.ctx:
        win = sb("win", [P, KD, 2 * DI])
        convw, convb = sb("convw", [P, NCH, KC]), sb("convb", [P, NCH])
        wx = sb("wx", [P, NCH, DTR + 2 * NST])
        wdt, bdt = sb("wdt", [DTR, DI]), sb("bdt", [P, NCH])
        A, Dp = sb("A", [P, NCH, NST]), sb("Dp", [P, NCH])
        wout = sb("wout", [P, NCH, D])
        ln = LayerNorm(st, e)
        xnT = sb("xnT", [P, KD, T])
        xcp = sb("xcp", [P, NCH, NB, LP])
        xz = sb("xz", [P, 2, 2 * NCH, GT])
        th = sb("th", [P, NCH, GT])
        delta, dx = sb("delta", [P, 2, NCH, GT]), sb("dx", [P, 2, NCH, GT])
        dbc = sb("dbc", [DTR + 2 * NST, GT])
        bcb = sb("bcb", [P, 2, 2, CQ, GT])
        dA = sb("dA", [P, DB, CQ, GT])
        h = sb("h", [P, HB, CQ, GT])
        yz = sb("yz", [P, NCH, GT])
        psy = ps("psy", [P, NCH, GT])
        psw = ps("psw", [P, 2, GT])
        pso = ps("pso", [P, 512])

        LOADS = [(win[:, :, :], d["b_win"]), (convw[:, :, :], d["b_convw"]), (convb[:, :], d["b_convb"]),
                 (wx[:, :, :], d["b_wx"]), (wdt[:, :], d["b_wdt"]), (bdt[:, :], d["b_bdt"]),
                 (A[:, :, :], d["b_alog"]), (Dp[:, :], d["b_dp"]), (wout[:, :, :], d["b_wout"])]
        W_ALL = 16 * len(LOADS)
        rows = d["bc_rows"]
        PER = (7, 6)

        def buf(t, g):
            v = t[:, bass.ds(g % 2, 1)]
            return v.rearrange("p o c n -> p (o c) n")

        def wait_bank(eng, name, g, r, more):
            eng.wait_ge(sem(name, r % 2), PER[r % 2] * g + r // 2 + more)

        NP = 15
        TENSOR_AT = (0, 1, 3, 4, 6, 7, 9, 10, None, 16, 20, 21, 22, 23, None)
        SCALAR_AT = (3, 4, 6, 7, 9, 10, 12, 13, 14, 18, 23, 24, 25, 26, 27)
        VECTOR_AT = (4, 5, 8, 9) + (None,) * 11
        POOL_AT = (None,) * 14 + (31,)

        def interleave(eng, piece, step, at):
            for r in range(NP):
                if at[r] is not None:
                    piece(0, r)
            with eng.Fori(0, NG - 1) as g:
                for i in range(NQ * NCH):
                    step(g, i)
                    for r in range(NP):
                        if at[r] == i:
                            piece(g + 1, r)
            for i in range(NQ * NCH):
                step(NG - 1, i)

        with nc.Block() as block:
            @block.sync
            def _(sp):
                for dst, src in LOADS:
                    sp.dma_start(dst, src).then_inc(sem("weights"), 16)

                def load(g, nq, first=False):
                    if nq == 0:
                        sp.wait_ge(sem("rows_stored"), 16 * (g + 1))
                    if not first:
                        last = NCH * (nq - 1) - 1
                        sp.wait_ge(sem("hc", last % HB), PG * g + last // HB + 1)
                    for k in range(2):
                        src = rows[bass.ds(g, 1), k * NST + CQ * nq:k * NST + CQ * nq + CQ, :].rearrange("o n t -> (o n t)")
                        sp.dma_start(bcb[:, nq % 2, k].rearrange("p n t -> p (n t)"), src.partition_broadcast(P)).then_inc(sem("bcast", nq % 2), 16)

                load(0, 0, True)
                load(0, 1, True)
                with sp.Fori(0, NG - 1) as g:
                    for nq in range(2, NQ):
                        load(g, nq)
                    load(g + 1, 0)
                    load(g + 1, 1)
                for nq in range(2, NQ):
                    load(NG - 1, nq)

            @block.tensor
            def _(pe):
                with pe.Fori(0, NT // 2) as p:
                    for u in range(2):
                        ln.tensor_tile(pe, p, u)
                for u in range(2):
                    pe.wait_ge(sem("xnT_ready", u), NT // 2)
                pe.wait_ge(sem("weights"), W_ALL)

                def piece(g, r):
                    if r < 8:
                        wait_bank(pe, "psw_free", g, r, 0)
                        for k in range(KD):
                            mm = pe.matmul(psw[:, r % 2, :], win[:, k, r * P:(r + 1) * P], xnT[:, k, bass.ds(GT * g, GT)],
                                           start=(k == 0), stop=(k == KD - 1))
                        mm.then_inc(sem("psw_ready", r % 2), 1)
                    elif r == 9:
                        pe.wait_ge(sem("silu"), g + 1)
                        wait_bank(pe, "psw_free", g, 8, 0)
                        for c in range(NCH):
                            mm = pe.matmul(psw[0:DTR + 2 * NST, 0, :], wx[:, c, :], buf(xz, g)[:, c, :], start=(c == 0), stop=(c == NCH - 1))
                        mm.then_inc(sem("psw_ready", 0), 1)
                    elif 10 <= r < 14:
                        c = r - 10
                        pe.wait_ge(sem("dbc"), g + 1)
                        wait_bank(pe, "psw_free", g, 9 + c, 0)
                        pe.matmul(psw[:, (9 + c) % 2, :], wdt[:, c * P:(c + 1) * P], dbc[0:DTR, :], start=True, stop=True
                                  ).then_inc(sem("psw_ready", (9 + c) % 2), 1)

                def step(g, i):
                    s, c, nq = i % HB, i % NCH, i // NCH
                    if nq == 0:
                        pe.wait_ge(sem("y", c), g)
                    pe.wait_ge(sem("hc", s), PG * g + i // HB + 1)
                    for j in range(CQ):
                        mm = pe.matmul(psy[:, c, :], ident[:, :], h[:, s, j, :], start=(nq == 0 and j == 0),
                                       stop=(nq == NQ - 1 and j == CQ - 1))
                    mm.then_inc(sem("h_free", s), 1)
                    if i == NQ * NCH - 1:
                        pe.wait_ge(sem("yz"), NCH * (g + 1))
                        for t in range(GT // P):
                            out = [pso, ln.psT][t % 2]
                            pe.wait_ge(sem("x_added", t % 2), 2 * g + t // 2)
                            for cc in range(NCH):
                                mm = pe.matmul(out[:, 0:D], yz[:, cc, t * P:(t + 1) * P], wout[:, cc, :], start=(cc == 0), stop=(cc == NCH - 1))
                            mm.then_inc(sem("out", t % 2), 1)

                interleave(pe, piece, step, TENSOR_AT)

            @block.scalar
            def _(a):
                ln.scalar_std(a)
                a.wait_ge(sem("weights"), W_ALL)
                a.activation(A[:, :, :], A[:, :, :], ACT.Exp).then_inc(sem("A_exp"), 1)
                with a.Fori(0, NT // 2) as p:
                    for u in range(2):
                        ln.scalar_tile(a, p, u, xnT[:, :, bass.ds(P * (2 * p + u), P)])
                a.wait_ge(sem("pads"), 2)

                def piece(g, r):
                    if r < 8:
                        wait_bank(a, "psw_ready", g, r, 1)
                        if r < NCH:
                            a.wait_ge(sem("conv", r), g)
                            out = xcp[:, r, :, KC - 1:LP]
                        else:
                            out = buf(xz, g)[:, r, :].rearrange("p (b l) -> p b l", b=NB)
                        carry_waits(a, sem("passed_act"))
                        a.activation(out, psw[:, r % 2, :].rearrange("p (b l) -> p b l", b=NB), ACT.Copy).then_inc(sem("psw_free", r % 2), 1)
                    elif r == 8:
                        for c in range(NCH):
                            a.wait_ge(sem("conv", c), g + 1)
                        for c in range(6, 8):
                            wait_bank(a, "psw_free", g, c, 1)
                        carry_waits(a, sem("passed_act"))
                        a.activation(buf(xz, g), buf(xz, g), ACT.Silu).then_inc(sem("silu"), 1)
                    elif r == 9:
                        wait_bank(a, "psw_ready", g, 8, 1)
                        a.wait_ge(sem("rows_stored"), 16 * g)
                        a.activation(dbc[:, :], psw[0:DTR + 2 * NST, 0, :], ACT.Copy).then_inc(sem("psw_free", 0), 1)
                        wait_bank(a, "psw_free", g, 8, 1)
                        a.sem_inc(sem("dbc"), 1)
                        a.dma_start(rows[bass.ds(g, 1)].rearrange("o n t -> (o n) t"), dbc[DTR:DTR + 2 * NST, :]).then_inc(sem("rows_stored"), 16)
                    elif 10 <= r < 14:
                        c = r - 10
                        wait_bank(a, "psw_ready", g, 9 + c, 1)
                        if c == 0:
                            a.wait_ge(sem("delta"), g)
                        src = psw[:, (9 + c) % 2, :]
                        carry_waits(a, sem("passed_act"))
                        a.activation(buf(delta, g)[:, c, :], src, ACT.Relu, bias=bdt[:, c:c + 1])
                        a.activation(th[:, c, :], src, ACT.Abs, bias=bdt[:, c:c + 1]).then_inc(sem("psw_free", (9 + c) % 2), 1)
                    elif r == 14:
                        a.wait_ge(sem("psw_free", 0), 7 * g + 7)
                        a.wait_ge(sem("psw_free", 1), 6 * g + 6)
                        a.activation(th[:, :, :], th[:, :, :], ACT.Exp, scale=-1.0).then_inc(sem("sp_exp"), 1)
                        a.wait_ge(sem("sp_exp"), g + 1)
                        a.activation(th[:, :, :], th[:, :, :], ACT.Ln, bias=1.0).then_inc(sem("sp_ln"), 1)

                def step(g, i):
                    s, c, nq = i % DB, i % NCH, i // NCH
                    if i == 0:
                        a.wait_ge(sem("delta"), g + 1)
                        a.wait_ge(sem("A_neg"), 1)
                    a.wait_ge(sem("scan", s), PD * g + i // DB)
                    carry_waits(a, sem("passed_act"))
                    dv = buf(delta, g)[:, c, :].rearrange("p (b l) -> p b l", b=NB)[:, :, 1:S]
                    for j in range(CQ):
                        n = CQ * nq + j
                        ins = a.activation(dA[:, s, j, :].rearrange("p (b l) -> p b l", b=NB)[:, :, 1:S], dv, ACT.Exp,
                                           scale=A[:, c, n:n + 1])
                    ins.then_inc(sem("dA", s), 1)

                interleave(a, piece, step, SCALAR_AT)
                a.wait_ge(sem("rows_stored"), 16 * NG)

            @block.gpsimd
            def _(g_):
                g_.memset(dA[:, :, :, :], 0.0).then_inc(sem("pads"), 1)
                g_.memset(xcp[:, :, :, 0:KC - 1], 0.0).then_inc(sem("pads"), 1)

                def piece(g, r):
                    if r == 14:
                        g_.wait_ge(sem("sp_ln"), g + 1)
                        carry_waits(g_, sem("passed_pool"))
                        g_.tensor_tensor(buf(delta, g), buf(delta, g), th[:, :, :], ALU.add).then_inc(sem("delta"), 1)
                        g_.wait_ge(sem("delta"), g + 1)
                        carry_waits(g_, sem("passed_pool"))
                        g_.tensor_tensor(buf(dx, g), buf(delta, g), buf(xz, g)[:, 0:NCH, :], ALU.mult).then_inc(sem("dx"), 1)
                        g_.wait_ge(sem("dx"), g + 1)

                def step(g, i):
                    s, c, nq = i % HB, i % NCH, i // NCH
                    g_.wait_ge(sem("h_free", s), PG * g + i // HB)
                    if c == 0:
                        g_.wait_ge(sem("bcast", nq % 2), 32 * (NQ // 2 * g + nq // 2 + 1))
                    carry_waits(g_, sem("passed_pool"))
                    g_.tensor_tensor(h[:, s], bc(buf(dx, g)[:, c:c + 1, :], [P, CQ, GT]), bcb[:, nq % 2, 0], ALU.mult).then_inc(sem("bx", s), 1)

                interleave(g_, piece, step, POOL_AT)

            @block.vector
            def _(v):
                ln.vector_stats(v)
                with v.Fori(0, NT // 2) as p:
                    for u in range(2):
                        ln.vector_tile(v, p, u)
                v.wait_ge(sem("weights"), W_ALL)
                v.wait_ge(sem("A_exp"), 1)
                v.tensor_scalar(A[:, :, :], A[:, :, :], -1.0, None, ALU.mult).then_inc(sem("A_neg"), 1)
                v.wait_ge(sem("pads"), 2)

                def piece(g, r):
                    if r < NCH:
                        wait_bank(v, "psw_free", g, r, 1)
                        acc = buf(xz, g)[:, r, :].rearrange("p (b l) -> p b l", b=NB)
                        v.tensor_scalar(acc, xcp[:, r, :, 0:S], convw[:, r, 0:1], convb[:, r:r + 1], ALU.mult, ALU.add).then_inc(sem("cv", r), 1)
                        for k in range(1, KC):
                            v.wait_ge(sem("cv", r), 3 * g + k)
                            v.scalar_tensor_tensor(acc, xcp[:, r, :, k:k + S], convw[:, r, k:k + 1], acc, ALU.mult, ALU.add
                                                   ).then_inc(sem("cv" if k < KC - 1 else "conv", r), 1)

                def step(g, i):
                    s, q, c, nq = i % HB, i % DB, i % NCH, i // NCH
                    k = PG * g + i // HB
                    v.wait_ge(sem("dA", q), PD * g + i // DB + 1)
                    v.wait_ge(sem("bx", s), k + 1)
                    hs = h[:, s].rearrange("p j n -> p (j n)")
                    v.tensor_tensor_scan(hs, dA[:, q].rearrange("p j n -> p (j n)"), hs, 0.0, ALU.mult, ALU.add).then_inc(sem("scan", q), 1)
                    v.wait_ge(sem("scan", q), PD * g + i // DB + 1)
                    v.tensor_tensor(h[:, s], h[:, s], bcb[:, nq % 2, 1], ALU.mult).then_inc(sem("hc", s), 1)
                    if nq == NQ - 1:
                        v.wait_ge(sem("h_free", s), k + 1)
                        if c < 2:
                            v.wait_ge(sem("out", c), 2 * g)
                        v.scalar_tensor_tensor(yz[:, c, :], buf(xz, g)[:, c, :], Dp[:, c:c + 1], psy[:, c, :], ALU.mult, ALU.add).then_inc(sem("y", c), 1)
                        v.wait_ge(sem("y", c), g + 1)
                        v.tensor_tensor(yz[:, c, :], yz[:, c, :], buf(xz, g)[:, NCH + c, :], ALU.mult).then_inc(sem("yz"), 1)
                    if i == NQ * NCH - 1:
                        for t in range(GT // P):
                            out = [pso, ln.psT][t % 2]
                            v.wait_ge(sem("out", t % 2), 2 * g + t // 2 + 1)
                            xt = X[:, bass.ds(4 * g + t, 1), :].rearrange("p o d -> p (o d)")
                            v.tensor_tensor(xt, xt, out[:, 0:D], ALU.add).then_inc(sem("x_added", t % 2), 1)

                interleave(v, piece, step, VECTOR_AT)


def stage_moe(nc, e, d, layer):
    st = Stage(nc, f"m{layer}")
    sb, ps, sem = st.sb, st.ps, st.sem
    X, ident = e["X"], e["ident"]
    capped = layer == 0
    K = K0 if capped else K1
    NB_ = E if capped else NB1
    BW, NBW = (IH, 2) if capped else (F1, 1)
    NSB = SB0 if capped else 1
    slot_tok, xn, y = d[f"slot_tok{layer}"], d[f"xn{layer}"], d[f"y{layer}"]
    TR = NB_ // 2 if not capped else E
    NTR = NB_ // TR
    R = 4

    with st.ctx:
        xnT = sb("xnT", [P, KD, T])
        gslot = sb("gslot", [P, NT, K], U32)
        wts = sb("wts", [P, NT, K])
        ebrow = sb("ebrow", [1, NB_], U32)

        r = Stage(nc, f"m{layer}r")
        rs = r.sem
        with r.ctx:
            gw, gb = r.sb("gw", [P, KD, E]), r.sb("gb", [P, E])
            iota, ltri, ones = r.sb("iota", [P, E]), r.sb("ltri", [P, P]), r.sb("ones", [P, P])
            base, iotab = r.sb("base", [P, E]), r.sb("iotab", [P, 2])
            tokid = r.sb("tokid", [P, NT], I32)
            ln = LayerNorm(r, e)
            xts = r.sb("xts", [P, 2, KD, P])
            sc, sel = r.sb("sc", [P, NT, E]), r.sb("sel", [P, NT, E])
            ex = r.sb("ex", [P, NT, E])
            row = r.sb("row", [P, 4, NT])
            top, topi, topf = r.sb("top", [P, NT, 8]), r.sb("topi", [P, NT, 8], U32), r.sb("topf", [P, NT, 8])
            oh, pr = r.sb("oh", [P, NT, K, E]), r.sb("pr", [P, NT, K, E])
            mask = r.sb("mask", [P, NT, E])
            before = r.sb("before", [P, NT + 1, E])
            slotf = r.sb("slotf", [P, NT, K])
            sloti = r.sb("sloti", [P, NT, K], U32)
            ids, idt = r.sb("ids", [P, 2, K], U32), r.sb("idt", [P, 2], I32)
            zero = r.sb("zero", [P, NB_], I32)
            nb = r.sb("nb", [P, 4, E])
            nbi = r.sb("nbi", [P, 2, E], I32)
            ebc = r.sb("ebc", [P, 2])
            ebr = r.sb("ebr", [1, 2, P])
            gt8, gs = r.sb("gt8", [P, NT, NGR, 8]), r.sb("gs", [P, NT, NGR])
            gm = r.sb("gm", [P, NT, NGR])
            psl = r.ps("psl", [P, NT, E])
            psc = r.ps("psc", [P, NT, E])
            pst = r.ps("pst", [P, NT, E])

            LOADS = [(gw[:, :, :], d[f"m{layer}_gw"]), (gb[:, :], d[f"m{layer}_gb"].partition_broadcast(P)),
                     (iota[:, :], d["iota_e"].partition_broadcast(P)), (ltri[:, :], d["ltri"]), (ones[:, :], d["ones"]),
                     (base[:, :], d["slot_base"].partition_broadcast(P)), (iotab[:, :], d["iota_b"]), (tokid[:, :], d["tokid"])]
            W_ALL = 16 * len(LOADS)

            with nc.Block() as block:
                @block.sync
                def _(sp):
                    for dst, src in LOADS:
                        sp.dma_start(dst, src).then_inc(rs("weights"), 16)
                    sp.wait_ge(rs("zero"), 1)
                    sp.dma_start(slot_tok.rearrange("(p n) o -> p (n o)", p=P), zero[:, :]).then_inc(rs("table_clear"), 16)
                    with sp.Fori(0, NT // 2) as p:
                        for u in range(2):
                            sp.wait_ge(rs("xs_ready", u), p + 1)
                            sp.dma_start(xn.rearrange("(t p) d -> t p d", p=P)[2 * p + u], ln.xs[:, u, :]).then_inc(rs("xs_stored", u), 16)
                    for u in range(2):
                        sp.wait_ge(rs("xs_stored", u), 16 * (NT // 2))
                    sp.wait_ge(rs("table_clear"), 16)

                @block.tensor
                def _(pe):
                    pe.wait_ge(rs("weights"), W_ALL)
                    with pe.Fori(0, NT // 2) as p:
                        for u in range(2):
                            t = 2 * p + u
                            ln.tensor_tile(pe, p, u)
                            pe.wait_ge(rs("xts", u), p + 1)
                            pe.wait_ge(rs("logits_out", 1 - u), p + u)
                            for k in range(KD):
                                mm = pe.matmul(psc[:, 8 * u, :], xts[:, u, k, :], gw[:, k, :], start=(k == 0), stop=(k == KD - 1))
                            mm.then_inc(rs("logits", u), 1)
                    pe.wait_ge(rs("mask"), 1)
                    for u in range(2):
                        pe.wait_ge(rs("logits_out", u), NT // 2)
                    for n in range(2):
                        pe.matmul(psl[:, 8 * n:8 * n + 8, :].rearrange("p t e -> p (t e)"), ltri[:, :],
                                  mask[:, 8 * n:8 * n + 8, :].rearrange("p t e -> p (t e)"), start=True, stop=True)
                    for n in range(2):
                        mm = pe.matmul(pst[:, 8 * n:8 * n + 8, :].rearrange("p t e -> p (t e)"), ones[:, :],
                                       mask[:, 8 * n:8 * n + 8, :].rearrange("p t e -> p (t e)"), start=True, stop=True)
                    mm.then_inc(rs("ranks"), 1)
                    if not capped:
                        pe.wait_ge(rs("ebc"), 1)
                        for n in range(2):
                            mm = pe.matmul(psc[0:1, 0:2, :].rearrange("p a b -> p (a b)") if n == 0 else psc[0:1, 2:4, :].rearrange("p a b -> p (a b)"),
                                           ebc[:, n:n + 1], ident[:, :], start=True, stop=True)
                        mm.then_inc(rs("ebt"), 1)

                @block.scalar
                def _(a):
                    ln.scalar_std(a)
                    with a.Fori(0, NT // 2) as p:
                        for u in range(2):
                            t = 2 * p + u
                            a.wait_ge(rs("logits", u), p)
                            ln.scalar_tile(a, p, u, xnT[:, :, bass.ds(P * t, P)])
                            a.activation(xts[:, u], ln.psT[:, 0:D].rearrange("p (k n) -> p k n", k=KD), ACT.Copy).then_inc(rs("xts", u), 1)
                            a.wait_ge(rs("logits", u), p + 1)
                            carry_waits(a, rs("passed_act"))
                            a.activation(sc[:, bass.ds(t, 1), :].rearrange("p o e -> p (o e)"), psc[:, 8 * u, :], ACT.Copy).then_inc(rs("logits_out", u), 1)
                    if capped:
                        a.wait_ge(rs("shifted"), 1)
                        a.activation(ex[:, :, :], sc[:, :, :], ACT.Exp).then_inc(rs("exp"), 1)
                    else:
                        for u in range(2):
                            a.wait_ge(rs("logits_out", u), NT // 2)
                        a.activation(ex[:, :, :], sc[:, :, :], ACT.Exp, scale=-1.0).then_inc(rs("exp"), 1)

                @block.gpsimd
                def _(g):
                    g.memset(zero[:, :], 0).then_inc(rs("zero"), 1)
                    g.wait_ge(rs("weights"), W_ALL)
                    g.wait_ge(rs("table_clear"), 16)
                    g.wait_ge(rs("sloti"), 1)
                    with g.Fori(0, NT // 2) as p:
                        for u in range(2):
                            t = 2 * p + u
                            g.wait_ge(rs("scattered", u), 16 * K * p)
                            carry_waits(g, rs("passed_pool"))
                            g.tensor_copy(ids[:, u, :], sloti[:, bass.ds(t, 1), :].rearrange("p o k -> p (o k)")).then_inc(rs("ids"), 1)
                            g.tensor_copy(idt[:, u:u + 1], tokid[:, bass.ds(t, 1)]).then_inc(rs("ids"), 1)
                            g.wait_ge(rs("ids"), 2 * t + 2)
                            carry_waits(g, rs("passed_pool"))
                            for k in range(K):
                                g.indirect_dma_start(out=slot_tok, out_offset=bass.IndirectOffsetOnAxis(ap=ids[:, u, k:k + 1], axis=0),
                                                     in_=idt[:, u:u + 1], in_offset=None, bounds_check=NB_ * P - 1, oob_is_err=False
                                                     ).then_inc(rs("scattered", u), 16)
                    for u in range(2):
                        g.wait_ge(rs("scattered", u), 16 * K * (NT // 2))

                @block.vector
                def _(v):
                    v.wait_ge(rs("weights"), W_ALL)
                    n_step = [0]

                    def step(ins):
                        n_step[0] += 1
                        ins.then_inc(rs("chain"), 1)
                        v.wait_ge(rs("chain"), n_step[0])

                    ln.vector_stats(v)
                    with v.Fori(0, NT // 2) as p:
                        for u in range(2):
                            v.wait_ge(rs("xs_stored", u), 16 * p)
                            carry_waits(v, rs("passed_dve"))
                            ln.vector_tile(v, p, u)
                    for u in range(2):
                        v.wait_ge(rs("logits_out", u), NT // 2)
                    NE = [P, NT, E]
                    if capped:
                        step(v.tensor_reduce(row[:, 0, :], sc[:, :, :], AX_X, ALU.max))
                        v.tensor_tensor(sc[:, :, :], sc[:, :, :], bc(row[:, 0, :, None], NE), ALU.subtract).then_inc(rs("shifted"), 1)
                        v.wait_ge(rs("exp"), 1)
                        step(v.tensor_reduce(row[:, 1, :], ex[:, :, :], AX_X, ALU.add))
                        step(v.reciprocal(row[:, 2, :], row[:, 1, :]))
                        step(v.tensor_tensor(sc[:, :, :], ex[:, :, :], bc(row[:, 2, :, None], NE), ALU.mult))
                        step(v.tensor_tensor(sel[:, :, :], sc[:, :, :], bc(gb[:, None, :], NE), ALU.add))
                    else:
                        v.wait_ge(rs("exp"), 1)
                        step(v.tensor_scalar(ex[:, :, :], ex[:, :, :], 1.0, None, ALU.add))
                        step(v.reciprocal(sc[:, :, :], ex[:, :, :]))
                        step(v.tensor_tensor(sel[:, :, :], sc[:, :, :], bc(gb[:, None, :], NE), ALU.add))
                        for t in range(NT):
                            for k in range(NGR):
                                ins = v.max(gt8[:, t, k, :], sel[:, t, 8 * k:8 * k + 8])
                        step(ins)
                        step(v.tensor_tensor(gs[:, :, :], gt8[:, :, :, 0], gt8[:, :, :, 1], ALU.add))
                        for t in range(NT):
                            ins = v.max(top[:, t, :], gs[:, t, :])
                        step(ins)
                        for t in range(NT):
                            ins = v.max_index(topi[:, t, :], top[:, t, :], gs[:, t, :])
                        step(ins)
                        step(v.tensor_copy(topf[:, :, 0:TOPG], topi[:, :, 0:TOPG]))
                        g4 = pr[:, :, 0:TOPG, 0:NGR]
                        step(v.tensor_tensor(pr[:, :, 0, 0:NGR], bc(iota[:, None, 0:NGR], [P, NT, NGR]), bc(topf[:, :, 0:1], [P, NT, NGR]), ALU.is_equal))
                        for k in range(1, TOPG):
                            step(v.tensor_tensor(pr[:, :, k, 0:NGR], bc(iota[:, None, 0:NGR], [P, NT, NGR]), bc(topf[:, :, k:k + 1], [P, NT, NGR]), ALU.is_equal))
                        step(v.tensor_reduce(gm[:, :, :], g4.rearrange("p t k g -> p t g k"), AX_X, ALU.add))
                        step(v.tensor_tensor(sel[:, :, :].rearrange("p t (g k) -> p t g k", k=8), sel[:, :, :].rearrange("p t (g k) -> p t g k", k=8),
                                             bc(gm[:, :, :, None], [P, NT, NGR, 8]), ALU.mult))
                    for t in range(NT):
                        ins = v.max(top[:, t, :], sel[:, t, :])
                    step(ins)
                    for t in range(NT):
                        ins = v.max_index(topi[:, t, :], top[:, t, :], sel[:, t, :])
                    step(ins)
                    step(v.tensor_copy(topf[:, :, :], topi[:, :, :]))
                    for k in range(K):
                        ins = v.tensor_tensor(oh[:, :, k, :], bc(iota[:, None, :], NE), bc(topf[:, :, k:k + 1], NE), ALU.is_equal)
                    step(ins)
                    v.tensor_reduce(mask[:, :, :], oh[:, :, :, :].rearrange("p t k e -> p t e k"), AX_X, ALU.add).then_inc(rs("mask"), 1)
                    for k in range(K):
                        ins = v.tensor_tensor(pr[:, :, k, :], oh[:, :, k, :], sc[:, :, :], ALU.mult)
                    step(ins)
                    step(v.tensor_reduce(wts[:, :, :], pr[:, :, :, :], AX_X, ALU.add))
                    if not capped:
                        step(v.tensor_reduce(row[:, 0, :], wts[:, :, :], AX_X, ALU.add))
                        step(v.tensor_scalar(row[:, 0, :], row[:, 0, :], 1e-20, None, ALU.add))
                        step(v.reciprocal(row[:, 1, :], row[:, 0, :]))
                        step(v.tensor_scalar(wts[:, :, :], wts[:, :, :], RSCALE, None, ALU.mult))
                        step(v.tensor_tensor(wts[:, :, :], wts[:, :, :], bc(row[:, 1, :, None], [P, NT, K]), ALU.mult))
                    v.wait_ge(rs("ranks"), 1)
                    step(v.memset(before[:, 0, :], 0.0))
                    for t in range(NT):
                        step(v.tensor_tensor(before[:, t + 1, :], before[:, t, :], pst[:, t, :], ALU.add))
                    step(v.tensor_tensor(sel[:, :, :], before[:, 0:NT, :], psl[:, :, :], ALU.add))
                    if capped:
                        step(v.tensor_scalar(ex[:, :, :], sel[:, :, :], float(CAP0), DROPPED, ALU.is_ge, ALU.mult))
                        step(v.tensor_tensor(sel[:, :, :], sel[:, :, :], ex[:, :, :], ALU.add))
                        step(v.tensor_tensor(sel[:, :, :], sel[:, :, :], bc(base[:, None, :], NE), ALU.add))
                    else:
                        step(v.tensor_scalar(nb[:, 0, :], before[:, NT, :], float(P - 1), None, ALU.add))
                        step(v.tensor_copy(nbi[:, 0, :], nb[:, 0, :]))
                        step(v.tensor_single_scalar(nbi[:, 1, :], nbi[:, 0, :], 7, ALU.arith_shift_right))
                        step(v.tensor_copy(nb[:, 1, :], nbi[:, 1, :]))
                        step(v.tensor_tensor_scan(nb[:, 2, :], ones[:, 0:E], nb[:, 1, :], 0.0, ALU.mult, ALU.add))
                        step(v.tensor_tensor(nb[:, 3, :], nb[:, 2, :], nb[:, 1, :], ALU.subtract))
                        step(v.tensor_scalar(nb[:, 3, :], nb[:, 3, :], float(P), None, ALU.mult))
                        step(v.tensor_tensor(sel[:, :, :], sel[:, :, :], bc(nb[:, 3:4, :], NE), ALU.add))
                        for n in range(2):
                            step(v.tensor_scalar(ex[:, n, :], nb[:, 2, :], iotab[:, n:n + 1], None, ALU.is_le))
                        step(v.tensor_reduce(ebc[:, :], ex[:, 0:2, :], AX_X, ALU.add))
                        v.tensor_scalar(ebc[:, :], ebc[:, :], float(E - 1), None, ALU.min).then_inc(rs("ebc"), 1)
                        v.wait_ge(rs("ebt"), 1)
                        step(v.tensor_copy(ebrow[:, :], psc[0:1, 0:4, :].rearrange("p a b -> p (a b)")[:, 0:NB_]))
                    for k in range(K):
                        ins = v.tensor_tensor(pr[:, :, k, :], oh[:, :, k, :], sel[:, :, :], ALU.mult)
                    step(ins)
                    step(v.tensor_reduce(slotf[:, :, :], pr[:, :, :, :], AX_X, ALU.add))
                    v.tensor_copy(sloti[:, :, :], slotf[:, :, :]).then_inc(rs("sloti"), 1)
                    if capped:
                        step(v.tensor_scalar(top[:, :, 0:K], slotf[:, :, :], float(SLOTS0), None, ALU.is_lt))
                        step(v.tensor_tensor(wts[:, :, :], wts[:, :, :], top[:, :, 0:K], ALU.mult))
                        step(v.tensor_scalar(slotf[:, :, :], slotf[:, :, :], float(SLOTS0 - 1), None, ALU.min))
                    step(v.tensor_copy(gslot[:, :, :], slotf[:, :, :]))

        x = Stage(nc, f"m{layer}x")
        xs = x.sem
        with x.ctx:
            tabi, tabf = x.sb("tabi", [TR, NTR, P], I32), x.sb("tabf", [TR, NTR, P])
            tok = x.sb("tok", [P, NB_], U32)
            tokb = x.sb("tokb", [P, R, 1], U32)
            xb = x.sb("xb", [P, R, D])
            xe = x.sb("xe", [P, 2, KD, P])
            w13 = x.sb("w13", [P, R, KD, 2, NBW, BW])
            w2 = x.sb("w2", [BW, R, NBW, D])
            sg, hT = x.sb("sg", [BW, 2, NBW, P]), x.sb("hT", [BW, 2, NBW, P])
            yb = x.sb("yb", [P, R, D])
            psx = [x.ps(f"psx{u}", [P, 512]) for u in range(2)]
            psh = [x.ps(f"psh{u}", [P, 2, NBW, P] if capped else [P, 4, NBW, P]) for u in range(2)]
            psyy = [x.ps(f"psy{u}", [P, 512]) for u in range(2)]
            NR = NB_ // R

            def used(p, j):
                return (R // 2) * p + j // 2

            with nc.Block() as block:
                @block.sync
                def _(sp):
                    sp.dma_start(tabi[:, :, :], slot_tok.rearrange("(n r p) o -> r n (p o)", p=P, r=TR)).then_inc(xs("table"), 16)

                    def weights(p, j):
                        b = R * p + j
                        if not capped:
                            b = sp.value_load(ebrow[0:1, bass.ds(b, 1)], min_val=0, max_val=E - 1)
                        sp.dma_start(w13[:, j].rearrange("p k g n i -> p (k g n i)"), d[f"m{layer}_w13"][bass.ds(b, 1)].rearrange("o p n -> (o p) n")).then_inc(xs("w", j), 16)
                        sp.dma_start(w2[:, j].rearrange("p n d -> p (n d)"), d[f"m{layer}_w2"][bass.ds(b, 1)].rearrange("o p n -> (o p) n")).then_inc(xs("w", j), 16)

                    for j in range(R):
                        weights(0, j)
                    with sp.Fori(0, NR - 1) as p:
                        for j in range(R):
                            sp.wait_ge(xs("y_done", j % 2), used(p, j) + 1)
                            weights(p + 1, j)

                @block.gpsimd
                def _(g):
                    g.wait_ge(xs("tok"), NTR)
                    with g.Fori(0, NR) as p:
                        for j in range(R):
                            g.wait_ge(xs("xb", j), 16 * p)
                            g.wait_ge(xs("xb_used", j), p)
                            carry_waits(g, xs("passed_pool"))
                            g.tensor_copy(tokb[:, j, :], tok[:, bass.ds(R * p + j, 1)]).then_inc(xs("tokb", j), 1)
                            g.wait_ge(xs("tokb", j), p + 1)
                            carry_waits(g, xs("passed_pool"))
                            g.indirect_dma_start(out=xb[:, j, :], out_offset=None, in_=xn,
                                                 in_offset=bass.IndirectOffsetOnAxis(ap=tokb[:, j, :], axis=0)).then_inc(xs("xb", j), 16)

                @block.tensor
                def _(pe):
                    pe.wait_ge(xs("tabf"), 1)
                    for n in range(NTR):
                        pe.transpose(psx[n][:, 0:TR], tabf[:, n, :], ident[0:TR, 0:TR]).then_inc(xs("tok_turned"), 1)
                    pe.wait_ge(xs("tok"), NTR)

                    def turn(p, j):
                        u = j % 2
                        pe.wait_ge(xs("xb", j), 16 * (p + 1))
                        pe.wait_ge(xs("xe", u), used(p, j))
                        for k in range(KD):
                            mm = pe.transpose(psx[u][:, k * P:(k + 1) * P], xb[:, j, k * P:(k + 1) * P], ident[:, :])
                        mm.then_inc(xs("xb_used", j), 1)

                    def hidden(p, j):
                        u = j % 2
                        pe.wait_ge(xs("w", j), 32 * (p + 1))
                        pe.wait_ge(xs("xe", u), used(p, j) + 1)
                        pe.wait_ge(xs("hT", u), used(p, j))
                        for k2 in range(2):
                            for n in range(NBW):
                                for k in range(KD):
                                    mm = pe.matmul(psh[u][0:BW, k2, n, :], w13[:, j, k, k2, n, :], xe[:, u, k, :],
                                                   start=(k == 0), stop=(k == KD - 1))
                        mm.then_inc(xs("h_done", u), 1)

                    def output(p, j):
                        u = j % 2
                        pe.wait_ge(xs("hT", u), used(p, j) + 1)
                        pe.wait_ge(xs("yb", u), used(p, j))
                        for n in range(NBW):
                            mm = pe.matmul(psyy[u][:, 0:D], hT[:, u, n, :], w2[:, j, n, :], start=(n == 0), stop=(n == NBW - 1))
                        mm.then_inc(xs("y_done", u), 1)

                    in_steps(pe, [turn, hidden, output], NR, R)

                @block.scalar
                def _(a):
                    def rows(p, j):
                        u = j % 2
                        a.wait_ge(xs("xb_used", j), p + 1)
                        a.wait_ge(xs("h_done", u), used(p, j))
                        a.activation(xe[:, u].rearrange("p k n -> p (k n)"), psx[u][:, 0:D], ACT.Copy).then_inc(xs("xe", u), 1)

                    def gate(p, j):
                        u = j % 2
                        a.wait_ge(xs("h_done", u), used(p, j) + 1)
                        a.wait_ge(xs("hT", u), used(p, j))
                        a.activation(sg[:, u], psh[u][0:BW, 0], ACT.Silu).then_inc(xs("sg", u), 1)

                    def store(p, j):
                        u = j % 2
                        a.wait_ge(xs("yb", u), used(p, j) + 1)
                        a.dma_start(y.rearrange("(b p) d -> b p d", p=P)[bass.ds(R * p + j, 1)].rearrange("o p d -> (o p) d"), yb[:, j, :]).then_inc(xs("y_stored", j), 16)

                    in_steps(a, [rows, gate, store], NR, R)
                    for j in range(R):
                        a.wait_ge(xs("y_stored", j), 16 * NR)

                @block.vector
                def _(v):
                    v.wait_ge(xs("table"), 16)
                    v.tensor_copy(tabf[:, :, :], tabi[:, :, :]).then_inc(xs("tabf"), 1)
                    for n in range(NTR):
                        v.wait_ge(xs("tok_turned"), n + 1)
                        v.tensor_copy(tok[:, n * TR:(n + 1) * TR], psx[n][:, 0:TR]).then_inc(xs("tok"), 1)

                    def gated(p, j):
                        u = j % 2
                        v.wait_ge(xs("sg", u), used(p, j) + 1)
                        v.wait_ge(xs("y_done", u), used(p, j))
                        v.tensor_tensor(hT[:, u], sg[:, u], psh[u][0:BW, 1], ALU.mult).then_inc(xs("hT", u), 1)

                    def outputs(p, j):
                        u = j % 2
                        v.wait_ge(xs("y_stored", j), 16 * p)
                        v.wait_ge(xs("y_done", u), used(p, j) + 1)
                        v.tensor_copy(yb[:, j, :], psyy[u][:, 0:D]).then_inc(xs("yb", u), 1)

                    in_steps(v, [gated, outputs], NR, R)

        c = Stage(nc, f"m{layer}c")
        cs = c.sem
        with c.ctx:
            ws13, ws2 = c.sb("ws13", [P, KD, 2, NSB, BW]), c.sb("ws2", [BW, NSB, D])
            sgs, hs = c.sb("sgs", [BW, 2, GT]), c.sb("hs", [BW, NSB, GT])
            gi = c.sb("gi", [P, 2, K], U32)
            yg = c.sb("yg", [P, 2, K, D])
            pgu = [c.ps(f"pgu{n}", [P, 2, GT]) for n in range(2)]
            pso = [c.ps(f"pso{n}", [P, 512]) for n in range(2)]
            UPG = NSB

            with nc.Block() as block:
                @block.sync
                def _(sp):
                    sp.dma_start(ws13[:, :, :, :, :], d[f"m{layer}_ws13"]).then_inc(cs("weights"), 16)
                    sp.dma_start(ws2[:, :, :], d[f"m{layer}_ws2"]).then_inc(cs("weights"), 16)

                @block.gpsimd
                def _(g):
                    with g.Fori(0, NT // 2) as p:
                        for u in range(2):
                            g.wait_ge(cs("yg", u), 16 * K * p)
                            g.wait_ge(cs("yg_used", u), p)
                            carry_waits(g, cs("passed_pool"))
                            g.tensor_copy(gi[:, u, :], gslot[:, bass.ds(2 * p + u, 1), :].rearrange("p o k -> p (o k)")).then_inc(cs("gi", u), 1)
                            g.wait_ge(cs("gi", u), p + 1)
                            carry_waits(g, cs("passed_pool"))
                            for k in range(K):
                                g.indirect_dma_start(out=yg[:, u, k, :], out_offset=None, in_=y,
                                                     in_offset=bass.IndirectOffsetOnAxis(ap=gi[:, u, k:k + 1], axis=0)).then_inc(cs("yg", u), 16)

                @block.tensor
                def _(pe):
                    pe.wait_ge(cs("weights"), 32)
                    with pe.Fori(0, NG) as g:
                        for n in range(NSB):
                            s = n % 2
                            nth = (NSB + 1 - s) // 2
                            pe.wait_ge(cs("hs", s), nth * g + n // 2)
                            for k2 in range(2):
                                for k in range(KD):
                                    mm = pe.matmul(pgu[s][0:BW, k2, :], ws13[:, k, k2, n, :], xnT[:, k, bass.ds(GT * g, GT)],
                                                   start=(k == 0), stop=(k == KD - 1))
                            mm.then_inc(cs("gu", s), 1)
                        for s in range(min(2, NSB)):
                            nth = (NSB + 1 - s) // 2
                            pe.wait_ge(cs("hs", s), nth * (g + 1))
                        for t in range(4):
                            pe.wait_ge(cs("x_added", t % 2), 2 * g + t // 2)
                            for n in range(NSB):
                                mm = pe.matmul(pso[t % 2][:, 0:D], hs[:, n, t * P:(t + 1) * P], ws2[:, n, :], start=(n == 0), stop=(n == NSB - 1))
                            mm.then_inc(cs("out", t % 2), 1)

                @block.scalar
                def _(a):
                    with a.Fori(0, NG) as g:
                        for n in range(NSB):
                            s = n % 2
                            nth = (NSB + 1 - s) // 2
                            a.wait_ge(cs("hs", s), nth * g + n // 2)
                            a.wait_ge(cs("gu", s), nth * g + n // 2 + 1)
                            a.activation(sgs[:, s, :], pgu[s][0:BW, 0, :], ACT.Silu).then_inc(cs("sgs", s), 1)

                @block.vector
                def _(v):
                    with v.Fori(0, NG) as g:
                        if NSB:
                            for n in range(NSB):
                                s = n % 2
                                nth = (NSB + 1 - s) // 2
                                if n == 0:
                                    for q in range(2):
                                        v.wait_ge(cs("out", q), 2 * g)
                                v.wait_ge(cs("sgs", s), nth * g + n // 2 + 1)
                                v.tensor_tensor(hs[:, n, :], sgs[:, s, :], pgu[s][0:BW, 1, :], ALU.mult).then_inc(cs("hs", s), 1)
                        for t in range(4):
                            u = t % 2
                            k_ = 2 * g + t // 2
                            xt = X[:, bass.ds(4 * g + t, 1), :].rearrange("p o d -> p (o d)")
                            v.wait_ge(cs("out", u), k_ + 1)
                            v.tensor_tensor(xt, xt, pso[u][:, 0:D], ALU.add).then_inc(cs("x_added", u), 1)
                            v.wait_ge(cs("x_added", u), k_ + 1)
                            v.wait_ge(cs("yg", u), 16 * K * (k_ + 1))
                            carry_waits(v, cs("passed_dve"))
                            for k in range(K):
                                ins = v.scalar_tensor_tensor(xt, yg[:, u, k, :], wts[:, bass.ds(4 * g + t, 1), k:k + 1].rearrange("p o k -> p (o k)"),
                                                             xt, ALU.mult, ALU.add)
                                if k < K - 1:
                                    ins.then_inc(cs("acc", u), 1)
                                    v.wait_ge(cs("acc", u), (K - 1) * k_ + k + 1)
                                    carry_waits(v, cs("passed_dve"))
                            ins.then_inc(cs("yg_used", u), 1)


def stage_moe0(nc, e, d):
    stage_moe(nc, e, d, 0)


def stage_moe1(nc, e, d):
    stage_moe(nc, e, d, 1)


def stage_cross(nc, e, d):
    st = Stage(nc, "x")
    sb, ps, sem = st.sb, st.ps, st.sem
    X, ident = e["X"], e["ident"]
    F2, HP, NR = 2, H // 2, 4
    ISC = float(HK) ** -0.5

    with st.ctx:
        wq, wk, wv, wo = (sb(n, [P, KD, D]) for n in ("wq", "wk", "wv", "wo"))
        bq, bk, bv = (sb(n, [P, F2]) for n in ("bq", "bk", "bv"))
        bo, one = sb("bo", [1, D]), sb("one", [1, P])
        maskr, bm = sb("maskr", [P, SK]), sb("bm", [P, 2])
        xnT, qT = sb("xnT", [P, KD, T]), sb("qT", [P, F2, T])
        c = sb("c", [P, 2, KD, SK])
        kT = sb("kT", [P, 2, F2, SK])
        val = sb("val", [P, 2, 2, D])
        qblk = sb("qblk", [P, 2, F2, 2, S])
        s = sb("s", [P, 2, HP, SK])
        mx, nm, sm, rs_ = (sb(n, [P, 2, HP]) for n in ("mx", "nm", "sm", "rs"))
        pT = sb("pT", [P, 2, HP, 2, P])
        oc, oT = sb("oc", [P, D]), sb("oT", [P, F2, P])

        LOADS = [(wq[:, :, :], d["x_wq"]), (wk[:, :, :], d["x_wk"]), (wv[:, :, :], d["x_wv"]), (wo[:, :, :], d["x_wo"]),
                 (bq[:, :], d["x_bq"]), (bk[:, :], d["x_bk"]), (bv[:, :], d["x_bv"]), (bo[:, :], d["x_bo"]),
                 (one[:, :], d["ones"][0:1, :]), (maskr[0:S, :], d["x_mask"]), (maskr[S:P, :], d["x_mask"]), (bm[:, :], d["pair_mask"])]
        W_ALL = 16 * len(LOADS)

        q = Stage(nc, "xq")
        qs = q.sem
        with q.ctx:
            ln = LayerNorm(q, e)
            pq = [q.ps(f"pq{n}", [P, GT]) for n in range(2)]
            with nc.Block() as block:
                @block.sync
                def _(sp):
                    for dst, src in LOADS:
                        sp.dma_start(dst, src).then_inc(qs("weights"), 16)
                    sp.wait_ge(qs("weights"), W_ALL)

                @block.tensor
                def _(pe):
                    pe.wait_ge(qs("weights"), W_ALL)
                    with pe.Fori(0, NT // 2) as p:
                        for u in range(2):
                            ln.tensor_tile(pe, p, u)
                    for u in range(2):
                        pe.wait_ge(qs("xnT_ready", u), NT // 2)
                    with pe.Fori(0, NG) as g:
                        for f in range(F2):
                            pe.wait_ge(qs("q_out", f), g)
                            for k in range(KD):
                                mm = pe.matmul(pq[f][:, :], wq[:, k, f * P:(f + 1) * P], xnT[:, k, bass.ds(GT * g, GT)], start=(k == 0), stop=(k == KD - 1))
                            mm.then_inc(qs("q_done", f), 1)

                @block.scalar
                def _(a):
                    ln.scalar_std(a)
                    with a.Fori(0, NT // 2) as p:
                        for u in range(2):
                            ln.scalar_tile(a, p, u, xnT[:, :, bass.ds(P * (2 * p + u), P)])
                    a.wait_ge(qs("weights"), W_ALL)
                    with a.Fori(0, NG) as g:
                        for f in range(F2):
                            a.wait_ge(qs("q_done", f), g + 1)
                            carry_waits(a, qs("passed_act"))
                            a.activation(qT[:, f, bass.ds(GT * g, GT)], pq[f][:, :], ACT.Identity, bias=bq[:, f:f + 1]).then_inc(qs("q_out", f), 1)

                @block.vector
                def _(v):
                    ln.vector_stats(v)
                    with v.Fori(0, NT // 2) as p:
                        for u in range(2):
                            ln.vector_tile(v, p, u)

        psS = ps("psS", [P, NR, F2, SK])
        psP = [ps(f"psP{n}", [P, 512]) for n in range(2)]
        psK = ps("psK", [P, 2, D])
        psO = ps("psO", [P, 512])

        def schedule(eng, start, step, finish):
            start()
            step(0, 0, False, True)
            step(0, 1, False, True)
            with eng.Fori(1, NT - 1) as p:
                step(p, 0, True, True)
                step(p, 1, False, True)
            step(NT - 1, 0, True, False)
            step(NT - 1, 1, False, False)
            finish(NT - 1)

        with nc.Block() as block:
            @block.sync
            def _(sp):
                ctx_v = d["ctxT"].rearrange("(g b) p k n -> g b p k n", b=2)
                with sp.Fori(0, NT) as p:
                    for u in range(2):
                        sp.wait_ge(sem("v_done", u), p)
                        sp.dma_start(c[:, u], ctx_v[bass.ds(p, 1), u].rearrange("o p k n -> (o p) k n")
                                     ).then_inc(sem("ctx", u), 16)

            @block.gpsimd
            def _(g):
                with g.Fori(0, NT) as p:
                    for u in range(2):
                        g.wait_ge(sem("s_done", u), p)
                        carry_waits(g, sem("passed_pool"))
                        for f in range(F2):
                            ins = g.tensor_tensor(qblk[:, u, f], bc(qT[:, f, bass.ds(P * p + S * u, S)].rearrange("p (o n) -> p o n", o=1), [P, 2, S]),
                                                  bc(bm[:, :, None], [P, 2, S]), ALU.mult)
                        ins.then_inc(sem("qblk", u), 1)

            @block.tensor
            def _(pe):
                def keys(p, u):
                    pe.wait_ge(sem("ctx", u), 16 * (p + 1))
                    pe.wait_ge(sem("v_out"), 2 * p + u)
                    for f in range(F2):
                        for k in range(KD):
                            mm = pe.matmul(psK[:, f, :], wk[:, k, f * P:(f + 1) * P], c[:, u, k, :], start=(k == 0), stop=(k == KD - 1))
                    mm.then_inc(sem("k_done"), 1)

                def values(p, u):
                    pe.wait_ge(sem("k_out"), 2 * p + u + 1)
                    for t in range(2):
                        for k in range(KD):
                            mm = pe.matmul(psK[:, t, :], c[:, u, k, t * P:(t + 1) * P], wv[:, k, :], start=(k == 0), stop=(k == KD - 1))
                    mm.then_inc(sem("v_done", u), 1)

                def scores(p, u):
                    b = 2 * p + u
                    pe.wait_ge(sem("k_out"), b + 1)
                    pe.wait_ge(sem("qblk", u), p + 1)
                    pe.wait_ge(sem("masked"), b)
                    for f in range(F2):
                        for r in range(NR):
                            mm = pe.matmul(psS[:, r, f, :], qblk[32 * r:32 * r + 32, u, f].rearrange("p a n -> p (a n)"),
                                           kT[32 * r:32 * r + 32, u, f, :], start=True, stop=True)
                    mm.then_inc(sem("s_done", u), 1)

                def turn(p, u, h):
                    b = 2 * p + u
                    for n in range(2):
                        pe.wait_ge(sem("pT", n), 2 * b + h)
                        for i in range(4):
                            hp, t = 4 * h + 2 * n + i // 2, i % 2
                            mm = pe.transpose(psP[n][:, i * P:(i + 1) * P], s[:, u, hp, t * P:(t + 1) * P], ident[:, :])
                        mm.then_inc(sem("p_turned", n), 1)

                def turn_oc(p):
                    pe.wait_ge(sem("oc"), 2 * p + 2)
                    for f in range(F2):
                        mm = pe.transpose(psO[:, f * P:(f + 1) * P], oc[:, f * P:(f + 1) * P], ident[:, :])
                    mm.then_inc(sem("oc_turned"), 1)

                def project(p):
                    pe.wait_ge(sem("oT"), p + 1)
                    pe.matmul(psO[:, 0:D], one[:, :], bo[:, :], start=True, stop=False)
                    for f in range(F2):
                        mm = pe.matmul(psO[:, 0:D], oT[:, f, :], wo[:, f, :], start=False, stop=(f == F2 - 1))
                    mm.then_inc(sem("y_done"), 1)

                def start():
                    for u in range(2):
                        keys(0, u)
                        scores(0, u)
                        values(0, u)

                def step(p, u, joined, ahead):
                    b = 2 * p + u
                    pe.wait_ge(sem("exp", u), p + 1)
                    turn(p, u, 0)
                    if joined:
                        turn_oc(p - 1)
                    if ahead:
                        keys(p + 1, u)
                    turn(p, u, 1)
                    if joined:
                        project(p - 1)
                    if ahead:
                        scores(p + 1, u)
                    for n in range(2):
                        pe.wait_ge(sem("pT", n), 2 * b + 2)
                    pe.wait_ge(sem("v_out"), b + 1)
                    pe.wait_ge(sem("oc"), b)
                    if joined:
                        pe.wait_ge(sem("x_added"), p)
                    for hp in range(HP):
                        r, f = hp // 2, hp % 2
                        for t in range(2):
                            mm = pe.matmul(psO[:, hp * 32:hp * 32 + 32], pT[:, u, hp, t, :], val[:, u, t, f * P + 32 * r:f * P + 32 * r + 32],
                                           start=(t == 0), stop=(t == 1))
                    mm.then_inc(sem("o_done", u), 1)
                    if ahead:
                        values(p + 1, u)

                def finish(p):
                    turn_oc(p)
                    project(p)

                schedule(pe, start, step, finish)

            @block.scalar
            def _(a):
                def keys(p, u):
                    a.wait_ge(sem("s_done", u), p)
                    a.wait_ge(sem("k_done"), 2 * p + u + 1)
                    for f in range(F2):
                        ins = a.activation(kT[:, u, f, :], psK[:, f, :], ACT.Identity, bias=bk[:, f:f + 1])
                    ins.then_inc(sem("k_out"), 1)

                def values(p, u):
                    a.wait_ge(sem("o_done", u), p)
                    a.wait_ge(sem("v_done", u), p + 1)
                    a.activation(val[:, u], psK[:, :, :], ACT.Copy).then_inc(sem("v_out"), 1)

                def exps(p, u):
                    a.wait_ge(sem("nm", u), p + 1)
                    a.wait_ge(sem("rsum", u), p)
                    for hp in range(HP):
                        ins = a.activation(s[:, u, hp, :], s[:, u, hp, :], ACT.Exp, bias=nm[:, u, hp:hp + 1], scale=ISC,
                                           accum_out=sm[:, u, hp:hp + 1])
                    ins.then_inc(sem("exp", u), 1)

                def turned(p, u, h):
                    a.wait_ge(sem("p_turned", 1), 2 * (2 * p + u) + h + 1)
                    a.activation(pT[:, u, 4 * h + 2:4 * h + 4].rearrange("p h t n -> p (h t n)"), psP[1][:, :], ACT.Copy).then_inc(sem("pT", 1), 1)

                def finish(p):
                    a.wait_ge(sem("y_done"), p)
                    a.wait_ge(sem("oc_turned"), p + 1)
                    for f in range(F2):
                        ins = a.activation(oT[:, f, :], psO[:, f * P:(f + 1) * P], ACT.Identity, bias=bv[:, f:f + 1])
                    ins.then_inc(sem("oT"), 1)

                def start():
                    for u in range(2):
                        keys(0, u)
                        values(0, u)
                    exps(0, 0)

                def step(p, u, joined, ahead):
                    turned(p, u, 0)
                    if joined:
                        finish(p - 1)
                    if ahead:
                        keys(p + 1, u)
                    turned(p, u, 1)
                    if u == 0:
                        exps(p, 1)
                    elif ahead:
                        exps(p + 1, 0)
                    if ahead:
                        values(p + 1, u)

                schedule(a, start, step, finish)

            @block.vector
            def _(v):
                def scores(p, u, ahead):
                    b = 2 * p + u
                    v.wait_ge(sem("s_done", u), p + 1)
                    if ahead:
                        v.wait_ge(sem("p_turned", 1), 2 * b - 2)
                    carry_waits(v, sem("passed_dve"))
                    for hp in range(HP):
                        r, f = hp // 2, hp % 2
                        ins = v.tensor_tensor_reduce(s[:, u, hp, :], psS[:, r, f, :], maskr[:, :], 1.0, -3.0e38, ALU.add, ALU.max,
                                                     mx[:, u, hp:hp + 1])
                    ins.then_inc(sem("masked"), 1)
                    v.wait_ge(sem("masked"), b + 1)
                    v.tensor_scalar(nm[:, u, :], mx[:, u, :], -ISC, None, ALU.mult).then_inc(sem("nm", u), 1)

                def turned(p, u, h):
                    v.wait_ge(sem("p_turned", 0), 2 * (2 * p + u) + h + 1)
                    v.tensor_copy(pT[:, u, 4 * h:4 * h + 2].rearrange("p h t n -> p (h t n)"), psP[0][:, :]).then_inc(sem("pT", 0), 1)

                def start():
                    scores(0, 0, False)
                    scores(0, 1, False)

                def step(p, u, joined, ahead):
                    turned(p, u, 0)
                    turned(p, u, 1)
                    if joined:
                        finish(p - 1)
                    if ahead:
                        scores(p + 1, u, True)
                    v.wait_ge(sem("exp", u), p + 1)
                    v.reciprocal(rs_[:, u, :], sm[:, u, :]).then_inc(sem("rsum", u), 1)
                    v.wait_ge(sem("rsum", u), p + 1)
                    v.wait_ge(sem("oc_turned"), p)
                    v.wait_ge(sem("o_done", u), p + 1)
                    for h2 in range(2):
                        lo = S * h2
                        src = psO[lo:lo + S, 0:HP * 32].rearrange("p (r f c) -> p r f c", r=NR, f=F2)[:, :, :, HK * h2:HK * h2 + HK]
                        w = bc(rs_[lo:lo + S, u, :].rearrange("p (r f) -> p r f", f=F2)[:, :, :, None], [S, NR, F2, HK])
                        out = oc[S * u:S * u + S, :].rearrange("p (f r c) -> p r f c", f=F2, r=NR)[:, :, :, HK * h2:HK * h2 + HK]
                        ins = v.tensor_tensor(out, src, w, ALU.mult)
                    ins.then_inc(sem("oc"), 1)

                def finish(p):
                    v.wait_ge(sem("y_done"), p + 1)
                    carry_waits(v, sem("passed_dve"))
                    xt = X[:, bass.ds(p, 1), :].rearrange("p o d -> p (o d)")
                    v.tensor_tensor(xt, xt, psO[:, 0:D], ALU.add).then_inc(sem("x_added"), 1)

                schedule(v, start, step, finish)


def stage_self(nc, e, d):
    st = Stage(nc, "s")
    sb, ps, sem = st.sb, st.ps, st.sem
    X, ident = e["X"], e["ident"]
    F2, HP, NR = 2, H // 2, 4
    ISC = float(HK) ** -0.5

    with st.ctx:
        wq, wqs, wk, wks, wv, wo = (sb(n, [P, KD, D]) for n in ("wq", "wqs", "wk", "wks", "wv", "wo"))
        cos, sin = sb("cos", [P, S]), sb("sin", [P, S])
        causal, bm = sb("causal", [P, S]), sb("bm", [P, 2])
        xnT = sb("xnT", [P, KD, T])
        qT, kT = sb("qT", [P, F2, T]), sb("kT", [P, F2, T])
        vall = sb("vall", [P, NT, D])

        q = Stage(nc, "sq")
        qs = q.sem
        with q.ctx:
            ln = LayerNorm(q, e)
            xts = q.sb("xts", [P, 2, KD, P])
            ra = q.sb("ra", [P, 2, 2, GT])
            psv = q.ps("psv", [P, 512])
            pr = [[q.ps(f"pr{n}{m}", [P, GT]) for m in range(2)] for n in range(2)]

            LOADS = [(wq[:, :, :], d["s_wq"]), (wqs[:, :, :], d["s_wqs"]), (wk[:, :, :], d["s_wk"]), (wks[:, :, :], d["s_wks"]),
                     (wv[:, :, :], d["s_wv"]), (wo[:, :, :], d["s_wo"]), (cos[:, :], d["s_cos"]), (sin[:, :], d["s_sin"]),
                     (causal[:, :], d["s_causal"]), (bm[:, :], d["pair_mask"])]
            W_ALL = 16 * len(LOADS)
            UNITS = [(w, ws, out, f) for w, ws, out in ((wq, wqs, qT), (wk, wks, kT)) for f in range(F2)]

            with nc.Block() as block:
                @block.sync
                def _(sp):
                    for dst, src in LOADS:
                        sp.dma_start(dst, src).then_inc(qs("weights"), 16)
                    sp.wait_ge(qs("weights"), W_ALL)

                @block.tensor
                def _(pe):
                    pe.wait_ge(qs("weights"), W_ALL)
                    with pe.Fori(0, NT // 2) as p:
                        for u in range(2):
                            ln.tensor_tile(pe, p, u)
                            pe.wait_ge(qs("xts", u), p + 1)
                            pe.wait_ge(qs("v_out", 1 - u), p + u)
                            for k in range(KD):
                                mm = pe.matmul(psv[:, 0:D], xts[:, u, k, :], wv[:, k, :], start=(k == 0), stop=(k == KD - 1))
                            mm.then_inc(qs("v_done", u), 1)
                    with pe.Fori(0, NG) as g:
                        for i, (w, ws, _, f) in enumerate(UNITS):
                            n = i % 2
                            pe.wait_ge(qs("turned", n), 4 * g + 2 * (i // 2))
                            for m, ww in enumerate((w, ws)):
                                for k in range(KD):
                                    mm = pe.matmul(pr[n][m][:, :], ww[:, k, f * P:(f + 1) * P], xnT[:, k, bass.ds(GT * g, GT)], start=(k == 0), stop=(k == KD - 1))
                            mm.then_inc(qs("qk", n), 1)

                @block.scalar
                def _(a):
                    ln.scalar_std(a)
                    with a.Fori(0, NT // 2) as p:
                        for u in range(2):
                            t = 2 * p + u
                            a.wait_ge(qs("v_done", u), p)
                            ln.scalar_tile(a, p, u, xnT[:, :, bass.ds(P * t, P)])
                            a.activation(xts[:, u], ln.psT[:, 0:D].rearrange("p (k n) -> p k n", k=KD), ACT.Copy).then_inc(qs("xts", u), 1)
                            a.wait_ge(qs("v_done", u), p + 1)
                            carry_waits(a, qs("passed_act"))
                            a.activation(vall[:, bass.ds(t, 1), :].rearrange("p o d -> p (o d)"), psv[:, 0:D], ACT.Copy).then_inc(qs("v_out", u), 1)

                @block.vector
                def _(v):
                    ln.vector_stats(v)
                    with v.Fori(0, NT // 2) as p:
                        for u in range(2):
                            ln.vector_tile(v, p, u)
                    v.wait_ge(qs("weights"), W_ALL)
                    with v.Fori(0, NG) as g:
                        for i, (_, _, out, f) in enumerate(UNITS):
                            n = i % 2
                            v.wait_ge(qs("qk", n), 2 * g + i // 2 + 1)
                            shape = [P, GT // S, S]
                            for m, tab in enumerate((cos, sin)):
                                v.tensor_tensor(ra[:, n, m, :].rearrange("p (b s) -> p b s", s=S), pr[n][m][:, :].rearrange("p (b s) -> p b s", s=S),
                                                bc(tab[:, None, :], shape), ALU.mult).then_inc(qs("turned", n), 1)
                            v.wait_ge(qs("turned", n), 4 * g + 2 * (i // 2) + 2)
                            carry_waits(v, qs("passed_dve"))
                            v.tensor_tensor(out[:, f, bass.ds(GT * g, GT)], ra[:, n, 0, :], ra[:, n, 1, :], ALU.add).then_inc(qs("rotated", n), 1)

        kb, vb = sb("kb", [P, 2, F2, P]), sb("vb", [P, 2, D])
        qblk = sb("qblk", [P, 2, F2, 2, 2, S])
        s = sb("s", [P, 2, NR, F2, 2, S])
        mx = sb("mx", [P, 2, 4, 4 * NR])
        pT = sb("pT", [P, 2, HP, P])
        oc, oT = sb("oc", [P, D]), sb("oT", [P, F2, P])
        psS = ps("psS", [P, NR, 512])
        psP = ps("psP", [P, 2, 512])
        psO = ps("psO", [P, 2, 512])
        NP2 = NT // 2

        def schedule(eng, start, step, finish):
            start()
            step(0, 0, False, True)
            step(0, 1, True, True)
            with eng.Fori(1, NP2 - 1) as p:
                step(p, 0, True, True)
                step(p, 1, True, True)
            step(NP2 - 1, 0, True, False)
            step(NP2 - 1, 1, True, False)
            finish(NP2 - 1, 1)

        def before(p, u):
            return (p, 0) if u == 1 else (p - 1, 1)

        with nc.Block() as block:
            @block.gpsimd
            def _(g):
                def queries(p, u):
                    t = 2 * p + u
                    g.wait_ge(sem("s_done", u), p)
                    carry_waits(g, sem("passed_pool"))
                    for f in range(F2):
                        for b in range(2):
                            g.tensor_tensor(qblk[:, u, f, b], bc(qT[:, f, bass.ds(P * t + S * b, S)].rearrange("p (o n) -> p o n", o=1), [P, 2, S]),
                                            bc(bm[:, :, None], [P, 2, S]), ALU.mult)
                    g.tensor_copy(kb[:, u], kT[:, :, bass.ds(P * t, P)]).then_inc(sem("ready", u), 1)

                def start():
                    queries(0, 0)
                    queries(0, 1)

                def step(p, u, joined, ahead):
                    g.wait_ge(sem("o_done", u), p)
                    carry_waits(g, sem("passed_pool"))
                    g.tensor_copy(vb[:, u, :], vall[:, bass.ds(2 * p + u, 1), :].rearrange("p o d -> p (o d)")).then_inc(sem("v_ready", u), 1)
                    if ahead:
                        queries(p + 1, u)

                def finish(p, u):
                    pass

                schedule(g, start, step, finish)

            @block.tensor
            def _(pe):
                def scores(p, u):
                    pe.wait_ge(sem("ready", u), p + 1)
                    pe.wait_ge(sem("masked", 1 - u), p + u)
                    for f in range(F2):
                        for b in range(2):
                            for r in range(NR):
                                o = (2 * f + b) * S
                                mm = pe.matmul(psS[:, r, o:o + S], qblk[32 * r:32 * r + 32, u, f, b].rearrange("p a n -> p (a n)"),
                                               kb[32 * r:32 * r + 32, u, f, S * b:S * b + S], start=True, stop=True)
                    mm.then_inc(sem("s_done", u), 1)

                def turn_oc(p, u, last=False):
                    pe.wait_ge(sem("oc"), 2 * p + u + 1)
                    if not last:
                        pe.wait_ge(sem("pT", 0), 2 * p + u + 2)
                    for f in range(F2):
                        mm = pe.transpose(psP[:, 0, f * P:(f + 1) * P], oc[:, f * P:(f + 1) * P], ident[:, :])
                    mm.then_inc(sem("oc_turned"), 1)

                def project(p, u, last=False):
                    pe.wait_ge(sem("oT"), 2 * p + u + 1)
                    if not last:
                        pe.wait_ge(sem("pT", 1), 2 * p + u + 2)
                    for f in range(F2):
                        mm = pe.matmul(psP[:, 1, 0:D], oT[:, f, :], wo[:, f, :], start=(f == 0), stop=(f == F2 - 1))
                    mm.then_inc(sem("y_done"), 1)

                def start():
                    scores(0, 0)
                    scores(0, 1)

                def step(p, u, joined, ahead):
                    t = 2 * p + u
                    pe.wait_ge(sem("exp", u), p + 1)
                    if joined:
                        pe.wait_ge(sem("oT"), t - 1)
                        pe.wait_ge(sem("x_added"), t - 1)
                    for h in range(2):
                        pe.wait_ge(sem("pT", h), t)
                        for i in range(4):
                            hp = 4 * h + i
                            mm = pe.transpose(psP[:, h, i * P:(i + 1) * P], s[:, u, hp // 2, hp % 2].rearrange("p b k -> p (b k)"), ident[:, :])
                        mm.then_inc(sem("p_turned", h), 1)
                    if joined:
                        turn_oc(*before(p, u))
                    if ahead:
                        scores(p + 1, u)
                    if joined:
                        project(*before(p, u))
                    for h in range(2):
                        pe.wait_ge(sem("pT", h), t + 1)
                    pe.wait_ge(sem("v_ready", u), p + 1)
                    pe.wait_ge(sem("oc"), t)
                    for hp in range(HP):
                        r, f = hp // 2, hp % 2
                        for b in range(2):
                            mm = pe.matmul(psO[:, b, hp * 32:hp * 32 + 32], pT[S * b:S * b + S, u, hp, :],
                                           vb[S * b:S * b + S, u, f * P + 32 * r:f * P + 32 * r + 32], start=True, stop=True)
                    mm.then_inc(sem("o_done", u), 1)

                def finish(p, u):
                    turn_oc(p, u, True)
                    project(p, u, True)

                schedule(pe, start, step, finish)

            @block.scalar
            def _(a):
                def exps(p, u):
                    a.wait_ge(sem("shifted", u), p + 1)
                    a.activation(s[:, u], s[:, u], ACT.Exp, scale=ISC).then_inc(sem("exp", u), 1)

                def start():
                    exps(0, 0)

                def step(p, u, joined, ahead):
                    a.wait_ge(sem("p_turned", 0), 2 * p + u + 1)
                    a.activation(pT[:, u, 0:4].rearrange("p h n -> p (h n)"), psP[:, 0, :], ACT.Copy).then_inc(sem("pT", 0), 1)
                    if joined:
                        finish(*before(p, u))
                    if u == 0:
                        exps(p, 1)
                    elif ahead:
                        exps(p + 1, 0)

                def finish(p, u):
                    t = 2 * p + u
                    a.wait_ge(sem("y_done"), t)
                    a.wait_ge(sem("oc_turned"), t + 1)
                    a.activation(oT[:, :, :].rearrange("p f n -> p (f n)"), psP[:, 0, 0:D], ACT.Copy).then_inc(sem("oT"), 1)

                schedule(a, start, step, finish)

            @block.vector
            def _(v):
                def shifted(p, u, ahead):
                    v.wait_ge(sem("s_done", u), p + 1)
                    if ahead:
                        v.wait_ge(sem("p_turned", 1), 2 * p + u - 1)
                    carry_waits(v, sem("passed_dve"))
                    sv = s[:, u].rearrange("p r f b k -> p r (f b) k")
                    flat = s[:, u].rearrange("p r f b k -> p (r f b) k")
                    v.tensor_tensor(sv, psS[:, :, 0:4 * S].rearrange("p r (o k) -> p r o k", k=S), bc(causal[:, None, None, :], [P, NR, 4, S]),
                                    ALU.add).then_inc(sem("masked", u), 1)
                    v.wait_ge(sem("masked", u), p + 1)
                    v.tensor_reduce(mx[:, u, 0, :], flat, AX_X, ALU.max).then_inc(sem("max", u), 1)
                    v.wait_ge(sem("max", u), p + 1)
                    v.tensor_tensor(flat, flat, bc(mx[:, u, 0, :, None], [P, 4 * NR, S]), ALU.subtract).then_inc(sem("shifted", u), 1)

                def start():
                    shifted(0, 0, False)
                    shifted(0, 1, False)

                def step(p, u, joined, ahead):
                    t = 2 * p + u
                    v.wait_ge(sem("exp", u), p + 1)
                    v.tensor_reduce(mx[:, u, 1, :], s[:, u].rearrange("p r f b k -> p (r f b) k"), AX_X, ALU.add).then_inc(sem("sum", u), 1)
                    v.wait_ge(sem("p_turned", 1), t + 1)
                    v.tensor_copy(pT[:, u, 4:8].rearrange("p h n -> p (h n)"), psP[:, 1, :]).then_inc(sem("pT", 1), 1)
                    v.wait_ge(sem("sum", u), p + 1)
                    v.reciprocal(mx[:, u, 2, :], mx[:, u, 1, :]).then_inc(sem("rsum", u), 1)
                    v.wait_ge(sem("rsum", u), p + 1)
                    if joined:
                        finish(*before(p, u))
                    if ahead:
                        shifted(p + 1, u, True)
                    v.wait_ge(sem("oc_turned"), t)
                    v.wait_ge(sem("o_done", u), p + 1)
                    for b in range(2):
                        for h2 in range(2):
                            lo = S * h2
                            src = psO[lo:lo + S, b, 0:HP * 32].rearrange("p (r f c) -> p r f c", r=NR, f=F2)[:, :, :, HK * h2:HK * h2 + HK]
                            w = bc(mx[lo:lo + S, u, 2, :].rearrange("p (r f b) -> p r f b", f=F2, b=2)[:, :, :, b:b + 1], [S, NR, F2, HK])
                            out = oc[S * b:S * b + S, :].rearrange("p (f r c) -> p r f c", f=F2, r=NR)[:, :, :, HK * h2:HK * h2 + HK]
                            ins = v.tensor_tensor(out, src, w, ALU.mult)
                    ins.then_inc(sem("oc"), 1)

                def finish(p, u):
                    t = 2 * p + u
                    v.wait_ge(sem("y_done"), t + 1)
                    carry_waits(v, sem("passed_dve"))
                    xt = X[:, bass.ds(t, 1), :].rearrange("p o d -> p (o d)")
                    v.tensor_tensor(xt, xt, psP[:, 1, 0:D], ALU.add).then_inc(sem("x_added"), 1)

                schedule(v, start, step, finish)


def build(nc, d, out, stages):
    ctx = ExitStack()
    with ctx:
        X = ctx.enter_context(nc.sbuf_tensor("X", [P, NT, D], F32))
        ident = ctx.enter_context(nc.sbuf_tensor("ident", [P, P], F32))
        loaded = ctx.enter_context(nc.semaphore("x_loaded"))
        stored = ctx.enter_context(nc.semaphore("x_stored"))
        e = {"X": X, "ident": ident}
        with nc.Block() as block:
            @block.sync
            def _(sp):
                sp.dma_start(X[:, :, :], d["x"].rearrange("(t p) d -> p t d", p=P)).then_inc(loaded, 16)
                sp.dma_start(ident[:, :], d["ident"]).then_inc(loaded, 16)
                sp.wait_ge(loaded, 32)
        for s in stages:
            with nc.cleanup_on_exit():
                s(nc, e, d)
        with nc.Block() as block:
            @block.sync
            def _(sp):
                sp.dma_start(out.rearrange("(t p) d -> p t d", p=P), X[:, :, :]).then_inc(stored, 16)
                sp.wait_ge(stored, 16)


def rope_tables(pos, dim, base=10000.0):
    half = dim // 2
    inv = (np.float32(1.0) / np.power(np.float32(base), np.arange(half, dtype=np.float32) / np.float32(half))).astype(np.float32)
    ang = pos.astype(np.float32)[:, None] * inv
    c, s = np.cos(ang).astype(np.float32), np.sin(ang).astype(np.float32)
    return np.concatenate([c, c], 1), np.concatenate([-s, s], 1)


def layout(i):
    f = {}
    c = np.ascontiguousarray
    f["x"] = c(i["x"].reshape(T, D))
    f["ident"] = np.eye(P, dtype=np.float32)
    ctx = i["ctx_1024"]
    f["ctxT"] = c(ctx.reshape(B, SK, KD, P).transpose(0, 3, 2, 1))
    f["seg"] = c(i["itok_BxS_0_511"].reshape(NT, P).T)
    w = i["L0_xattn_w_kv_comp"]
    f["kcompT"] = c(w.T)
    f["kcomp"] = c(w.reshape(KD, P, KVC).transpose(1, 0, 2))
    f["krope"] = c(i["L0_xattn_w_k_rope"])
    f["qup"] = c(i["L0_xattn_w_q_up"].reshape(QC, H, HD).transpose(2, 1, 0))
    f["kup"] = c(i["L0_xattn_w_k_up"].reshape(KVC, H, HD).transpose(2, 1, 0))
    f["vup"] = c(i["L0_xattn_w_v_up"].reshape(KVC, H, HD).transpose(2, 1, 0))
    f["wout"] = c(i["L0_xattn_w_out"].reshape(H, HD, D).transpose(1, 0, 2))
    f["wqd"] = c(i["L0_xattn_w_q_down"].reshape(KD, P, QC).transpose(1, 0, 2))
    f["qrope"] = c(i["L0_xattn_w_q_rope"].reshape(QC, H, RD))
    ck, sk = rope_tables(np.arange(SK), RD)
    f["cosk"] = c(np.tile(ck.reshape(2, P, RD), (2, 1, 1)).transpose(1, 0, 2))
    f["sink"] = c(np.tile(sk.reshape(2, P, RD), (2, 1, 1)).transpose(1, 0, 2))
    cq, sq = rope_tables(np.arange(P) % S, RD)
    f["cosq"], f["sinq"] = cq, -sq
    b = np.arange(T).reshape(NT, P).T // S
    f["rows"] = c(np.stack([b * SK, KROWS + b], 1).astype(np.float32))
    f["meanw"] = np.full((P, 1), 1.0 / SK, np.float32)
    f["b_win"] = c(i["L0_attn_W_in"].T.reshape(KD, P, 2 * DI).transpose(1, 0, 2))
    f["b_convw"] = c(i["L0_attn_conv_w"].reshape(NCH, P, KC).transpose(1, 0, 2))
    f["b_convb"] = c(i["L0_attn_conv_b"].reshape(NCH, P).T)
    f["b_wx"] = c(i["L0_attn_W_x"].T.reshape(NCH, P, DTR + 2 * NST).transpose(1, 0, 2))
    f["b_wdt"] = c(i["L0_attn_W_dt"].T)
    f["b_bdt"] = c(i["L0_attn_b_dt"].reshape(NCH, P).T)
    f["b_alog"] = c(i["L0_attn_A_log"].reshape(NCH, P, NST).transpose(1, 0, 2))
    f["b_dp"] = c(i["L0_attn_Dp"].reshape(NCH, P).T)
    f["b_wout"] = c(i["L0_attn_W_out"].T.reshape(NCH, P, D).transpose(1, 0, 2))
    f["iota_e"] = np.arange(E, dtype=np.float32)
    f["slot_base"] = np.arange(E, dtype=np.float32) * CAP0
    f["iota_b"] = c(np.arange(2 * P, dtype=np.float32).reshape(2, P).T)
    f["tokid"] = c(np.arange(T, dtype=np.int32).reshape(NT, P).T)
    f["ltri"] = np.triu(np.ones((P, P), np.float32), 1)
    f["ones"] = np.ones((P, P), np.float32)

    def by_row(w):
        return w.reshape(KD, P, -1).transpose(1, 0, 2)

    f["m0_gw"], f["m0_gb"] = c(by_row(i["L0_ffn_gate_w"].T)), c(i["L0_ffn_gate_b"])
    w1, w3 = (i[f"L0_ffn_{n}"].reshape(E, 2, IH, KD, P) for n in ("w1", "w3"))
    f["m0_w13"] = c(np.stack([w1, w3], 1).transpose(0, 5, 4, 1, 2, 3).reshape(E, P, -1))
    f["m0_w2"] = c(i["L0_ffn_w2"].reshape(E, D, 2, IH).transpose(0, 3, 2, 1).reshape(E, IH, -1))
    w1, w3 = (i[f"L0_ffn_{n}"].reshape(SB0, IH, KD, P) for n in ("ws1", "ws3"))
    f["m0_ws13"] = c(np.stack([w1, w3], 0).transpose(4, 3, 0, 1, 2))
    f["m0_ws2"] = c(i["L0_ffn_ws2"].reshape(D, SB0, IH).transpose(2, 1, 0))
    f["m1_gw"], f["m1_gb"] = c(by_row(i["L1_ffn_w_router"])), c(i["L1_ffn_b_router"])
    w1, w3 = (i[f"L1_ffn_{n}"].reshape(E, KD, P, F1) for n in ("we_gate", "we_up"))
    f["m1_w13"] = c(np.stack([w1, w3], 1).transpose(0, 3, 2, 1, 4).reshape(E, P, -1))
    f["m1_w2"] = c(i["L1_ffn_we_down"])
    w1, w3 = (i[f"L1_ffn_{n}"].reshape(KD, P, F1) for n in ("ws_gate", "ws_up"))
    f["m1_ws13"] = c(np.stack([w1, w3], 0).transpose(2, 1, 0, 3).reshape(P, KD, 2, 1, F1))
    f["m1_ws2"] = c(i["L1_ffn_ws_down"].reshape(F1, 1, D))
    for n in "qkv":
        f[f"x_w{n}"] = c(by_row(i[f"L1_xattn_W{n}"].transpose(1, 0, 2).reshape(D, D)))
        f[f"x_b{n}"] = c(i[f"L1_xattn_b{n}"].reshape(2, P).T)
    f["x_wo"] = c(by_row(i["L1_xattn_Wo"].T))
    f["x_bo"] = c(i["L1_xattn_bo"].reshape(1, D))
    f["x_mask"] = c(i["fside_SxS2_0"])
    f["pair_mask"] = (np.arange(P)[:, None] // HK % 2 == np.arange(2)).astype(np.float32)
    swap = np.arange(D).reshape(H, 2, HK // 2)[:, ::-1].reshape(D)
    for n in "qk":
        w = i[f"L1_attn_W{n}"]
        f[f"s_w{n}"], f[f"s_w{n}s"] = c(by_row(w.T)), c(by_row(w[swap].T))
    f["s_wv"], f["s_wo"] = c(by_row(i["L1_attn_Wv"].T)), c(by_row(i["L1_attn_Wo"].T))
    cs, sn = rope_tables(np.arange(S), HK)
    f["s_cos"], f["s_sin"] = c(np.tile(cs.T, (P // HK, 1))), c(np.tile(sn.T, (P // HK, 1)))
    f["s_causal"] = np.where(np.arange(S)[None, :] > np.arange(P)[:, None] % S, NEG, 0.0).astype(np.float32)
    return f


STAGES = [stage_mla, stage_mamba, stage_moe0, stage_cross, stage_self, stage_moe1]
SCRATCH = {"key_table": ([KROWS + B, KVC + RD], F32), "bc_rows": ([NG, 2 * NST, GT], F32),
           "slot_tok0": ([SLOTS0, 1], I32), "slot_tok1": ([SLOTS1, 1], I32), "xn0": ([T, D], F32), "xn1": ([T, D], F32),
           "y0": ([SLOTS0, D], F32), "y1": ([SLOTS1, D], F32)}


def kernel(**inputs):
    import concourse.bacc as bacc
    from concourse.bass_utils import run_bass_kernel_spmd

    nc = bacc.Bacc("TRN2", target_bir_lowering=False, num_devices=1)
    arrays = layout({k: np.asarray(v) for k, v in inputs.items()})
    d = {n: nc.dram_tensor(f"in_{n}", a.shape, mybir.dt.from_np(a.dtype), kind="ExternalInput").ap()
         for n, a in arrays.items()}
    for n, (shape, dt) in SCRATCH.items():
        d[n] = nc.dram_tensor(f"scratch_{n}", shape, dt).ap()
    out = nc.dram_tensor("out_x", [T, D], F32, kind="ExternalOutput").ap()
    build(nc, d, out, STAGES)
    r = run_bass_kernel_spmd(nc, [{f"in_{n}": a for n, a in arrays.items()}], core_ids=[0])
    return r.results[0]["out_x"].reshape(B, S, D)
```

```python
from contextlib import ExitStack

import numpy as np

import concourse.bass as bass
from concourse import mybir

F32 = mybir.dt.float32
I32 = mybir.dt.int32
U32 = mybir.dt.uint32
BF16 = mybir.dt.bfloat16
ALU = mybir.AluOpType
ACT = mybir.ActivationFunctionType
AX_X = mybir.AxisListType.X

P = 128
B, S, D = 32, 64, 256
SK = 256
T = B * S
NT = T // P
KD = D // P
H = 16
LN_EPS = 1e-5
NEG = -1.0e30

HD, KVC, QC, RD = 64, 64, 96, 64
LOOK = 3
KROWS = B * SK

DI, NST, DTR, KC = 512, 16, 64, 4
NCH = DI // P
GT = 512
NG = T // GT

E = 64
CAP0, K0, I0, SI0 = 128, 6, 176, 352
K1, F1, NGR, TOPG, RSCALE = 8, 128, 8, 4, 2.5
IH = I0 // 2
SB0 = SI0 // IH
SLOTS0 = E * CAP0
NB1 = T * K1 // P + E
SLOTS1 = NB1 * P
DROPPED = 1.0e6

HK = 16


class Stage:

    def __init__(self, nc, name):
        self.nc, self.name, self.ctx, self.sems = nc, name, ExitStack(), {}

    def sb(self, name, shape, dt=F32):
        return self.ctx.enter_context(self.nc.sbuf_tensor(f"{self.name}_{name}", shape, dt))

    def ps(self, name, shape):
        return self.ctx.enter_context(self.nc.psum_tensor(f"{self.name}_{name}", shape, F32))

    def sem(self, name, u=0):
        if (name, u) not in self.sems:
            self.sems[name, u] = self.nc.alloc_semaphore(f"{self.name}_{name}{u}")
        return self.sems[name, u]


def bc(ap, shape):
    return ap.broadcast_to(shape)


class LayerNorm:

    def __init__(self, st, e, other=None):
        self.st, self.e = st, e
        self.stats = st.sb("stats", [P, NT, 6])
        self.mean = st.sb("mean", [P, NT])
        self.rstd = st.sb("rstd", [P, NT])
        self.tmp = st.sb("lntmp", [P, 2, NT])
        self.xs = st.sb("xs", [P, 2, D])
        self.psT = st.ps("psT", [P, 512])
        self.shared = other is None
        self.banks = [self.psT, self.psT if other is None else other]

    def vector_stats(self, v):
        st, X = self.st, self.e["X"]
        for t in range(NT):
            v.bn_stats(self.stats[:, t, :], X[:, t, :]).then_inc(st.sem("bn"), 1)
        v.wait_ge(st.sem("bn"), NT)
        s = self.stats
        v.tensor_tensor(self.tmp[:, 0, :], s[:, :, 1], s[:, :, 4], ALU.add).then_inc(st.sem("ln"), 1)
        v.tensor_tensor(self.tmp[:, 1, :], s[:, :, 1], s[:, :, 4], ALU.subtract).then_inc(st.sem("ln"), 1)
        v.tensor_tensor(self.rstd[:, :], s[:, :, 2], s[:, :, 5], ALU.add).then_inc(st.sem("ln"), 1)
        v.wait_ge(st.sem("ln"), 3)
        v.tensor_scalar(self.mean[:, :], self.tmp[:, 0, :], 0.5, None, ALU.mult).then_inc(st.sem("ln"), 1)
        v.scalar_tensor_tensor(self.tmp[:, 1, :], self.tmp[:, 1, :], 0.25, self.tmp[:, 1, :],
                               ALU.mult, ALU.mult).then_inc(st.sem("ln"), 1)
        v.tensor_scalar(self.rstd[:, :], self.rstd[:, :], 1.0 / D, LN_EPS, ALU.mult, ALU.add).then_inc(st.sem("ln"), 1)
        v.wait_ge(st.sem("ln"), 6)
        v.tensor_tensor(self.tmp[:, 0, :], self.rstd[:, :], self.tmp[:, 1, :], ALU.add).then_inc(st.sem("ln_var"), 1)
        v.wait_ge(st.sem("ln_std"), 1)
        v.reciprocal(self.rstd[:, :], self.tmp[:, 1, :]).then_inc(st.sem("ln_rstd"), 1)
        v.wait_ge(st.sem("ln_rstd"), 1)

    def scalar_std(self, a):
        st = self.st
        a.wait_ge(st.sem("ln_var"), 1)
        a.activation(self.tmp[:, 1, :], self.tmp[:, 0, :], ACT.Sqrt).then_inc(st.sem("ln_std"), 1)

    def vector_tile(self, v, p, u):
        st, X, t = self.st, self.e["X"], 2 * p + u
        v.wait_ge(st.sem("xs_free", u), p)
        v.tensor_scalar(self.xs[:, u, :], X[:, t, :], self.mean[:, bass.ds(t, 1)],
                        self.rstd[:, bass.ds(t, 1)], ALU.subtract, ALU.mult).then_inc(st.sem("xs_ready", u), 1)

    def tensor_tile(self, pe, p, u):
        st = self.st
        pe.wait_ge(st.sem("xs_ready", u), p + 1)
        if self.shared:
            pe.wait_ge(st.sem("xnT_ready", 1 - u), p + u)
        else:
            pe.wait_ge(st.sem("xnT_ready", u), p)
        for k in range(KD):
            mm = pe.transpose(self.banks[u][:, k * P:(k + 1) * P], self.xs[:, u, k * P:(k + 1) * P], self.e["ident"][:, :])
        mm.then_inc(st.sem("xs_free", u), 1)

    def scalar_tile(self, a, p, u, out):
        st = self.st
        a.wait_ge(st.sem("xs_free", u), p + 1)
        carry_waits(a, st.sem("passed_act"))
        a.activation(out, self.banks[u][:, 0:D].rearrange("p (k n) -> p k n", k=KD), ACT.Copy).then_inc(st.sem("xnT_ready", u), 1)


def in_steps(eng, parts, n, R, order=None):
    lag = len(parts) - 1
    assert n > lag // R

    def step(p, j, begun=lag + 1, over=0):
        for i in order or range(lag + 1):
            a = j + lag - i
            if parts[i] and over <= i < begun:
                parts[i](p + a // R, a % R)

    for j in range(-lag, 0):
        step(0, j, begun=lag + j + 1)
    rounds = n - 1 - (lag - 1) // R if lag else n
    with eng.Fori(0, rounds) as p:
        for j in range(R):
            step(p, j)
    for b in range(R * rounds, R * n):
        step(b // R, b % R, over=lag + b - R * n + 1)


def carry_waits(eng, passed):
    eng.sem_inc(passed, 1)


def stage_mla(nc, e, d):
    st = Stage(nc, "a")
    sb, ps, sem = st.sb, st.ps, st.sem
    X, ident = e["X"], e["ident"]
    table = d["key_table"]
    W2 = KVC + RD

    with st.ctx:
        kcompT, krope = sb("kcompT", [KVC, D]), sb("krope", [KVC, RD])
        qup, kup, vup, wout = (sb("qup", [HD, H, QC]), sb("kup", [HD, H, KVC]),
                               sb("vup", [HD, H, KVC]), sb("wout", [HD, H, D]))
        wqd = sb("wqd", [P, KD, QC])
        wk = sb("wk", [P, KD, W2])
        wq = sb("wq", [QC, H, W2])
        wo = sb("wo", [P, H // 2, D])
        cosk, sink = sb("cosk", [P, 4, RD]), sb("sink", [P, 4, RD])
        cosq, sinq = sb("cosq", [P, RD]), sb("sinq", [P, RD])
        segi, segf = sb("segi", [P, NT], I32), sb("segf", [P, NT])
        rows = sb("rows", [P, 2, NT])
        key = sb("key", [P, LOOK, NT])
        good = sb("good", [P, LOOK, NT])
        none = sb("none", [P, 2, NT])
        idx = sb("idx", [P, LOOK, NT])
        meanw = sb("meanw", [P, 1])
        c = sb("c", [P, 2, 2, KD, SK])
        tab = sb("tab", [P, 2, 4, W2])
        ra = sb("ra", [P, 2, 2, 4, RD])
        mrow = sb("mrow", [1, 2, 2, W2])
        ln = LayerNorm(st, e)
        xts = sb("xts", [P, 2, KD, P])
        qc = sb("qc", [QC, 2, P])
        q = sb("q", [P, 2, H, W2])
        kg = sb("kg", [P, 2, LOOK, W2])
        kra = sb("kra", [P, 2, 2, LOOK, RD])
        idxt = sb("idxt", [P, 2, 4], U32)
        prod = sb("prod", [P, LOOK, H, W2])
        sc = sb("sc", [P, 2, H, 4])
        mx = sb("mx", [P, 2, 4, H])
        ol = sb("ol", [P, 2, 3, H, KVC])
        oT = sb("oT", [P, 2, 8, P])
        seen = sb("seen", [P, NT, LOOK])
        psk = ps("psk", [P, 4, 512])
        psm = ps("psm", [P, 2, 512])
        aux = ps("aux", [P, 512])

        LOADS = [(kcompT[:, :], d["kcompT"]), (krope[:, :], d["krope"]), (qup[:, :, :], d["qup"]),
                 (kup[:, :, :], d["kup"]), (vup[:, :, :], d["vup"]), (wout[:, :, :], d["wout"]),
                 (wqd[:, :, :], d["wqd"]), (wk[:, :, 0:KVC], d["kcomp"]), (wq[:, :, KVC:W2], d["qrope"]),
                 (cosk[:, :, :], d["cosk"]), (sink[:, :, :], d["sink"]), (cosq[:, :], d["cosq"]),
                 (sinq[:, :], d["sinq"]), (segi[:, :], d["seg"]), (rows[:, :, :], d["rows"]),
                 (meanw[:, :], d["meanw"])]
        W_ALL = 16 * len(LOADS)
        ctx_v = d["ctxT"].rearrange("(g b) p k n -> g p b k n", b=2)
        tab_v = table[0:KROWS, :].rearrange("(g j p) c -> g p j c", p=P, j=4)
        mean_v = table[KROWS:KROWS + B, :].rearrange("(g b) c -> g (b c)", b=2)

        with nc.Block() as block:
            @block.sync
            def _(sp):
                for dst, src in LOADS:
                    sp.dma_start(dst, src).then_inc(sem("weights"), 16)
                with sp.Fori(0, NT // 2) as p:
                    for u in range(2):
                        sp.wait_ge(sem("keys_done", u), p)
                        sp.dma_start(c[:, u], ctx_v[2 * p + u]).then_inc(sem("ctx", u), 16)

            @block.tensor
            def _(pe):
                pe.wait_ge(sem("weights"), W_ALL)
                for k in range(KD):
                    mm = pe.matmul(psk[:, 0, k * RD:(k + 1) * RD], kcompT[:, k * P:(k + 1) * P], krope[:, :],
                                   start=True, stop=True)
                for h in range(H):
                    mm = pe.matmul(psk[0:QC, 1 + h // 8, (h % 8) * KVC:(h % 8 + 1) * KVC], qup[:, h, :], kup[:, h, :],
                                   start=True, stop=True)
                mm.then_inc(sem("prep"), 1)
                for r in range(4):
                    if r:
                        pe.wait_ge(sem("wo_copied"), r)
                    else:
                        pe.wait_ge(sem("prep_copied"), 2 + KD)
                    for i in range(4):
                        h = 4 * r + i
                        mm = pe.matmul(psm[64 * (h % 2):64 * (h % 2) + KVC, i // 2, 0:D], vup[:, h, :], wout[:, h, :],
                                       start=True, stop=True)
                    mm.then_inc(sem("wo_prod"), 1)
                pe.wait_ge(sem("wo_copied"), 4)

                def keys(p, u):
                    pe.wait_ge(sem("ctx", u), 16 * (p + 1))
                    pe.wait_ge(sem("rope", u), p)
                    pe.wait_ge(sem("nope", u), p)
                    for j in range(4):
                        for k in range(KD):
                            mm = pe.matmul(psk[:, u, j * P:(j + 1) * P], c[:, u, j // 2, k, (j % 2) * P:(j % 2 + 1) * P],
                                           wk[:, k, :], start=(k == 0), stop=(k == KD - 1))
                    mm.then_inc(sem("keys_done", u), 1)

                def mean(p, u):
                    pe.wait_ge(sem("rope", u), p + 1)
                    pe.wait_ge(sem("nope", u), p + 1)
                    pe.wait_ge(sem("mean_copied", u), p)
                    for j in range(4):
                        mm = pe.matmul(psm[0:1, u, (j // 2) * W2:(j // 2 + 1) * W2], meanw[:, :], tab[:, u, j, :],
                                       start=(j % 2 == 0), stop=(j % 2 == 1))
                    mm.then_inc(sem("mean_done", u), 1)

                in_steps(pe, [keys, mean], NT // 2, 2)

            @block.scalar
            def _(a):
                ln.scalar_std(a)
                a.wait_ge(sem("prep"), 1)
                for k in range(KD):
                    a.activation(wk[:, k, KVC:W2], psk[:, 0, k * RD:(k + 1) * RD], ACT.Copy).then_inc(sem("prep_copied"), 1)
                for k in range(2):
                    a.activation(wq[:, 8 * k:8 * k + 8, 0:KVC], psk[0:QC, 1 + k, :].rearrange("p (h c) -> p h c", h=8),
                                 ACT.Copy).then_inc(sem("prep_copied"), 1)
                for r in range(4):
                    a.wait_ge(sem("wo_prod"), r + 1)
                    a.activation(wo[:, 2 * r:2 * r + 2, :], psm[:, 0:2, 0:D], ACT.Copy).then_inc(sem("wo_copied"), 1)

                def nope(p, u):
                    a.wait_ge(sem("keys_done", u), p + 1)
                    a.wait_ge(sem("tab_stored", u), 16 * p)
                    a.wait_ge(sem("mean_done", u), p)
                    a.activation(tab[:, u, :, 0:KVC], psk[:, u, :].rearrange("p (j c) -> p j c", j=4)[:, :, 0:KVC],
                                 ACT.Copy).then_inc(sem("nope", u), 1)

                def mean(p, u):
                    a.wait_ge(sem("mean_done", u), p + 1)
                    a.wait_ge(sem("mean_stored", u), 16 * p)
                    a.activation(mrow[:, u, :, :].rearrange("p b c -> p (b c)"), psm[0:1, u, 0:2 * W2],
                                 ACT.Copy).then_inc(sem("mean_copied", u), 1)
                    a.wait_ge(sem("mean_copied", u), p + 1)
                    a.dma_start(mean_v[bass.ds(2 * p + u, 1), :], mrow[:, u, :, :].rearrange("p b c -> p (b c)")).then_inc(sem("mean_stored", u), 16)

                in_steps(a, [nope, mean], NT // 2, 2)

            @block.gpsimd
            def _(g):
                with g.Fori(0, NT // 2) as p:
                    for u in range(2):
                        g.wait_ge(sem("rope", u), p + 1)
                        g.wait_ge(sem("nope", u), p + 1)
                        g.dma_start(tab_v[2 * p + u], tab[:, u]).then_inc(sem("tab_stored", u), 16)
                for u in range(2):
                    g.wait_ge(sem("tab_stored", u), 16 * (NT // 2))
                    g.wait_ge(sem("mean_stored", u), 16 * (NT // 2))

            @block.vector
            def _(v):
                ln.vector_stats(v)
                v.wait_ge(sem("weights"), W_ALL)
                v.tensor_copy(segf[:, :], segi[:, :]).then_inc(sem("seg"), 1)
                v.wait_ge(sem("seg"), 1)
                for j in range(LOOK):
                    v.tensor_scalar(key[:, j, :], segf[:, :], float(-j), None, ALU.add).then_inc(sem("seg"), 1)
                v.tensor_scalar(none[:, 0, :], segf[:, :], 0.0, None, ALU.is_lt).then_inc(sem("seg"), 1)
                v.tensor_scalar(none[:, 1, :], segf[:, :], float(SK + LOOK - 1), None, ALU.is_ge).then_inc(sem("seg"), 1)
                v.wait_ge(sem("seg"), 6)
                v.tensor_scalar(good[:, :, :], key[:, :, :], 0.0, None, ALU.is_ge).then_inc(sem("seg"), 1)
                v.tensor_scalar(idx[:, :, :], key[:, :, :], float(SK), None, ALU.is_lt).then_inc(sem("seg"), 1)
                v.tensor_tensor(none[:, 0, :], none[:, 0, :], none[:, 1, :], ALU.add).then_inc(sem("seg"), 1)
                v.wait_ge(sem("seg"), 9)
                v.tensor_tensor(good[:, :, :], good[:, :, :], idx[:, :, :], ALU.mult).then_inc(sem("seg"), 1)
                v.wait_ge(sem("seg"), 10)
                v.tensor_scalar(idx[:, :, :], key[:, :, :], 0.0, float(SK - 1), ALU.max, ALU.min).then_inc(sem("seg"), 1)
                v.wait_ge(sem("seg"), 11)
                v.tensor_tensor(idx[:, :, :], idx[:, :, :], bc(rows[:, 0, None, :], [P, LOOK, NT]), ALU.add).then_inc(sem("seg"), 1)
                v.tensor_tensor(good[:, 0, :], good[:, 0, :], none[:, 0, :], ALU.add).then_inc(sem("seg"), 1)
                v.wait_ge(sem("seg"), 13)
                v.tensor_tensor(none[:, 1, :], rows[:, 1, :], idx[:, 0, :], ALU.subtract).then_inc(sem("seg"), 1)
                v.wait_ge(sem("seg"), 14)
                v.tensor_tensor(none[:, 1, :], none[:, 1, :], none[:, 0, :], ALU.mult).then_inc(sem("seg"), 1)
                v.wait_ge(sem("seg"), 15)
                v.tensor_tensor(idx[:, 0, :], idx[:, 0, :], none[:, 1, :], ALU.add).then_inc(sem("seg"), 1)
                v.tensor_scalar(seen[:, :, :].rearrange("p t j -> p j t"), good[:, :, :], -1.0, -NEG, ALU.add, ALU.mult).then_inc(sem("seg"), 1)
                v.wait_ge(sem("seg"), 17)
                with v.Fori(0, NT // 2) as p:
                    for u in range(2):
                        v.wait_ge(sem("nope", u), p + 1)
                        v.wait_ge(sem("tab_stored", u), 16 * p)
                        kr = psk[:, u, :].rearrange("p (j c) -> p j c", j=4)[:, :, KVC:W2]
                        hf = RD // 2
                        v.tensor_tensor(ra[:, u, 0], kr, cosk[:, :, :], ALU.mult).then_inc(sem("ra", u), 1)
                        v.tensor_tensor(ra[:, u, 1, :, 0:hf], kr[:, :, hf:RD], sink[:, :, 0:hf], ALU.mult).then_inc(sem("ra", u), 1)
                        v.tensor_tensor(ra[:, u, 1, :, hf:RD], kr[:, :, 0:hf], sink[:, :, hf:RD], ALU.mult).then_inc(sem("ra", u), 1)
                        v.wait_ge(sem("ra", u), 3 * p + 3)
                        v.tensor_tensor(tab[:, u, :, KVC:W2], ra[:, u, 0], ra[:, u, 1], ALU.add).then_inc(sem("rope", u), 1)

        SCALE = float(1.0 / np.sqrt(np.float32(HD + RD)))
        hf = RD // 2
        with nc.Block() as block:
            @block.gpsimd
            def _(g):
                def front(p, u):
                    g.wait_ge(sem("idxt", u), p + 1)
                    g.wait_ge(sem("ol", u), 3 * p)
                    carry_waits(g, sem("passed_pool"))
                    for j in range(LOOK):
                        g.indirect_dma_start(out=kg[:, u, j, :], out_offset=None, in_=table[:, :],
                                             in_offset=bass.IndirectOffsetOnAxis(ap=idxt[:, u, j:j + 1], axis=0)
                                             ).then_inc(sem("kg", u), 16)

                def weighted(p, u):
                    g.wait_ge(sem("probs", u), p + 1)
                    g.wait_ge(sem("ol_free", u), p)
                    for j in range(LOOK):
                        g.tensor_tensor(ol[:, u, j], bc(sc[:, u, :, j:j + 1], [P, H, KVC]),
                                        bc(kg[:, u, j:j + 1, 0:KVC], [P, H, KVC]), ALU.mult).then_inc(sem("ol", u), 1)
                    g.wait_ge(sem("ol", u), 3 * p + 3)
                    g.tensor_tensor(ol[:, u, 0], ol[:, u, 0], ol[:, u, 1], ALU.add).then_inc(sem("osum", u), 1)
                    g.wait_ge(sem("osum", u), p + 1)
                    g.tensor_tensor(ol[:, u, 0], ol[:, u, 0], ol[:, u, 2], ALU.add).then_inc(sem("o_lat", u), 1)

                in_steps(g, [front, None, weighted], NT // 2, 2, order=(2, 0))

            @block.tensor
            def _(pe):
                def front(p, u):
                    t = 2 * p + u
                    pe.wait_ge(sem("qc"), t)
                    ln.tensor_tile(pe, p, u)
                    pe.wait_ge(sem("xnT_ready", u), p + 1)
                    for k in range(KD):
                        mm = pe.matmul(ln.psT[0:QC, D:D + P], wqd[:, k, :], xts[:, u, k, :], start=(k == 0), stop=(k == KD - 1))
                    mm.then_inc(sem("qc_done"), 1)
                    pe.wait_ge(sem("qc"), t + 1)
                    pe.wait_ge(sem("q", 1 - u), p + u)
                    for n in range(4):
                        mm = pe.matmul(psk[:, n, :], qc[:, u, :], wq[:, 4 * n:4 * n + 4, :].rearrange("p h c -> p (h c)"),
                                       start=True, stop=True)
                    mm.then_inc(sem("q_done"), 1)

                def turn(p, u):
                    t = 2 * p + u
                    pe.wait_ge(sem("o_lat", u), p + 1)
                    pe.wait_ge(sem("oT"), t)
                    for n in range(8):
                        mm = pe.transpose(psm[:, n // 4, (n % 4) * P:(n % 4 + 1) * P],
                                          ol[:, u, 0].rearrange("p h c -> p (h c)")[:, n * P:(n + 1) * P], ident[:, :])
                    mm.then_inc(sem("ol_free", u), 1)

                def output(p, u):
                    t = 2 * p + u
                    pe.wait_ge(sem("oT"), t + 1)
                    pe.wait_ge(sem("x_added"), t)
                    for n in range(8):
                        mm = pe.matmul(aux[:, 0:D], oT[:, u, n, :], wo[:, n, :], start=(n == 0), stop=(n == 7))
                    mm.then_inc(sem("y_done"), 1)

                in_steps(pe, [front, None, turn, output], NT // 2, 2, order=(0, 3, 2))

            @block.scalar
            def _(a):
                def front(p, u):
                    t = 2 * p + u
                    a.wait_ge(sem("qc_done"), 2 * p)
                    ln.scalar_tile(a, p, u, xts[:, u])
                    a.wait_ge(sem("qc_done"), t + 1)
                    a.activation(qc[:, u, :], ln.psT[0:QC, D:D + P], ACT.Copy).then_inc(sem("qc"), 1)
                    a.wait_ge(sem("q_done"), t + 1)
                    a.wait_ge(sem("scores", u), p)
                    a.activation(q[:, u].rearrange("p h c -> p (h c)"), psk[:, :, :].rearrange("p n c -> p (n c)"), ACT.Copy).then_inc(sem("q", u), 1)

                def exps(p, u):
                    a.wait_ge(sem("shifted", u), p + 1)
                    a.activation(sc[:, u, :, 0:LOOK], sc[:, u, :, 0:LOOK], ACT.Exp).then_inc(sem("exp", u), 1)

                def turned(p, u):
                    a.wait_ge(sem("ol_free", u), p + 1)
                    a.activation(oT[:, u].rearrange("p n c -> p (n c)"), psm[:, :, :].rearrange("p n c -> p (n c)"), ACT.Copy).then_inc(sem("oT"), 1)

                in_steps(a, [front, exps, turned], NT // 2, 2)

            @block.vector
            def _(v):
                def front(p, u):
                    v.wait_ge(sem("kg", u), 48 * p)
                    v.tensor_copy(idxt[:, u, 0:LOOK], idx[:, :, bass.ds(2 * p + u, 1)].rearrange("p j o -> p (j o)")).then_inc(sem("idxt", u), 1)
                    ln.vector_tile(v, p, u)

                def scores(p, u):
                    t = 2 * p + u
                    v.wait_ge(sem("kg", u), 48 * (p + 1))
                    kk = kg[:, u, :, KVC:W2]
                    v.tensor_tensor(kra[:, u, 0], kk, bc(cosq[:, None, :], [P, LOOK, RD]), ALU.mult).then_inc(sem("kra", u), 1)
                    v.tensor_tensor(kra[:, u, 1, :, 0:hf], kk[:, :, hf:RD], bc(sinq[:, None, 0:hf], [P, LOOK, hf]), ALU.mult).then_inc(sem("kra", u), 1)
                    v.tensor_tensor(kra[:, u, 1, :, hf:RD], kk[:, :, 0:hf], bc(sinq[:, None, hf:RD], [P, LOOK, hf]), ALU.mult).then_inc(sem("kra", u), 1)
                    v.wait_ge(sem("kra", u), 3 * p + 3)
                    v.tensor_tensor(kk, kra[:, u, 0], kra[:, u, 1], ALU.add).then_inc(sem("kr", u), 1)
                    v.wait_ge(sem("kr", u), p + 1)
                    v.wait_ge(sem("q", u), p + 1)
                    v.wait_ge(sem("ol", u), 3 * p)
                    for j in range(LOOK):
                        for h in range(H):
                            ins = v.tensor_tensor_reduce(prod[:, j, h, :], q[:, u, h, :], kg[:, u, j, :], 1.0, 0.0, ALU.mult, ALU.add,
                                                         sc[:, u, h, j:j + 1])
                    ins.then_inc(sem("sdot", u), 1)
                    v.wait_ge(sem("sdot", u), p + 1)
                    s3 = sc[:, u, :, 0:LOOK]
                    v.scalar_tensor_tensor(s3, s3, SCALE, bc(seen[:, bass.ds(t, 1), :], [P, H, LOOK]),
                                           ALU.mult, ALU.add).then_inc(sem("scores", u), 1)
                    v.wait_ge(sem("scores", u), p + 1)
                    v.tensor_reduce(mx[:, u, 0, :], s3, AX_X, ALU.max).then_inc(sem("smax", u), 1)
                    v.wait_ge(sem("smax", u), p + 1)
                    v.tensor_tensor(s3, s3, bc(mx[:, u, 0, :, None], [P, H, LOOK]), ALU.subtract).then_inc(sem("shifted", u), 1)
                    v.wait_ge(sem("exp", u), p + 1)
                    v.tensor_reduce(mx[:, u, 1, :], s3, AX_X, ALU.add).then_inc(sem("ssum", u), 1)
                    v.wait_ge(sem("ssum", u), p + 1)
                    v.reciprocal(mx[:, u, 2, :], mx[:, u, 1, :]).then_inc(sem("srec", u), 1)
                    v.wait_ge(sem("srec", u), p + 1)
                    v.tensor_tensor(s3, s3, bc(mx[:, u, 2, :, None], [P, H, LOOK]), ALU.mult).then_inc(sem("probs", u), 1)

                def added(p, u):
                    t = 2 * p + u
                    v.wait_ge(sem("y_done"), t + 1)
                    v.tensor_tensor(X[:, bass.ds(t, 1), :].rearrange("p o d -> p (o d)"), X[:, bass.ds(t, 1), :].rearrange("p o d -> p (o d)"),
                                    aux[:, 0:D], ALU.add).then_inc(sem("x_added"), 1)

                in_steps(v, [front, scores, None, added], NT // 2, 2)


def stage_mamba(nc, e, d):
    st = Stage(nc, "b")
    sb, ps, sem = st.sb, st.ps, st.sem
    X, ident = e["X"], e["ident"]
    NB, CQ = GT // S, 2
    NQ = NST // CQ
    HB, DB = 8, 4
    PG, PD = NQ * NCH // HB, NQ * NCH // DB
    LP = S + KC - 1

    with st.ctx:
        win = sb("win", [P, KD, 2 * DI])
        convw, convb = sb("convw", [P, NCH, KC]), sb("convb", [P, NCH])
        wx = sb("wx", [P, NCH, DTR + 2 * NST])
        wdt, bdt = sb("wdt", [DTR, DI]), sb("bdt", [P, NCH])
        A, Dp = sb("A", [P, NCH, NST]), sb("Dp", [P, NCH])
        wout = sb("wout", [P, NCH, D])
        pso = ps("pso", [P, 512])
        ln = LayerNorm(st, e, pso)
        xnT = sb("xnT", [P, KD, T])
        xcp = sb("xcp", [P, NCH, NB, LP])
        xz = sb("xz", [P, 2, 2 * NCH, GT])
        th = sb("th", [P, NCH, GT])
        delta, dx = sb("delta", [P, 2, NCH, GT]), sb("dx", [P, 2, NCH, GT])
        dbc = sb("dbc", [DTR + 2 * NST, GT])
        bcb = sb("bcb", [P, 2, 2, CQ, GT])
        dA = sb("dA", [P, DB, CQ, GT])
        h = sb("h", [P, HB, CQ, GT])
        yz = sb("yz", [P, NCH, GT])
        psy = ps("psy", [P, NCH, GT])
        psw = ps("psw", [P, 2, GT])

        LOADS = [(win[:, :, :], d["b_win"]), (convw[:, :, :], d["b_convw"]), (convb[:, :], d["b_convb"]),
                 (wx[:, :, :], d["b_wx"]), (wdt[:, :], d["b_wdt"]), (bdt[:, :], d["b_bdt"]),
                 (A[:, :, :], d["b_alog"]), (Dp[:, :], d["b_dp"]), (wout[:, :, :], d["b_wout"])]
        W_ALL = 16 * len(LOADS)
        rows = d["bc_rows"]
        PER = (7, 6)

        def buf(t, g):
            v = t[:, bass.ds(g % 2, 1)]
            return v.rearrange("p o c n -> p (o c) n")

        def wait_bank(eng, name, g, r, more):
            eng.wait_ge(sem(name, r % 2), PER[r % 2] * g + r // 2 + more)

        NP = 15
        TENSOR_AT = (8, 9, 10, 12, 12, 12, 13, 13, None, 18, 21, 21, 22, 23, None)
        SCALAR_AT = (11, 12, 13, 13, 16, 17, 18, 21, 21, 23, 28, 28, 31, 31, 31)
        VECTOR_AT = (12, 13, 16, 17) + (None,) * 11
        POOL_AT = (None,) * 14 + (31,)
        STEPS, FIRST = NQ * NCH, 8
        TENSOR_TAIL = (None,) * 4 + (33, 33, 36, 37)
        VECTOR_TAIL = (30, 31, 31, 32, 36, 37, 39, 39)
        NO_TAIL = (None,) * 8

        def interleave(eng, piece, step, tail, at, tail_at):
            def tails(g, i):
                for r in range(8):
                    if tail_at[r] == i:
                        tail(g, r)

            for r in range(NP):
                if at[r] is not None:
                    piece(0, r)
            for i in range(FIRST):
                step(0, i)
            with eng.Fori(0, NG - 1) as g:
                for i in range(FIRST, STEPS):
                    step(g, i)
                    tails(g, i)
                    for r in range(NP):
                        if at[r] == i:
                            piece(g + 1, r)
                for i in range(FIRST):
                    step(g + 1, i)
                    tails(g, STEPS + i)
            for i in range(FIRST, STEPS):
                step(NG - 1, i)
                tails(NG - 1, i)
            for i in range(FIRST):
                tails(NG - 1, STEPS + i)

        with nc.Block() as block:
            @block.sync
            def _(sp):
                for dst, src in LOADS:
                    sp.dma_start(dst, src).then_inc(sem("weights"), 16)

                def load(g, nq, first=False):
                    if nq == 0:
                        sp.wait_ge(sem("rows_stored"), 16 * (g + 1))
                    if not first:
                        last = NCH * (nq - 1) - 1
                        sp.wait_ge(sem("hc", last % HB), PG * g + last // HB + 1)
                    for k in range(2):
                        src = rows[bass.ds(g, 1), k * NST + CQ * nq:k * NST + CQ * nq + CQ, :].rearrange("o n t -> (o n t)")
                        sp.dma_start(bcb[:, nq % 2, k].rearrange("p n t -> p (n t)"), src.partition_broadcast(P)).then_inc(sem("bcast", nq % 2), 16)

                load(0, 0, True)
                load(0, 1, True)
                with sp.Fori(0, NG - 1) as g:
                    for nq in range(2, NQ):
                        load(g, nq)
                    load(g + 1, 0)
                    load(g + 1, 1)
                for nq in range(2, NQ):
                    load(NG - 1, nq)

            @block.tensor
            def _(pe):
                with pe.Fori(0, NT // 2) as p:
                    for u in range(2):
                        ln.tensor_tile(pe, p, u)
                for u in range(2):
                    pe.wait_ge(sem("xnT_ready", u), NT // 2)
                pe.wait_ge(sem("weights"), W_ALL)

                def piece(g, r):
                    if r < 8:
                        wait_bank(pe, "psw_free", g, r, 0)
                        for k in range(KD):
                            mm = pe.matmul(psw[:, r % 2, :], win[:, k, r * P:(r + 1) * P], xnT[:, k, bass.ds(GT * g, GT)],
                                           start=(k == 0), stop=(k == KD - 1))
                        mm.then_inc(sem("psw_ready", r % 2), 1)
                    elif r == 9:
                        pe.wait_ge(sem("silu"), g + 1)
                        wait_bank(pe, "psw_free", g, 8, 0)
                        for c in range(NCH):
                            mm = pe.matmul(psw[0:DTR + 2 * NST, 0, :], wx[:, c, :], buf(xz, g)[:, c, :], start=(c == 0), stop=(c == NCH - 1))
                        mm.then_inc(sem("psw_ready", 0), 1)
                    elif 10 <= r < 14:
                        c = r - 10
                        pe.wait_ge(sem("dbc"), g + 1)
                        wait_bank(pe, "psw_free", g, 9 + c, 0)
                        pe.matmul(psw[:, (9 + c) % 2, :], wdt[:, c * P:(c + 1) * P], dbc[0:DTR, :], start=True, stop=True
                                  ).then_inc(sem("psw_ready", (9 + c) % 2), 1)

                def step(g, i):
                    s, c, nq = i % HB, i % NCH, i // NCH
                    if nq == 0:
                        pe.wait_ge(sem("y", c), g)
                    pe.wait_ge(sem("hc", s), PG * g + i // HB + 1)
                    for j in range(CQ):
                        mm = pe.matmul(psy[:, c, :], ident[:, :], h[:, s, j, :], start=(nq == 0 and j == 0),
                                       stop=(nq == NQ - 1 and j == CQ - 1))
                    mm.then_inc(sem("h_free", s), 1)

                def tail(g, r):
                    t = r - 4
                    if t == 0:
                        pe.wait_ge(sem("yz"), NCH * (g + 1))
                    out = [pso, ln.psT][t % 2]
                    pe.wait_ge(sem("x_added", t % 2), 2 * g + t // 2)
                    for cc in range(NCH):
                        mm = pe.matmul(out[:, 0:D], yz[:, cc, t * P:(t + 1) * P], wout[:, cc, :], start=(cc == 0), stop=(cc == NCH - 1))
                    mm.then_inc(sem("out", t % 2), 1)

                interleave(pe, piece, step, tail, TENSOR_AT, TENSOR_TAIL)

            @block.scalar
            def _(a):
                ln.scalar_std(a)
                a.wait_ge(sem("weights"), W_ALL)
                a.activation(A[:, :, :], A[:, :, :], ACT.Exp).then_inc(sem("A_exp"), 1)
                with a.Fori(0, NT // 2) as p:
                    for u in range(2):
                        ln.scalar_tile(a, p, u, xnT[:, :, bass.ds(P * (2 * p + u), P)])
                a.wait_ge(sem("pads"), 2)

                def piece(g, r):
                    if r < 8:
                        wait_bank(a, "psw_ready", g, r, 1)
                        if r < NCH:
                            a.wait_ge(sem("conv", r), g)
                            out = xcp[:, r, :, KC - 1:LP]
                        else:
                            out = buf(xz, g)[:, r, :].rearrange("p (b l) -> p b l", b=NB)
                        carry_waits(a, sem("passed_act"))
                        a.activation(out, psw[:, r % 2, :].rearrange("p (b l) -> p b l", b=NB), ACT.Copy).then_inc(sem("psw_free", r % 2), 1)
                    elif r == 8:
                        for c in range(NCH):
                            a.wait_ge(sem("conv", c), g + 1)
                        for c in range(6, 8):
                            wait_bank(a, "psw_free", g, c, 1)
                        carry_waits(a, sem("passed_act"))
                        a.activation(buf(xz, g), buf(xz, g), ACT.Silu).then_inc(sem("silu"), 1)
                    elif r == 9:
                        wait_bank(a, "psw_ready", g, 8, 1)
                        a.wait_ge(sem("rows_stored"), 16 * g)
                        a.activation(dbc[:, :], psw[0:DTR + 2 * NST, 0, :], ACT.Copy).then_inc(sem("psw_free", 0), 1)
                        wait_bank(a, "psw_free", g, 8, 1)
                        a.sem_inc(sem("dbc"), 1)
                        a.dma_start(rows[bass.ds(g, 1)].rearrange("o n t -> (o n) t"), dbc[DTR:DTR + 2 * NST, :]).then_inc(sem("rows_stored"), 16)
                    elif 10 <= r < 14:
                        c = r - 10
                        wait_bank(a, "psw_ready", g, 9 + c, 1)
                        if c == 0:
                            a.wait_ge(sem("delta"), g)
                        src = psw[:, (9 + c) % 2, :]
                        carry_waits(a, sem("passed_act"))
                        a.activation(buf(delta, g)[:, c, :], src, ACT.Relu, bias=bdt[:, c:c + 1])
                        a.activation(th[:, c, :], src, ACT.Abs, bias=bdt[:, c:c + 1]).then_inc(sem("psw_free", (9 + c) % 2), 1)
                    elif r == 14:
                        a.wait_ge(sem("psw_free", 0), 7 * g + 7)
                        a.wait_ge(sem("psw_free", 1), 6 * g + 6)
                        a.activation(th[:, :, :], th[:, :, :], ACT.Exp, scale=-1.0).then_inc(sem("sp_exp"), 1)
                        a.wait_ge(sem("sp_exp"), g + 1)
                        a.activation(th[:, :, :], th[:, :, :], ACT.Ln, bias=1.0).then_inc(sem("sp_ln"), 1)

                def step(g, i):
                    s, c, nq = i % DB, i % NCH, i // NCH
                    if i == 0:
                        a.wait_ge(sem("delta"), g + 1)
                        a.wait_ge(sem("A_neg"), 1)
                    a.wait_ge(sem("scan", s), PD * g + i // DB)
                    carry_waits(a, sem("passed_act"))
                    dv = buf(delta, g)[:, c, :].rearrange("p (b l) -> p b l", b=NB)[:, :, 1:S]
                    for j in range(CQ):
                        n = CQ * nq + j
                        ins = a.activation(dA[:, s, j, :].rearrange("p (b l) -> p b l", b=NB)[:, :, 1:S], dv, ACT.Exp,
                                           scale=A[:, c, n:n + 1])
                    ins.then_inc(sem("dA", s), 1)

                interleave(a, piece, step, None, SCALAR_AT, NO_TAIL)
                a.wait_ge(sem("rows_stored"), 16 * NG)

            @block.gpsimd
            def _(g_):
                g_.memset(dA[:, :, :, :], 0.0).then_inc(sem("pads"), 1)
                g_.memset(xcp[:, :, :, 0:KC - 1], 0.0).then_inc(sem("pads"), 1)

                def piece(g, r):
                    if r == 14:
                        g_.wait_ge(sem("sp_ln"), g + 1)
                        carry_waits(g_, sem("passed_pool"))
                        g_.tensor_tensor(buf(delta, g), buf(delta, g), th[:, :, :], ALU.add).then_inc(sem("delta"), 1)
                        g_.wait_ge(sem("delta"), g + 1)
                        carry_waits(g_, sem("passed_pool"))
                        g_.tensor_tensor(buf(dx, g), buf(delta, g), buf(xz, g)[:, 0:NCH, :], ALU.mult).then_inc(sem("dx"), 1)
                        g_.wait_ge(sem("dx"), g + 1)

                def step(g, i):
                    s, c, nq = i % HB, i % NCH, i // NCH
                    g_.wait_ge(sem("h_free", s), PG * g + i // HB)
                    if c == 0:
                        g_.wait_ge(sem("bcast", nq % 2), 32 * (NQ // 2 * g + nq // 2 + 1))
                    carry_waits(g_, sem("passed_pool"))
                    g_.tensor_tensor(h[:, s], bc(buf(dx, g)[:, c:c + 1, :], [P, CQ, GT]), bcb[:, nq % 2, 0], ALU.mult).then_inc(sem("bx", s), 1)

                interleave(g_, piece, step, None, POOL_AT, NO_TAIL)

            @block.vector
            def _(v):
                ln.vector_stats(v)
                with v.Fori(0, NT // 2) as p:
                    for u in range(2):
                        ln.vector_tile(v, p, u)
                v.wait_ge(sem("weights"), W_ALL)
                v.wait_ge(sem("A_exp"), 1)
                v.tensor_scalar(A[:, :, :], A[:, :, :], -1.0, None, ALU.mult).then_inc(sem("A_neg"), 1)
                v.wait_ge(sem("pads"), 2)

                def piece(g, r):
                    if r < NCH:
                        wait_bank(v, "psw_free", g, r, 1)
                        acc = buf(xz, g)[:, r, :].rearrange("p (b l) -> p b l", b=NB)
                        v.tensor_scalar(acc, xcp[:, r, :, 0:S], convw[:, r, 0:1], convb[:, r:r + 1], ALU.mult, ALU.add).then_inc(sem("cv", r), 1)
                        for k in range(1, KC):
                            v.wait_ge(sem("cv", r), 3 * g + k)
                            v.scalar_tensor_tensor(acc, xcp[:, r, :, k:k + S], convw[:, r, k:k + 1], acc, ALU.mult, ALU.add
                                                   ).then_inc(sem("cv" if k < KC - 1 else "conv", r), 1)

                def step(g, i):
                    s, q, c, nq = i % HB, i % DB, i % NCH, i // NCH
                    k = PG * g + i // HB
                    v.wait_ge(sem("dA", q), PD * g + i // DB + 1)
                    v.wait_ge(sem("bx", s), k + 1)
                    hs = h[:, s].rearrange("p j n -> p (j n)")
                    v.tensor_tensor_scan(hs, dA[:, q].rearrange("p j n -> p (j n)"), hs, 0.0, ALU.mult, ALU.add).then_inc(sem("scan", q), 1)
                    v.wait_ge(sem("scan", q), PD * g + i // DB + 1)
                    v.tensor_tensor(h[:, s], h[:, s], bcb[:, nq % 2, 1], ALU.mult).then_inc(sem("hc", s), 1)

                def tail(g, r):
                    if r < NCH:
                        c, i = r, STEPS - NCH + r
                        v.wait_ge(sem("h_free", i % HB), PG * g + i // HB + 1)
                        if c < 2:
                            v.wait_ge(sem("out", c), 2 * g)
                        v.scalar_tensor_tensor(yz[:, c, :], buf(xz, g)[:, c, :], Dp[:, c:c + 1], psy[:, c, :], ALU.mult, ALU.add).then_inc(sem("y", c), 1)
                        v.wait_ge(sem("y", c), g + 1)
                        v.tensor_tensor(yz[:, c, :], yz[:, c, :], buf(xz, g)[:, NCH + c, :], ALU.mult).then_inc(sem("yz"), 1)
                    else:
                        t = r - 4
                        out = [pso, ln.psT][t % 2]
                        v.wait_ge(sem("out", t % 2), 2 * g + t // 2 + 1)
                        carry_waits(v, sem("passed_dve"))
                        xt = X[:, bass.ds(4 * g + t, 1), :].rearrange("p o d -> p (o d)")
                        v.tensor_tensor(xt, xt, out[:, 0:D], ALU.add).then_inc(sem("x_added", t % 2), 1)

                interleave(v, piece, step, tail, VECTOR_AT, VECTOR_TAIL)


def stage_moe(nc, e, d, layer):
    st = Stage(nc, f"m{layer}")
    sb, ps, sem = st.sb, st.ps, st.sem
    X, ident = e["X"], e["ident"]
    capped = layer == 0
    K = K0 if capped else K1
    NB_ = E if capped else NB1
    BW, NBW = (IH, 2) if capped else (F1, 1)
    NSB = SB0 if capped else 1
    slot_tok, xn, y = d[f"slot_tok{layer}"], d[f"xn{layer}"], d[f"y{layer}"]
    TR = NB_ // 2 if not capped else E
    NTR = NB_ // TR
    R = 4 if capped else 8

    with st.ctx:
        xnT = sb("xnT", [P, KD, T])
        gslot = sb("gslot", [P, NT, K], U32)
        wts = sb("wts", [P, NT, K])
        ebrow = sb("ebrow", [1, NB_], U32)

        r = Stage(nc, f"m{layer}r")
        rs = r.sem
        with r.ctx:
            gw, gb = r.sb("gw", [P, KD, E]), r.sb("gb", [P, E])
            iota, ltri, ones = r.sb("iota", [P, E]), r.sb("ltri", [P, P]), r.sb("ones", [P, P])
            base, iotab = r.sb("base", [P, E]), r.sb("iotab", [P, 2])
            tokid = r.sb("tokid", [P, NT], I32)
            ln = LayerNorm(r, e, r.ps("psT2", [P, 512]))
            xts = r.sb("xts", [P, 2, KD, P])
            sc, sel = r.sb("sc", [P, NT, E]), r.sb("sel", [P, NT, E])
            ex = r.sb("ex", [P, NT, E])
            row = r.sb("row", [P, 4, NT])
            top, topi, topf = r.sb("top", [P, NT, 8]), r.sb("topi", [P, NT, 8], U32), r.sb("topf", [P, NT, 8])
            oh, pr = r.sb("oh", [P, NT, K, E], BF16), r.sb("pr", [P, NT, K, E])
            ltrib, onesb = r.sb("ltrib", [P, P], BF16), r.sb("onesb", [P, P], BF16)
            before = r.sb("before", [P, NT + 1, E])
            slotf = r.sb("slotf", [P, NT, K])
            sloti = r.sb("sloti", [P, K, NT], U32)
            ids = r.sb("ids", [P, 2, NT], U32)
            zero = r.sb("zero", [P, NB_], I32)
            nb = r.sb("nb", [P, 4, E])
            nbi = r.sb("nbi", [P, 2, E], I32)
            ebc = r.sb("ebc", [P, 2])
            ebr = r.sb("ebr", [1, 2, P])
            gt8, gs = r.sb("gt8", [P, NT, NGR, 8]), r.sb("gs", [P, NT, NGR])
            gm = r.sb("gm", [P, NT, NGR])
            ws13, ws2 = r.sb("ws13", [P, KD, 2, NSB, BW]), r.sb("ws2", [BW, NSB, D])
            sgs, hs = r.sb("sgs", [BW, 2, GT]), r.sb("hs", [BW, NSB, GT])
            psl = r.ps("psl", [P, NT, E])
            psc = r.ps("psc", [P, NT, E])
            pst = r.ps("pst", [P, NT, E])
            pgu = [t[:, :, :].rearrange("p (k t) e -> p k (t e)", k=2) for t in (psl, pst)]

            LOADS = [(gw[:, :, :], d[f"m{layer}_gw"]), (gb[:, :], d[f"m{layer}_gb"].partition_broadcast(P)),
                     (iota[:, :], d["iota_e"].partition_broadcast(P)), (ltri[:, :], d["ltri"]), (ones[:, :], d["ones"]),
                     (base[:, :], d["slot_base"].partition_broadcast(P)), (iotab[:, :], d["iota_b"]), (tokid[:, :], d["tokid"])]
            W_ALL = 16 * len(LOADS)

            with nc.Block() as block:
                @block.sync
                def _(sp):
                    for dst, src in LOADS:
                        sp.dma_start(dst, src).then_inc(rs("weights"), 16)
                    sp.dma_start(ws13[:, :, :, :, :], d[f"m{layer}_ws13"]).then_inc(rs("shared"), 16)
                    sp.dma_start(ws2[:, :, :], d[f"m{layer}_ws2"]).then_inc(rs("shared"), 16)
                    sp.wait_ge(rs("zero"), 1)
                    sp.dma_start(slot_tok.rearrange("(p n) o -> p (n o)", p=P), zero[:, :]).then_inc(rs("table_clear"), 16)
                    with sp.Fori(0, NT // 2) as p:
                        for u in range(2):
                            sp.wait_ge(rs("xs_ready", u), p + 1)
                            sp.dma_start(xn.rearrange("(t p) d -> t p d", p=P)[2 * p + u], ln.xs[:, u, :]).then_inc(rs("xs_stored", u), 16)
                    for u in range(2):
                        sp.wait_ge(rs("xs_stored", u), 16 * (NT // 2))
                    sp.wait_ge(rs("table_clear"), 16)

                @block.tensor
                def _(pe):
                    def logits(p, u):
                        pe.wait_ge(rs("weights"), W_ALL)
                        pe.wait_ge(rs("xts", u), p + 1)
                        pe.wait_ge(rs("logits_out", u), p)
                        for k in range(KD):
                            mm = pe.matmul(psc[:, 8 * u, :], xts[:, u, k, :], gw[:, k, :], start=(k == 0), stop=(k == KD - 1))
                        mm.then_inc(rs("logits", u), 1)

                    in_steps(pe, [lambda p, u: ln.tensor_tile(pe, p, u), logits], NT // 2, 2)
                    for u in range(2):
                        pe.wait_ge(rs("logits_out", u), NT // 2)
                    for k in range(K):
                        pe.wait_ge(rs("oh"), k + 1)
                        for ranks, w in ((psl, ltrib), (pst, onesb)):
                            for n in range(2):
                                mm = pe.matmul(ranks[:, 8 * n:8 * n + 8, :], w[:, :], oh[:, 8 * n:8 * n + 8, k, :], start=(k == 0), stop=(k == K - 1))
                    mm.then_inc(rs("ranks"), 1)
                    if not capped:
                        pe.wait_ge(rs("ebc"), 1)
                        for n in range(2):
                            mm = pe.matmul(psc[0:1, 0:2, :].rearrange("p a b -> p (a b)") if n == 0 else psc[0:1, 2:4, :].rearrange("p a b -> p (a b)"),
                                           ebc[:, n:n + 1], ident[:, :], start=True, stop=True)
                        mm.then_inc(rs("ebt"), 1)
                    pe.wait_ge(rs("shared"), 32)
                    pe.wait_ge(rs("sloti"), K)
                    with pe.Fori(0, NG) as g:
                        for n in range(NSB):
                            s = n % 2
                            nth = (NSB + 1 - s) // 2
                            pe.wait_ge(rs("hs", s), nth * g + n // 2)
                            for k2 in range(2):
                                for k in range(KD):
                                    mm = pe.matmul(pgu[s][0:BW, k2, :], ws13[:, k, k2, n, :], xnT[:, k, bass.ds(GT * g, GT)],
                                                   start=(k == 0), stop=(k == KD - 1))
                            mm.then_inc(rs("gu", s), 1)
                        for s in range(min(2, NSB)):
                            nth = (NSB + 1 - s) // 2
                            pe.wait_ge(rs("hs", s), nth * (g + 1))
                        for t in range(4):
                            pe.wait_ge(rs("x_added", t % 2), 2 * g + t // 2)
                            for n in range(NSB):
                                mm = pe.matmul(ln.banks[t % 2][:, 0:D], hs[:, n, t * P:(t + 1) * P], ws2[:, n, :], start=(n == 0), stop=(n == NSB - 1))
                            mm.then_inc(rs("out", t % 2), 1)

                @block.scalar
                def _(a):
                    ln.scalar_std(a)

                    def rows(p, u):
                        a.wait_ge(rs("logits", u), p)
                        ln.scalar_tile(a, p, u, xnT[:, :, bass.ds(P * (2 * p + u), P)])
                        a.activation(xts[:, u], ln.banks[u][:, 0:D].rearrange("p (k n) -> p k n", k=KD), ACT.Copy).then_inc(rs("xts", u), 1)

                    def logits(p, u):
                        a.wait_ge(rs("logits", u), p + 1)
                        carry_waits(a, rs("passed_act"))
                        a.activation(sc[:, bass.ds(2 * p + u, 1), :].rearrange("p o e -> p (o e)"), psc[:, 8 * u, :], ACT.Copy).then_inc(rs("logits_out", u), 1)

                    in_steps(a, [rows, logits], NT // 2, 2)
                    if capped:
                        a.wait_ge(rs("shifted"), 1)
                        a.activation(ex[:, :, :], sc[:, :, :], ACT.Exp).then_inc(rs("exp"), 1)
                    else:
                        for u in range(2):
                            a.wait_ge(rs("logits_out", u), NT // 2)
                        a.activation(ex[:, :, :], sc[:, :, :], ACT.Exp, scale=-1.0).then_inc(rs("exp"), 1)
                    with a.Fori(0, NG) as g:
                        for n in range(NSB):
                            s = n % 2
                            nth = (NSB + 1 - s) // 2
                            a.wait_ge(rs("hs", s), nth * g + n // 2)
                            a.wait_ge(rs("gu", s), nth * g + n // 2 + 1)
                            a.activation(sgs[:, s, :], pgu[s][0:BW, 0, :], ACT.Silu).then_inc(rs("sgs", s), 1)

                @block.gpsimd
                def _(g):
                    g.memset(zero[:, :], 0).then_inc(rs("zero"), 1)
                    g.wait_ge(rs("weights"), W_ALL)
                    g.wait_ge(rs("table_clear"), 16)
                    with g.Fori(0, K // 2) as p:
                        for u in range(2):
                            g.wait_ge(rs("sloti"), 2 * p + u + 1)
                            g.wait_ge(rs("scattered", u), 16 * NT * p)
                            carry_waits(g, rs("passed_pool"))
                            g.tensor_copy(ids[:, u, :], sloti[:, bass.ds(2 * p + u, 1), :].rearrange("p o t -> p (o t)")).then_inc(rs("ids", u), 1)
                            g.wait_ge(rs("ids", u), p + 1)
                            carry_waits(g, rs("passed_pool"))
                            for t in range(NT):
                                g.indirect_dma_start(out=slot_tok, out_offset=bass.IndirectOffsetOnAxis(ap=ids[:, u, t:t + 1], axis=0),
                                                     in_=tokid[:, t:t + 1], in_offset=None, bounds_check=NB_ * P - 1, oob_is_err=False
                                                     ).then_inc(rs("scattered", u), 16)
                    for u in range(2):
                        g.wait_ge(rs("scattered", u), 16 * NT * (K // 2))

                @block.vector
                def _(v):
                    n_step = [0]

                    def step(ins):
                        n_step[0] += 1
                        ins.then_inc(rs("chain"), 1)
                        v.wait_ge(rs("chain"), n_step[0])

                    ln.vector_stats(v)
                    with v.Fori(0, NT // 2) as p:
                        for u in range(2):
                            v.wait_ge(rs("xs_stored", u), 16 * p)
                            carry_waits(v, rs("passed_dve"))
                            ln.vector_tile(v, p, u)
                    v.wait_ge(rs("weights"), W_ALL)
                    for u in range(2):
                        v.wait_ge(rs("logits_out", u), NT // 2)
                    NE = [P, NT, E]
                    if capped:
                        step(v.tensor_reduce(row[:, 0, :], sc[:, :, :], AX_X, ALU.max))
                        v.tensor_tensor(sc[:, :, :], sc[:, :, :], bc(row[:, 0, :, None], NE), ALU.subtract).then_inc(rs("shifted"), 1)
                        v.wait_ge(rs("exp"), 1)
                        step(v.tensor_reduce(row[:, 1, :], ex[:, :, :], AX_X, ALU.add))
                        step(v.reciprocal(row[:, 2, :], row[:, 1, :]))
                        step(v.tensor_tensor(sc[:, :, :], ex[:, :, :], bc(row[:, 2, :, None], NE), ALU.mult))
                        step(v.tensor_tensor(sel[:, :, :], sc[:, :, :], bc(gb[:, None, :], NE), ALU.add))
                    else:
                        v.wait_ge(rs("exp"), 1)
                        step(v.tensor_scalar(ex[:, :, :], ex[:, :, :], 1.0, None, ALU.add))
                        step(v.reciprocal(sc[:, :, :], ex[:, :, :]))
                        step(v.tensor_tensor(sel[:, :, :], sc[:, :, :], bc(gb[:, None, :], NE), ALU.add))
                        for t in range(NT):
                            for k in range(NGR):
                                ins = v.max(gt8[:, t, k, :], sel[:, t, 8 * k:8 * k + 8])
                        step(ins)
                        step(v.tensor_tensor(gs[:, :, :], gt8[:, :, :, 0], gt8[:, :, :, 1], ALU.add))
                        for t in range(NT):
                            ins = v.max(top[:, t, :], gs[:, t, :])
                        step(ins)
                        for t in range(NT):
                            ins = v.max_index(topi[:, t, :], top[:, t, :], gs[:, t, :])
                        step(ins)
                        step(v.tensor_copy(topf[:, :, 0:TOPG], topi[:, :, 0:TOPG]))
                        g4 = pr[:, :, 0:TOPG, 0:NGR]
                        step(v.tensor_tensor(pr[:, :, 0, 0:NGR], bc(iota[:, None, 0:NGR], [P, NT, NGR]), bc(topf[:, :, 0:1], [P, NT, NGR]), ALU.is_equal))
                        for k in range(1, TOPG):
                            step(v.tensor_tensor(pr[:, :, k, 0:NGR], bc(iota[:, None, 0:NGR], [P, NT, NGR]), bc(topf[:, :, k:k + 1], [P, NT, NGR]), ALU.is_equal))
                        step(v.tensor_reduce(gm[:, :, :], g4.rearrange("p t k g -> p t g k"), AX_X, ALU.add))
                        step(v.tensor_tensor(sel[:, :, :].rearrange("p t (g k) -> p t g k", k=8), sel[:, :, :].rearrange("p t (g k) -> p t g k", k=8),
                                             bc(gm[:, :, :, None], [P, NT, NGR, 8]), ALU.mult))
                    for t in range(NT):
                        ins = v.max(top[:, t, :], sel[:, t, :])
                    step(ins)
                    for t in range(NT):
                        ins = v.max_index(topi[:, t, :], top[:, t, :], sel[:, t, :])
                    step(ins)
                    step(v.tensor_copy(topf[:, :, :], topi[:, :, :]))
                    v.tensor_copy(ltrib[:, :], ltri[:, :])
                    step(v.tensor_copy(onesb[:, :], ones[:, :]))
                    for k in range(K):
                        v.tensor_tensor(oh[:, :, k, :], bc(iota[:, None, :], NE), bc(topf[:, :, k:k + 1], NE), ALU.is_equal).then_inc(rs("oh"), 1)
                    v.wait_ge(rs("ranks"), 1)
                    step(v.memset(before[:, 0, :], 0.0))
                    for t in range(NT):
                        step(v.tensor_tensor(before[:, t + 1, :], before[:, t, :], pst[:, t, :], ALU.add))
                    step(v.tensor_tensor(sel[:, :, :], before[:, 0:NT, :], psl[:, :, :], ALU.add))
                    if capped:
                        step(v.tensor_scalar(ex[:, :, :], sel[:, :, :], float(CAP0), DROPPED, ALU.is_ge, ALU.mult))
                        step(v.tensor_tensor(sel[:, :, :], sel[:, :, :], ex[:, :, :], ALU.add))
                        step(v.tensor_tensor(sel[:, :, :], sel[:, :, :], bc(base[:, None, :], NE), ALU.add))
                    else:
                        step(v.tensor_scalar(nb[:, 0, :], before[:, NT, :], float(P - 1), None, ALU.add))
                        step(v.tensor_copy(nbi[:, 0, :], nb[:, 0, :]))
                        step(v.tensor_single_scalar(nbi[:, 1, :], nbi[:, 0, :], 7, ALU.arith_shift_right))
                        step(v.tensor_copy(nb[:, 1, :], nbi[:, 1, :]))
                        step(v.tensor_tensor_scan(nb[:, 2, :], ones[:, 0:E], nb[:, 1, :], 0.0, ALU.mult, ALU.add))
                        step(v.tensor_tensor(nb[:, 3, :], nb[:, 2, :], nb[:, 1, :], ALU.subtract))
                        step(v.tensor_scalar(nb[:, 3, :], nb[:, 3, :], float(P), None, ALU.mult))
                        step(v.tensor_tensor(sel[:, :, :], sel[:, :, :], bc(nb[:, 3:4, :], NE), ALU.add))
                    for k in range(K):
                        step(v.tensor_tensor(pr[:, :, k, :], oh[:, :, k, :], sel[:, :, :], ALU.mult))
                        step(v.tensor_reduce(slotf[:, :, k], pr[:, :, k, :], AX_X, ALU.add))
                        v.tensor_copy(sloti[:, k, :], slotf[:, :, k]).then_inc(rs("sloti"), 1)
                    if not capped:
                        for n in range(2):
                            step(v.tensor_scalar(ex[:, n, :], nb[:, 2, :], iotab[:, n:n + 1], None, ALU.is_le))
                        step(v.tensor_reduce(ebc[:, :], ex[:, 0:2, :], AX_X, ALU.add))
                        v.tensor_scalar(ebc[:, :], ebc[:, :], float(E - 1), None, ALU.min).then_inc(rs("ebc"), 1)
                        v.wait_ge(rs("ebt"), 1)
                        step(v.tensor_copy(ebrow[:, :], psc[0:1, 0:4, :].rearrange("p a b -> p (a b)")[:, 0:NB_]))
                    for k in range(K):
                        ins = v.tensor_tensor(pr[:, :, k, :], oh[:, :, k, :], sc[:, :, :], ALU.mult)
                    step(ins)
                    step(v.tensor_reduce(wts[:, :, :], pr[:, :, :, :], AX_X, ALU.add))
                    if not capped:
                        step(v.tensor_reduce(row[:, 0, :], wts[:, :, :], AX_X, ALU.add))
                        step(v.tensor_scalar(row[:, 0, :], row[:, 0, :], 1e-20, None, ALU.add))
                        step(v.reciprocal(row[:, 1, :], row[:, 0, :]))
                        step(v.tensor_scalar(wts[:, :, :], wts[:, :, :], RSCALE, None, ALU.mult))
                        step(v.tensor_tensor(wts[:, :, :], wts[:, :, :], bc(row[:, 1, :, None], [P, NT, K]), ALU.mult))
                    if capped:
                        step(v.tensor_scalar(top[:, :, 0:K], slotf[:, :, :], float(SLOTS0), None, ALU.is_lt))
                        step(v.tensor_tensor(wts[:, :, :], wts[:, :, :], top[:, :, 0:K], ALU.mult))
                        step(v.tensor_scalar(slotf[:, :, :], slotf[:, :, :], float(SLOTS0 - 1), None, ALU.min))
                    step(v.tensor_copy(gslot[:, :, :], slotf[:, :, :]))
                    with v.Fori(0, NG) as g:
                        for n in range(NSB):
                            s = n % 2
                            nth = (NSB + 1 - s) // 2
                            if n == 0:
                                for q in range(2):
                                    v.wait_ge(rs("out", q), 2 * g)
                            v.wait_ge(rs("sgs", s), nth * g + n // 2 + 1)
                            v.tensor_tensor(hs[:, n, :], sgs[:, s, :], pgu[s][0:BW, 1, :], ALU.mult).then_inc(rs("hs", s), 1)
                        for t in range(4):
                            v.wait_ge(rs("out", t % 2), 2 * g + t // 2 + 1)
                            carry_waits(v, rs("passed_dve"))
                            xt = X[:, bass.ds(4 * g + t, 1), :].rearrange("p o d -> p (o d)")
                            v.tensor_tensor(xt, xt, ln.banks[t % 2][:, 0:D], ALU.add).then_inc(rs("x_added", t % 2), 1)

        x = Stage(nc, f"m{layer}x")
        xs = x.sem
        with x.ctx:
            tabi, tabf = x.sb("tabi", [TR, NTR, P], I32), x.sb("tabf", [TR, NTR, P])
            tok = x.sb("tok", [P, NB_], U32)
            tokb = x.sb("tokb", [P, R, 1], U32)
            xb = x.sb("xb", [P, R, D])
            xe = x.sb("xe", [P, 2, KD, P])
            w13 = x.sb("w13", [P, R, KD, 2, NBW, BW])
            w2 = x.sb("w2", [BW, R, NBW, D])
            sg, hT = x.sb("sg", [BW, 2, NBW, P]), x.sb("hT", [BW, 2, NBW, P])
            yb = x.sb("yb", [P, R, D])
            psx = [x.ps(f"psx{u}", [P, 512]) for u in range(2)]
            psh = [x.ps(f"psh{u}", [P, 2, NBW, P] if capped else [P, 4, NBW, P]) for u in range(2)]
            psyy = [x.ps(f"psy{u}", [P, 512]) for u in range(2)]
            NR = NB_ // R

            def used(p, j):
                return (R // 2) * p + j // 2

            with nc.Block() as block:
                @block.sync
                def _(sp):
                    sp.dma_start(tabi[:, :, :], slot_tok.rearrange("(n r p) o -> r n (p o)", p=P, r=TR)).then_inc(xs("table"), 16)

                    def weights(p, j):
                        b = R * p + j
                        if not capped:
                            b = sp.value_load(ebrow[0:1, bass.ds(b, 1)], min_val=0, max_val=E - 1)
                        sp.dma_start(w13[:, j].rearrange("p k g n i -> p (k g n i)"), d[f"m{layer}_w13"][bass.ds(b, 1)].rearrange("o p n -> (o p) n")).then_inc(xs("w", j), 16)
                        sp.dma_start(w2[:, j].rearrange("p n d -> p (n d)"), d[f"m{layer}_w2"][bass.ds(b, 1)].rearrange("o p n -> (o p) n")).then_inc(xs("w", j), 16)

                    for j in range(R):
                        weights(0, j)
                    with sp.Fori(0, NR - 1) as p:
                        for j in range(R):
                            sp.wait_ge(xs("y_done", j % 2), used(p, j) + 1)
                            weights(p + 1, j)

                @block.gpsimd
                def _(g):
                    g.wait_ge(xs("tok"), NTR)
                    with g.Fori(0, NR) as p:
                        for j in range(R):
                            g.wait_ge(xs("xb", j), 16 * p)
                            g.wait_ge(xs("xb_used", j), p)
                            carry_waits(g, xs("passed_pool"))
                            g.tensor_copy(tokb[:, j, :], tok[:, bass.ds(R * p + j, 1)]).then_inc(xs("tokb", j), 1)
                            g.wait_ge(xs("tokb", j), p + 1)
                            carry_waits(g, xs("passed_pool"))
                            g.indirect_dma_start(out=xb[:, j, :], out_offset=None, in_=xn,
                                                 in_offset=bass.IndirectOffsetOnAxis(ap=tokb[:, j, :], axis=0)).then_inc(xs("xb", j), 16)

                @block.tensor
                def _(pe):
                    pe.wait_ge(xs("tabf"), 1)
                    for n in range(NTR):
                        pe.transpose(psx[n][:, 0:TR], tabf[:, n, :], ident[0:TR, 0:TR]).then_inc(xs("tok_turned"), 1)
                    pe.wait_ge(xs("tok"), NTR)

                    def turn(p, j):
                        u = j % 2
                        pe.wait_ge(xs("xb", j), 16 * (p + 1))
                        pe.wait_ge(xs("xe", u), used(p, j))
                        for k in range(KD):
                            mm = pe.transpose(psx[u][:, k * P:(k + 1) * P], xb[:, j, k * P:(k + 1) * P], ident[:, :])
                        mm.then_inc(xs("xb_used", j), 1)

                    def hidden(p, j):
                        u = j % 2
                        pe.wait_ge(xs("w", j), 32 * (p + 1))
                        pe.wait_ge(xs("xe", u), used(p, j) + 1)
                        pe.wait_ge(xs("hT", u), used(p, j))
                        for k2 in range(2):
                            for n in range(NBW):
                                for k in range(KD):
                                    mm = pe.matmul(psh[u][0:BW, k2, n, :], w13[:, j, k, k2, n, :], xe[:, u, k, :],
                                                   start=(k == 0), stop=(k == KD - 1))
                        mm.then_inc(xs("h_done", u), 1)

                    def output(p, j):
                        u = j % 2
                        pe.wait_ge(xs("hT", u), used(p, j) + 1)
                        pe.wait_ge(xs("yb", u), used(p, j))
                        for n in range(NBW):
                            mm = pe.matmul(psyy[u][:, 0:D], hT[:, u, n, :], w2[:, j, n, :], start=(n == 0), stop=(n == NBW - 1))
                        mm.then_inc(xs("y_done", u), 1)

                    in_steps(pe, [turn, hidden, output], NR, R)

                @block.scalar
                def _(a):
                    def rows(p, j):
                        u = j % 2
                        a.wait_ge(xs("xb_used", j), p + 1)
                        a.wait_ge(xs("h_done", u), used(p, j))
                        a.activation(xe[:, u].rearrange("p k n -> p (k n)"), psx[u][:, 0:D], ACT.Copy).then_inc(xs("xe", u), 1)

                    def gate(p, j):
                        u = j % 2
                        a.wait_ge(xs("h_done", u), used(p, j) + 1)
                        a.wait_ge(xs("hT", u), used(p, j))
                        a.activation(sg[:, u], psh[u][0:BW, 0], ACT.Silu).then_inc(xs("sg", u), 1)

                    def store(p, j):
                        u = j % 2
                        a.wait_ge(xs("yb", u), used(p, j) + 1)
                        a.dma_start(y.rearrange("(b p) d -> b p d", p=P)[bass.ds(R * p + j, 1)].rearrange("o p d -> (o p) d"), yb[:, j, :]).then_inc(xs("y_stored", j), 16)

                    in_steps(a, [rows, gate, store], NR, R)
                    for j in range(R):
                        a.wait_ge(xs("y_stored", j), 16 * NR)

                @block.vector
                def _(v):
                    v.wait_ge(xs("table"), 16)
                    v.tensor_copy(tabf[:, :, :], tabi[:, :, :]).then_inc(xs("tabf"), 1)
                    for n in range(NTR):
                        v.wait_ge(xs("tok_turned"), n + 1)
                        v.tensor_copy(tok[:, n * TR:(n + 1) * TR], psx[n][:, 0:TR]).then_inc(xs("tok"), 1)

                    def gated(p, j):
                        u = j % 2
                        v.wait_ge(xs("sg", u), used(p, j) + 1)
                        v.wait_ge(xs("y_done", u), used(p, j))
                        v.tensor_tensor(hT[:, u], sg[:, u], psh[u][0:BW, 1], ALU.mult).then_inc(xs("hT", u), 1)

                    def outputs(p, j):
                        u = j % 2
                        v.wait_ge(xs("y_stored", j), 16 * p)
                        v.wait_ge(xs("y_done", u), used(p, j) + 1)
                        v.tensor_copy(yb[:, j, :], psyy[u][:, 0:D]).then_inc(xs("yb", u), 1)

                    in_steps(v, [gated, outputs], NR, R)

        c = Stage(nc, f"m{layer}c")
        cs = c.sem
        with c.ctx:
            gi = c.sb("gi", [P, 2, K], U32)
            yg = c.sb("yg", [P, 2, K, D])
            with nc.Block() as block:
                @block.gpsimd
                def _(g):
                    with g.Fori(0, NT // 2) as p:
                        for u in range(2):
                            g.wait_ge(cs("yg", u), 16 * K * p)
                            g.wait_ge(cs("yg_used", u), p)
                            carry_waits(g, cs("passed_pool"))
                            g.tensor_copy(gi[:, u, :], gslot[:, bass.ds(2 * p + u, 1), :].rearrange("p o k -> p (o k)")).then_inc(cs("gi", u), 1)
                            g.wait_ge(cs("gi", u), p + 1)
                            carry_waits(g, cs("passed_pool"))
                            for k in range(K):
                                g.indirect_dma_start(out=yg[:, u, k, :], out_offset=None, in_=y,
                                                     in_offset=bass.IndirectOffsetOnAxis(ap=gi[:, u, k:k + 1], axis=0)).then_inc(cs("yg", u), 16)

                @block.vector
                def _(v):
                    with v.Fori(0, NT // 2) as p:
                        for u in range(2):
                            t = 2 * p + u
                            xt = X[:, bass.ds(t, 1), :].rearrange("p o d -> p (o d)")
                            v.wait_ge(cs("yg", u), 16 * K * (p + 1))
                            carry_waits(v, cs("passed_dve"))
                            for k in range(K):
                                ins = v.scalar_tensor_tensor(xt, yg[:, u, k, :], wts[:, bass.ds(t, 1), k:k + 1].rearrange("p o k -> p (o k)"),
                                                             xt, ALU.mult, ALU.add)
                                if k < K - 1:
                                    ins.then_inc(cs("acc", u), 1)
                                    v.wait_ge(cs("acc", u), (K - 1) * p + k + 1)
                                    carry_waits(v, cs("passed_dve"))
                            ins.then_inc(cs("yg_used", u), 1)


def stage_moe0(nc, e, d):
    stage_moe(nc, e, d, 0)


def stage_moe1(nc, e, d):
    stage_moe(nc, e, d, 1)


def stage_cross(nc, e, d):
    st = Stage(nc, "x")
    sb, ps, sem = st.sb, st.ps, st.sem
    X, ident = e["X"], e["ident"]
    F2, HP, NR = 2, H // 2, 4
    ISC = float(HK) ** -0.5

    with st.ctx:
        wq, wk, wv, wo = (sb(n, [P, KD, D]) for n in ("wq", "wk", "wv", "wo"))
        bq, bk, bv = (sb(n, [P, F2]) for n in ("bq", "bk", "bv"))
        bo, one = sb("bo", [1, D]), sb("one", [1, P])
        maskr, bm = sb("maskr", [P, SK]), sb("bm", [P, 2])
        xnT, qT = sb("xnT", [P, KD, T]), sb("qT", [P, F2, T])
        c = sb("c", [P, 2, KD, SK])
        kT = sb("kT", [P, 2, F2, SK])
        val = sb("val", [P, 2, 2, D])
        qblk = sb("qblk", [P, 2, F2, 2, S])
        s = sb("s", [P, 2, HP, SK])
        mx, nm, sm, rs_ = (sb(n, [P, 2, HP]) for n in ("mx", "nm", "sm", "rs"))
        pT = sb("pT", [P, 2, HP, 2, P])
        ov, oT = sb("ov", [P, F2, S]), sb("oT", [P, F2, P])

        LOADS = [(wq[:, :, :], d["x_wq"]), (wk[:, :, :], d["x_wk"]), (wv[:, :, :], d["x_wv"]), (wo[:, :, :], d["x_wo"]),
                 (bq[:, :], d["x_bq"]), (bk[:, :], d["x_bk"]), (bv[:, :], d["x_bv"]), (bo[:, :], d["x_bo"]),
                 (one[:, :], d["ones"][0:1, :]), (maskr[0:S, :], d["x_mask"]), (maskr[S:P, :], d["x_mask"]), (bm[:, :], d["pair_mask"])]
        W_ALL = 16 * len(LOADS)

        q = Stage(nc, "xq")
        qs = q.sem
        with q.ctx:
            ln = LayerNorm(q, e, q.ps("psT2", [P, 512]))
            pq = [q.ps(f"pq{n}", [P, GT]) for n in range(2)]
            with nc.Block() as block:
                @block.sync
                def _(sp):
                    for dst, src in LOADS:
                        sp.dma_start(dst, src).then_inc(qs("weights"), 16)
                    sp.wait_ge(qs("weights"), W_ALL)

                @block.tensor
                def _(pe):
                    with pe.Fori(0, NT // 2) as p:
                        for u in range(2):
                            ln.tensor_tile(pe, p, u)
                    pe.wait_ge(qs("weights"), W_ALL)
                    for u in range(2):
                        pe.wait_ge(qs("xnT_ready", u), NT // 2)
                    with pe.Fori(0, NG) as g:
                        for f in range(F2):
                            pe.wait_ge(qs("q_out", f), g)
                            for k in range(KD):
                                mm = pe.matmul(pq[f][:, :], wq[:, k, f * P:(f + 1) * P], xnT[:, k, bass.ds(GT * g, GT)], start=(k == 0), stop=(k == KD - 1))
                            mm.then_inc(qs("q_done", f), 1)

                @block.scalar
                def _(a):
                    ln.scalar_std(a)
                    with a.Fori(0, NT // 2) as p:
                        for u in range(2):
                            ln.scalar_tile(a, p, u, xnT[:, :, bass.ds(P * (2 * p + u), P)])
                    a.wait_ge(qs("weights"), W_ALL)
                    with a.Fori(0, NG) as g:
                        for f in range(F2):
                            a.wait_ge(qs("q_done", f), g + 1)
                            carry_waits(a, qs("passed_act"))
                            a.activation(qT[:, f, bass.ds(GT * g, GT)], pq[f][:, :], ACT.Identity, bias=bq[:, f:f + 1]).then_inc(qs("q_out", f), 1)

                @block.vector
                def _(v):
                    ln.vector_stats(v)
                    with v.Fori(0, NT // 2) as p:
                        for u in range(2):
                            ln.vector_tile(v, p, u)

        psS = ps("psS", [P, NR, F2, SK])
        psP = [ps(f"psP{n}", [P, 512]) for n in range(2)]
        psK = ps("psK", [P, 2, D])
        psO = ps("psO", [P, 512])

        def schedule(eng, start, step, finish):
            start()
            step(0, 0, False, True)
            step(0, 1, False, True)
            with eng.Fori(1, NT - 1) as p:
                step(p, 0, True, True)
                step(p, 1, False, True)
            step(NT - 1, 0, True, False)
            step(NT - 1, 1, False, False)
            finish(NT - 1)

        with nc.Block() as block:
            @block.sync
            def _(sp):
                ctx_v = d["ctxT"].rearrange("(g b) p k n -> g b p k n", b=2)
                with sp.Fori(0, NT) as p:
                    for u in range(2):
                        sp.wait_ge(sem("v_done", u), p)
                        sp.dma_start(c[:, u], ctx_v[bass.ds(p, 1), u].rearrange("o p k n -> (o p) k n")
                                     ).then_inc(sem("ctx", u), 16)

            @block.gpsimd
            def _(g):
                def queries(p, u):
                    g.wait_ge(sem("s_done", u), p)
                    carry_waits(g, sem("passed_pool"))
                    for f in range(F2):
                        ins = g.tensor_tensor(qblk[:, u, f], bc(qT[:, f, bass.ds(P * p + S * u, S)].rearrange("p (o n) -> p o n", o=1), [P, 2, S]),
                                              bc(bm[:, :, None], [P, 2, S]), ALU.mult)
                    ins.then_inc(sem("qblk", u), 1)

                def probs(p, u):
                    g.wait_ge(sem("rsum", u), p + 1)
                    g.tensor_tensor(s[:, u, 4:8, :], s[:, u, 4:8, :], bc(rs_[:, u, 4:8, None], [P, 4, SK]), ALU.mult).then_inc(sem("probs1", u), 1)

                def start():
                    queries(0, 0)
                    queries(0, 1)
                    probs(0, 0)

                def step(p, u, joined, ahead):
                    if ahead:
                        queries(p + 1, u)
                    if u == 0:
                        probs(p, 1)
                    elif ahead:
                        probs(p + 1, 0)

                def finish(p):
                    pass

                schedule(g, start, step, finish)

            @block.tensor
            def _(pe):
                def keys(p, u):
                    pe.wait_ge(sem("ctx", u), 16 * (p + 1))
                    pe.wait_ge(sem("v_out"), 2 * p + u)
                    for f in range(F2):
                        for k in range(KD):
                            mm = pe.matmul(psK[:, f, :], wk[:, k, f * P:(f + 1) * P], c[:, u, k, :], start=(k == 0), stop=(k == KD - 1))
                    mm.then_inc(sem("k_done"), 1)

                def values(p, u):
                    pe.wait_ge(sem("k_out"), 2 * p + u + 1)
                    for t in range(2):
                        for k in range(KD):
                            mm = pe.matmul(psK[:, t, :], c[:, u, k, t * P:(t + 1) * P], wv[:, k, :], start=(k == 0), stop=(k == KD - 1))
                    mm.then_inc(sem("v_done", u), 1)

                def scores(p, u):
                    b = 2 * p + u
                    pe.wait_ge(sem("k_out"), b + 1)
                    pe.wait_ge(sem("qblk", u), p + 1)
                    pe.wait_ge(sem("masked"), b)
                    for f in range(F2):
                        for r in range(NR):
                            mm = pe.matmul(psS[:, r, f, :], qblk[32 * r:32 * r + 32, u, f].rearrange("p a n -> p (a n)"),
                                           kT[32 * r:32 * r + 32, u, f, :], start=True, stop=True)
                    mm.then_inc(sem("s_done", u), 1)

                def turn(p, u, h):
                    b = 2 * p + u
                    pe.wait_ge(sem(f"probs{h}", u), p + 1)
                    for n in range(2):
                        pe.wait_ge(sem("pT", n), 2 * b + h)
                        for i in range(4):
                            hp, t = 4 * h + 2 * n + i // 2, i % 2
                            mm = pe.transpose(psP[n][:, i * P:(i + 1) * P], s[:, u, hp, t * P:(t + 1) * P], ident[:, :])
                        mm.then_inc(sem("p_turned", n), 1)

                def project(p):
                    pe.wait_ge(sem("taken0"), 2 * p + 2)
                    pe.matmul(psP[1][:, 0:D], one[:, :], bo[:, :], start=True, stop=False)
                    for f in range(F2):
                        mm = pe.matmul(psP[1][:, 0:D], oT[:, f, :], wo[:, f, :], start=False, stop=(f == F2 - 1))
                    mm.then_inc(sem("y_done"), 1)

                def start():
                    for u in range(2):
                        keys(0, u)
                        scores(0, u)
                        values(0, u)

                def step(p, u, joined, ahead):
                    b = 2 * p + u
                    pe.wait_ge(sem("taken1"), b)
                    if u == 1:
                        pe.wait_ge(sem("x_added"), p)
                    turn(p, u, 0)
                    if ahead:
                        keys(p + 1, u)
                    turn(p, u, 1)
                    if ahead:
                        scores(p + 1, u)
                    for n in range(2):
                        pe.wait_ge(sem("pT", n), 2 * b + 2)
                    if joined:
                        project(p - 1)
                    pe.wait_ge(sem("v_out"), b + 1)
                    pe.wait_ge(sem("taken0"), b)
                    for f in (1, 0):
                        out = (psO if f == 0 else psP[0])[:, :].rearrange("p (r n) -> p r n", r=NR)
                        for t in range(2):
                            mm = pe.matmul(out, val[:, u, t, f * P:(f + 1) * P],
                                           pT[:, u].rearrange("p (r f) t n -> p f t r n", f=F2)[:, f, t], start=(t == 0), stop=(t == 1))
                        mm.then_inc(sem(f"o_done{f}", u), 1)
                    if ahead:
                        values(p + 1, u)

                def finish(p):
                    project(p)

                schedule(pe, start, step, finish)

            @block.scalar
            def _(a):
                def keys(p, u):
                    a.wait_ge(sem("s_done", u), p)
                    a.wait_ge(sem("k_done"), 2 * p + u + 1)
                    for f in range(F2):
                        ins = a.activation(kT[:, u, f, :], psK[:, f, :], ACT.Identity, bias=bk[:, f:f + 1])
                    ins.then_inc(sem("k_out"), 1)

                def values(p, u):
                    a.wait_ge(sem("o_done0", u), p)
                    a.wait_ge(sem("v_done", u), p + 1)
                    a.activation(val[:, u], psK[:, :, :], ACT.Copy).then_inc(sem("v_out"), 1)

                def exps(p, u):
                    a.wait_ge(sem("nm", u), p + 1)
                    a.wait_ge(sem("rsum", u), p)
                    for hp in range(HP):
                        ins = a.activation(s[:, u, hp, :], s[:, u, hp, :], ACT.Exp, bias=nm[:, u, hp:hp + 1], scale=ISC,
                                           accum_out=sm[:, u, hp:hp + 1])
                    ins.then_inc(sem("exp", u), 1)

                def turned(p, u, h):
                    a.wait_ge(sem("p_turned", 1), 2 * (2 * p + u) + h + 1)
                    a.activation(pT[:, u, 4 * h + 2:4 * h + 4].rearrange("p h t n -> p (h t n)"), psP[1][:, :], ACT.Copy).then_inc(sem("pT", 1), 1)

                def finish(p):
                    pass

                def start():
                    for u in range(2):
                        keys(0, u)
                        values(0, u)
                    exps(0, 0)

                def step(p, u, joined, ahead):
                    turned(p, u, 0)
                    if ahead:
                        keys(p + 1, u)
                    turned(p, u, 1)
                    if u == 0:
                        exps(p, 1)
                    elif ahead:
                        exps(p + 1, 0)
                    if ahead:
                        values(p + 1, u)

                schedule(a, start, step, finish)

            @block.vector
            def _(v):
                def scores(p, u, ahead):
                    b = 2 * p + u
                    v.wait_ge(sem("s_done", u), p + 1)
                    if ahead:
                        v.wait_ge(sem("p_turned", 1), 2 * b - 2)
                    carry_waits(v, sem("passed_dve"))
                    for hp in range(HP):
                        r, f = hp // 2, hp % 2
                        ins = v.tensor_tensor_reduce(s[:, u, hp, :], psS[:, r, f, :], maskr[:, :], 1.0, -3.0e38, ALU.add, ALU.max,
                                                     mx[:, u, hp:hp + 1])
                    ins.then_inc(sem("masked"), 1)
                    v.wait_ge(sem("masked"), b + 1)
                    v.tensor_scalar(nm[:, u, :], mx[:, u, :], -ISC, None, ALU.mult).then_inc(sem("nm", u), 1)

                def turned(p, u, h):
                    v.wait_ge(sem("p_turned", 0), 2 * (2 * p + u) + h + 1)
                    v.tensor_copy(pT[:, u, 4 * h:4 * h + 2].rearrange("p h t n -> p (h t n)"), psP[0][:, :]).then_inc(sem("pT", 0), 1)

                def probs(p, u):
                    v.wait_ge(sem("exp", u), p + 1)
                    v.reciprocal(rs_[:, u, :], sm[:, u, :]).then_inc(sem("rsum", u), 1)
                    v.wait_ge(sem("rsum", u), p + 1)
                    v.tensor_tensor(s[:, u, 0:4, :], s[:, u, 0:4, :], bc(rs_[:, u, 0:4, None], [P, 4, SK]), ALU.mult).then_inc(sem("probs0", u), 1)

                def take(p, u):
                    b = 2 * p + u
                    v.wait_ge(sem("y_done"), p)
                    for f in (1, 0):
                        src = (psO if f == 0 else psP[0])[:, :].rearrange("p (r h n) -> p r h n", r=NR, h=2)
                        v.wait_ge(sem(f"o_done{f}", u), p + 1)
                        for r in range(NR):
                            q = slice(32 * r, 32 * r + 32)
                            ins = v.tensor_scalar(ov[q, f, :], src[q, r, 0, :], bm[q, 0:1], bv[q, f:f + 1], ALU.mult, ALU.add)
                        ins.then_inc(sem(f"first{f}"), 1)
                        v.wait_ge(sem(f"first{f}"), b + 1)
                        for r in range(NR):
                            q = slice(32 * r, 32 * r + 32)
                            ins = v.scalar_tensor_tensor(oT[q, f, S * u:S * u + S], src[q, r, 1, :], bm[q, 1:2], ov[q, f, :], ALU.mult, ALU.add)
                        ins.then_inc(sem(f"taken{f}"), 1)

                def start():
                    scores(0, 0, False)
                    scores(0, 1, False)
                    probs(0, 0)

                def step(p, u, joined, ahead):
                    turned(p, u, 0)
                    turned(p, u, 1)
                    if u == 0:
                        probs(p, 1)
                    elif ahead:
                        probs(p + 1, 0)
                    if ahead:
                        scores(p + 1, u, True)
                    if joined:
                        finish(p - 1)
                    take(p, u)

                def finish(p):
                    v.wait_ge(sem("y_done"), p + 1)
                    carry_waits(v, sem("passed_dve"))
                    xt = X[:, bass.ds(p, 1), :].rearrange("p o d -> p (o d)")
                    v.tensor_tensor(xt, xt, psP[1][:, 0:D], ALU.add).then_inc(sem("x_added"), 1)

                schedule(v, start, step, finish)


def stage_self(nc, e, d):
    st = Stage(nc, "s")
    sb, ps, sem = st.sb, st.ps, st.sem
    X, ident = e["X"], e["ident"]
    F2, HP, NR = 2, H // 2, 4
    ISC = float(HK) ** -0.5

    with st.ctx:
        wq, wqs, wk, wks, wv, wo = (sb(n, [P, KD, D]) for n in ("wq", "wqs", "wk", "wks", "wv", "wo"))
        cos, sin = sb("cos", [P, S]), sb("sin", [P, S])
        causal, bm, hm = sb("causal", [P, S]), sb("bm", [P, 2]), sb("hm", [P, 2])
        xnT = sb("xnT", [P, KD, T])
        qT, kT = sb("qT", [P, F2, T]), sb("kT", [P, F2, T])
        vall = sb("vall", [P, NT, D])

        q = Stage(nc, "sq")
        qs = q.sem
        with q.ctx:
            ln = LayerNorm(q, e, q.ps("psT2", [P, 512]))
            xts = q.sb("xts", [P, 2, KD, P])
            ra = q.sb("ra", [P, 2, 2, GT])
            psv = q.ps("psv", [P, 512])
            pr = [[q.ps(f"pr{n}{m}", [P, GT]) for m in range(2)] for n in range(2)]

            LOADS = [(wq[:, :, :], d["s_wq"]), (wqs[:, :, :], d["s_wqs"]), (wk[:, :, :], d["s_wk"]), (wks[:, :, :], d["s_wks"]),
                     (wv[:, :, :], d["s_wv"]), (wo[:, :, :], d["s_wo"]), (cos[:, :], d["s_cos"]), (sin[:, :], d["s_sin"]),
                     (causal[:, :], d["s_causal"]), (bm[:, :], d["pair_mask"]), (hm[:, :], d["half_mask"])]
            W_ALL = 16 * len(LOADS)
            UNITS = [(w, ws, out, f) for w, ws, out in ((wq, wqs, qT), (wk, wks, kT)) for f in range(F2)]

            with nc.Block() as block:
                @block.sync
                def _(sp):
                    for dst, src in LOADS:
                        sp.dma_start(dst, src).then_inc(qs("weights"), 16)
                    sp.wait_ge(qs("weights"), W_ALL)

                @block.tensor
                def _(pe):
                    def values(p, u):
                        pe.wait_ge(qs("weights"), W_ALL)
                        pe.wait_ge(qs("xts", u), p + 1)
                        pe.wait_ge(qs("v_out", 1 - u), p + u)
                        for k in range(KD):
                            mm = pe.matmul(psv[:, 0:D], xts[:, u, k, :], wv[:, k, :], start=(k == 0), stop=(k == KD - 1))
                        mm.then_inc(qs("v_done", u), 1)

                    in_steps(pe, [lambda p, u: ln.tensor_tile(pe, p, u), values], NT // 2, 2)
                    with pe.Fori(0, NG) as g:
                        for i, (w, ws, _, f) in enumerate(UNITS):
                            n = i % 2
                            pe.wait_ge(qs("turned", n), 4 * g + 2 * (i // 2))
                            for m, ww in enumerate((w, ws)):
                                for k in range(KD):
                                    mm = pe.matmul(pr[n][m][:, :], ww[:, k, f * P:(f + 1) * P], xnT[:, k, bass.ds(GT * g, GT)], start=(k == 0), stop=(k == KD - 1))
                            mm.then_inc(qs("qk", n), 1)

                @block.scalar
                def _(a):
                    ln.scalar_std(a)

                    def rows(p, u):
                        a.wait_ge(qs("v_done", u), p)
                        ln.scalar_tile(a, p, u, xnT[:, :, bass.ds(P * (2 * p + u), P)])
                        a.activation(xts[:, u], ln.banks[u][:, 0:D].rearrange("p (k n) -> p k n", k=KD), ACT.Copy).then_inc(qs("xts", u), 1)

                    def values(p, u):
                        a.wait_ge(qs("v_done", u), p + 1)
                        carry_waits(a, qs("passed_act"))
                        a.activation(vall[:, bass.ds(2 * p + u, 1), :].rearrange("p o d -> p (o d)"), psv[:, 0:D], ACT.Copy).then_inc(qs("v_out", u), 1)

                    in_steps(a, [rows, values], NT // 2, 2)

                @block.vector
                def _(v):
                    ln.vector_stats(v)
                    with v.Fori(0, NT // 2) as p:
                        for u in range(2):
                            ln.vector_tile(v, p, u)
                    v.wait_ge(qs("weights"), W_ALL)
                    with v.Fori(0, NG) as g:
                        for i, (_, _, out, f) in enumerate(UNITS):
                            n = i % 2
                            v.wait_ge(qs("qk", n), 2 * g + i // 2 + 1)
                            shape = [P, GT // S, S]
                            for m, tab in enumerate((cos, sin)):
                                v.tensor_tensor(ra[:, n, m, :].rearrange("p (b s) -> p b s", s=S), pr[n][m][:, :].rearrange("p (b s) -> p b s", s=S),
                                                bc(tab[:, None, :], shape), ALU.mult).then_inc(qs("turned", n), 1)
                            v.wait_ge(qs("turned", n), 4 * g + 2 * (i // 2) + 2)
                            carry_waits(v, qs("passed_dve"))
                            v.tensor_tensor(out[:, f, bass.ds(GT * g, GT)], ra[:, n, 0, :], ra[:, n, 1, :], ALU.add).then_inc(qs("rotated", n), 1)

        kb = sb("kb", [P, 2, F2, P])
        vb = sb("vb", [P, 2, 2, D])
        qblk = sb("qblk", [P, 2, F2, 2, 2, S])
        s = sb("s", [P, 2, NR, F2, 2, S])
        mx = sb("mx", [P, 2, 4, 4 * NR])
        pT = sb("pT", [P, 2, HP, P])
        oc, oT = sb("oc", [P, D]), sb("oT", [P, F2, P])
        psS = ps("psS", [P, NR, 512])
        psP = ps("psP", [P, 2, 512])
        psO = ps("psO", [P, HP, 2, 32])
        NP2 = NT // 2

        def schedule(eng, start, step, finish):
            start()
            step(0, 0, False, True)
            step(0, 1, True, True)
            with eng.Fori(1, NP2 - 1) as p:
                step(p, 0, True, True)
                step(p, 1, True, True)
            step(NP2 - 1, 0, True, False)
            step(NP2 - 1, 1, True, False)
            finish(NP2 - 1, 1)

        def before(p, u):
            return (p, 0) if u == 1 else (p - 1, 1)

        with nc.Block() as block:
            @block.gpsimd
            def _(g):
                def queries(p, u):
                    t = 2 * p + u
                    g.wait_ge(sem("s_done", u), p)
                    carry_waits(g, sem("passed_pool"))
                    for f in range(F2):
                        for b in range(2):
                            g.tensor_tensor(qblk[:, u, f, b], bc(qT[:, f, bass.ds(P * t + S * b, S)].rearrange("p (o n) -> p o n", o=1), [P, 2, S]),
                                            bc(bm[:, :, None], [P, 2, S]), ALU.mult)
                    g.tensor_copy(kb[:, u], kT[:, :, bass.ds(P * t, P)]).then_inc(sem("ready", u), 1)

                def start():
                    queries(0, 0)
                    queries(0, 1)

                def step(p, u, joined, ahead):
                    g.wait_ge(sem("o_done", u), p)
                    carry_waits(g, sem("passed_pool"))
                    g.tensor_tensor(vb[:, u], bc(vall[:, bass.ds(2 * p + u, 1), :], [P, 2, D]), bc(hm[:, :, None], [P, 2, D]),
                                    ALU.mult).then_inc(sem("v_ready", u), 1)
                    if ahead:
                        queries(p + 1, u)

                def finish(p, u):
                    pass

                schedule(g, start, step, finish)

            @block.tensor
            def _(pe):
                def scores(p, u):
                    pe.wait_ge(sem("ready", u), p + 1)
                    pe.wait_ge(sem("masked", 1 - u), p + u)
                    for f in range(F2):
                        for b in range(2):
                            for r in range(NR):
                                o = (2 * f + b) * S
                                mm = pe.matmul(psS[:, r, o:o + S], qblk[32 * r:32 * r + 32, u, f, b].rearrange("p a n -> p (a n)"),
                                               kb[32 * r:32 * r + 32, u, f, S * b:S * b + S], start=True, stop=True)
                    mm.then_inc(sem("s_done", u), 1)

                def turn_oc(p, u, last=False):
                    pe.wait_ge(sem("oc"), 2 * p + u + 1)
                    if not last:
                        pe.wait_ge(sem("pT", 0), 2 * p + u + 2)
                    for f in range(F2):
                        mm = pe.transpose(psP[:, 0, f * P:(f + 1) * P], oc[:, f * P:(f + 1) * P], ident[:, :])
                    mm.then_inc(sem("oc_turned"), 1)

                def project(p, u, last=False):
                    pe.wait_ge(sem("oT"), 2 * p + u + 1)
                    if not last:
                        pe.wait_ge(sem("pT", 1), 2 * p + u + 2)
                    for f in range(F2):
                        mm = pe.matmul(psP[:, 1, 0:D], oT[:, f, :], wo[:, f, :], start=(f == 0), stop=(f == F2 - 1))
                    mm.then_inc(sem("y_done"), 1)

                def start():
                    scores(0, 0)
                    scores(0, 1)

                def step(p, u, joined, ahead):
                    t = 2 * p + u
                    pe.wait_ge(sem("exp", u), p + 1)
                    if joined:
                        pe.wait_ge(sem("oT"), t - 1)
                        pe.wait_ge(sem("x_added"), t - 1)
                    for h in range(2):
                        pe.wait_ge(sem("pT", h), t)
                        for i in range(4):
                            hp = 4 * h + i
                            mm = pe.transpose(psP[:, h, i * P:(i + 1) * P], s[:, u, hp // 2, hp % 2].rearrange("p b k -> p (b k)"), ident[:, :])
                        mm.then_inc(sem("p_turned", h), 1)
                    if joined:
                        turn_oc(*before(p, u))
                    if ahead:
                        scores(p + 1, u)
                    if joined:
                        project(*before(p, u))
                    for h in range(2):
                        pe.wait_ge(sem("pT", h), t + 1)
                    pe.wait_ge(sem("v_ready", u), p + 1)
                    pe.wait_ge(sem("oc"), t)
                    for hp in range(HP):
                        r, f = hp // 2, hp % 2
                        mm = pe.matmul(psO[:, hp], pT[:, u, hp, :],
                                       vb[:, u, :, f * P + 32 * r:f * P + 32 * r + 32], start=True, stop=True)
                    mm.then_inc(sem("o_done", u), 1)

                def finish(p, u):
                    turn_oc(p, u, True)
                    project(p, u, True)

                schedule(pe, start, step, finish)

            @block.scalar
            def _(a):
                def exps(p, u):
                    a.wait_ge(sem("shifted", u), p + 1)
                    a.activation(s[:, u], s[:, u], ACT.Exp, scale=ISC).then_inc(sem("exp", u), 1)

                def start():
                    exps(0, 0)

                def step(p, u, joined, ahead):
                    a.wait_ge(sem("p_turned", 0), 2 * p + u + 1)
                    a.activation(pT[:, u, 0:4].rearrange("p h n -> p (h n)"), psP[:, 0, :], ACT.Copy).then_inc(sem("pT", 0), 1)
                    if joined:
                        finish(*before(p, u))
                    if u == 0:
                        exps(p, 1)
                    elif ahead:
                        exps(p + 1, 0)

                def finish(p, u):
                    t = 2 * p + u
                    a.wait_ge(sem("y_done"), t)
                    a.wait_ge(sem("oc_turned"), t + 1)
                    a.activation(oT[:, :, :].rearrange("p f n -> p (f n)"), psP[:, 0, 0:D], ACT.Copy).then_inc(sem("oT"), 1)

                schedule(a, start, step, finish)

            @block.vector
            def _(v):
                def shifted(p, u, ahead):
                    v.wait_ge(sem("s_done", u), p + 1)
                    if ahead:
                        v.wait_ge(sem("p_turned", 1), 2 * p + u - 1)
                    carry_waits(v, sem("passed_dve"))
                    sv = s[:, u].rearrange("p r f b k -> p r (f b) k")
                    flat = s[:, u].rearrange("p r f b k -> p (r f b) k")
                    v.tensor_tensor(sv, psS[:, :, 0:4 * S].rearrange("p r (o k) -> p r o k", k=S), bc(causal[:, None, None, :], [P, NR, 4, S]),
                                    ALU.add).then_inc(sem("masked", u), 1)
                    v.wait_ge(sem("masked", u), p + 1)
                    v.tensor_reduce(mx[:, u, 0, :], flat, AX_X, ALU.max).then_inc(sem("max", u), 1)
                    v.wait_ge(sem("max", u), p + 1)
                    v.tensor_tensor(flat, flat, bc(mx[:, u, 0, :, None], [P, 4 * NR, S]), ALU.subtract).then_inc(sem("shifted", u), 1)

                def start():
                    shifted(0, 0, False)
                    shifted(0, 1, False)

                def step(p, u, joined, ahead):
                    t = 2 * p + u
                    v.wait_ge(sem("exp", u), p + 1)
                    v.tensor_reduce(mx[:, u, 1, :], s[:, u].rearrange("p r f b k -> p (r f b) k"), AX_X, ALU.add).then_inc(sem("sum", u), 1)
                    v.wait_ge(sem("p_turned", 1), t + 1)
                    v.tensor_copy(pT[:, u, 4:8].rearrange("p h n -> p (h n)"), psP[:, 1, :]).then_inc(sem("pT", 1), 1)
                    v.wait_ge(sem("sum", u), p + 1)
                    v.reciprocal(mx[:, u, 2, :], mx[:, u, 1, :]).then_inc(sem("rsum", u), 1)
                    v.wait_ge(sem("rsum", u), p + 1)
                    if joined:
                        finish(*before(p, u))
                    if ahead:
                        shifted(p + 1, u, True)
                    v.wait_ge(sem("oc_turned"), t)
                    v.wait_ge(sem("o_done", u), p + 1)
                    for b in range(2):
                        for h2 in range(2):
                            lo = S * h2
                            src = psO[lo:lo + S, :, b, HK * h2:HK * h2 + HK].rearrange("p (r f) c -> p r f c", f=F2)
                            w = bc(mx[lo:lo + S, u, 2, :].rearrange("p (r f b) -> p r f b", f=F2, b=2)[:, :, :, b:b + 1], [S, NR, F2, HK])
                            out = oc[S * b:S * b + S, :].rearrange("p (f r c) -> p r f c", f=F2, r=NR)[:, :, :, HK * h2:HK * h2 + HK]
                            ins = v.tensor_tensor(out, src, w, ALU.mult)
                    ins.then_inc(sem("oc"), 1)

                def finish(p, u):
                    t = 2 * p + u
                    v.wait_ge(sem("y_done"), t + 1)
                    carry_waits(v, sem("passed_dve"))
                    xt = X[:, bass.ds(t, 1), :].rearrange("p o d -> p (o d)")
                    v.tensor_tensor(xt, xt, psP[:, 1, 0:D], ALU.add).then_inc(sem("x_added"), 1)

                schedule(v, start, step, finish)


def build(nc, d, out, stages):
    ctx = ExitStack()
    with ctx:
        X = ctx.enter_context(nc.sbuf_tensor("X", [P, NT, D], F32))
        ident = ctx.enter_context(nc.sbuf_tensor("ident", [P, P], F32))
        loaded = ctx.enter_context(nc.semaphore("x_loaded"))
        stored = ctx.enter_context(nc.semaphore("x_stored"))
        e = {"X": X, "ident": ident}
        with nc.Block() as block:
            @block.sync
            def _(sp):
                sp.dma_start(X[:, :, :], d["x"].rearrange("(t p) d -> p t d", p=P)).then_inc(loaded, 16)
                sp.dma_start(ident[:, :], d["ident"]).then_inc(loaded, 16)
                sp.wait_ge(loaded, 32)
        for s in stages:
            with nc.cleanup_on_exit():
                s(nc, e, d)
        with nc.Block() as block:
            @block.sync
            def _(sp):
                sp.dma_start(out.rearrange("(t p) d -> p t d", p=P), X[:, :, :]).then_inc(stored, 16)
                sp.wait_ge(stored, 16)


def rope_tables(pos, dim, base=10000.0):
    half = dim // 2
    inv = (np.float32(1.0) / np.power(np.float32(base), np.arange(half, dtype=np.float32) / np.float32(half))).astype(np.float32)
    ang = pos.astype(np.float32)[:, None] * inv
    c, s = np.cos(ang).astype(np.float32), np.sin(ang).astype(np.float32)
    return np.concatenate([c, c], 1), np.concatenate([-s, s], 1)


def layout(i):
    f = {}
    c = np.ascontiguousarray
    f["x"] = c(i["x"].reshape(T, D))
    f["ident"] = np.eye(P, dtype=np.float32)
    ctx = i["ctx_1024"]
    f["ctxT"] = c(ctx.reshape(B, SK, KD, P).transpose(0, 3, 2, 1))
    f["seg"] = c(i["itok_BxS_0_511"].reshape(NT, P).T)
    w = i["L0_xattn_w_kv_comp"]
    f["kcompT"] = c(w.T)
    f["kcomp"] = c(w.reshape(KD, P, KVC).transpose(1, 0, 2))
    f["krope"] = c(i["L0_xattn_w_k_rope"])
    f["qup"] = c(i["L0_xattn_w_q_up"].reshape(QC, H, HD).transpose(2, 1, 0))
    f["kup"] = c(i["L0_xattn_w_k_up"].reshape(KVC, H, HD).transpose(2, 1, 0))
    f["vup"] = c(i["L0_xattn_w_v_up"].reshape(KVC, H, HD).transpose(2, 1, 0))
    f["wout"] = c(i["L0_xattn_w_out"].reshape(H, HD, D).transpose(1, 0, 2))
    f["wqd"] = c(i["L0_xattn_w_q_down"].reshape(KD, P, QC).transpose(1, 0, 2))
    f["qrope"] = c(i["L0_xattn_w_q_rope"].reshape(QC, H, RD))
    ck, sk = rope_tables(np.arange(SK), RD)
    f["cosk"] = c(np.tile(ck.reshape(2, P, RD), (2, 1, 1)).transpose(1, 0, 2))
    f["sink"] = c(np.tile(sk.reshape(2, P, RD), (2, 1, 1)).transpose(1, 0, 2))
    cq, sq = rope_tables(np.arange(P) % S, RD)
    f["cosq"], f["sinq"] = cq, -sq
    b = np.arange(T).reshape(NT, P).T // S
    f["rows"] = c(np.stack([b * SK, KROWS + b], 1).astype(np.float32))
    f["meanw"] = np.full((P, 1), 1.0 / SK, np.float32)
    f["b_win"] = c(i["L0_attn_W_in"].T.reshape(KD, P, 2 * DI).transpose(1, 0, 2))
    f["b_convw"] = c(i["L0_attn_conv_w"].reshape(NCH, P, KC).transpose(1, 0, 2))
    f["b_convb"] = c(i["L0_attn_conv_b"].reshape(NCH, P).T)
    f["b_wx"] = c(i["L0_attn_W_x"].T.reshape(NCH, P, DTR + 2 * NST).transpose(1, 0, 2))
    f["b_wdt"] = c(i["L0_attn_W_dt"].T)
    f["b_bdt"] = c(i["L0_attn_b_dt"].reshape(NCH, P).T)
    f["b_alog"] = c(i["L0_attn_A_log"].reshape(NCH, P, NST).transpose(1, 0, 2))
    f["b_dp"] = c(i["L0_attn_Dp"].reshape(NCH, P).T)
    f["b_wout"] = c(i["L0_attn_W_out"].T.reshape(NCH, P, D).transpose(1, 0, 2))
    f["iota_e"] = np.arange(E, dtype=np.float32)
    f["slot_base"] = np.arange(E, dtype=np.float32) * CAP0
    f["iota_b"] = c(np.arange(2 * P, dtype=np.float32).reshape(2, P).T)
    f["tokid"] = c(np.arange(T, dtype=np.int32).reshape(NT, P).T)
    f["ltri"] = np.triu(np.ones((P, P), np.float32), 1)
    f["ones"] = np.ones((P, P), np.float32)

    def by_row(w):
        return w.reshape(KD, P, -1).transpose(1, 0, 2)

    f["m0_gw"], f["m0_gb"] = c(by_row(i["L0_ffn_gate_w"].T)), c(i["L0_ffn_gate_b"])
    w1, w3 = (i[f"L0_ffn_{n}"].reshape(E, 2, IH, KD, P) for n in ("w1", "w3"))
    f["m0_w13"] = c(np.stack([w1, w3], 1).transpose(0, 5, 4, 1, 2, 3).reshape(E, P, -1))
    f["m0_w2"] = c(i["L0_ffn_w2"].reshape(E, D, 2, IH).transpose(0, 3, 2, 1).reshape(E, IH, -1))
    w1, w3 = (i[f"L0_ffn_{n}"].reshape(SB0, IH, KD, P) for n in ("ws1", "ws3"))
    f["m0_ws13"] = c(np.stack([w1, w3], 0).transpose(4, 3, 0, 1, 2))
    f["m0_ws2"] = c(i["L0_ffn_ws2"].reshape(D, SB0, IH).transpose(2, 1, 0))
    f["m1_gw"], f["m1_gb"] = c(by_row(i["L1_ffn_w_router"])), c(i["L1_ffn_b_router"])
    w1, w3 = (i[f"L1_ffn_{n}"].reshape(E, KD, P, F1) for n in ("we_gate", "we_up"))
    f["m1_w13"] = c(np.stack([w1, w3], 1).transpose(0, 3, 2, 1, 4).reshape(E, P, -1))
    f["m1_w2"] = c(i["L1_ffn_we_down"])
    w1, w3 = (i[f"L1_ffn_{n}"].reshape(KD, P, F1) for n in ("ws_gate", "ws_up"))
    f["m1_ws13"] = c(np.stack([w1, w3], 0).transpose(2, 1, 0, 3).reshape(P, KD, 2, 1, F1))
    f["m1_ws2"] = c(i["L1_ffn_ws_down"].reshape(F1, 1, D))
    for n in "qkv":
        f[f"x_w{n}"] = c(by_row(i[f"L1_xattn_W{n}"].transpose(1, 0, 2).reshape(D, D)))
        f[f"x_b{n}"] = c(i[f"L1_xattn_b{n}"].reshape(2, P).T)
    f["x_wo"] = c(by_row(i["L1_xattn_Wo"].T))
    f["x_bo"] = c(i["L1_xattn_bo"].reshape(1, D))
    f["x_mask"] = c(i["fside_SxS2_0"])
    f["pair_mask"] = (np.arange(P)[:, None] // HK % 2 == np.arange(2)).astype(np.float32)
    f["half_mask"] = (np.arange(P)[:, None] // S == np.arange(2)).astype(np.float32)
    swap = np.arange(D).reshape(H, 2, HK // 2)[:, ::-1].reshape(D)
    for n in "qk":
        w = i[f"L1_attn_W{n}"]
        f[f"s_w{n}"], f[f"s_w{n}s"] = c(by_row(w.T)), c(by_row(w[swap].T))
    f["s_wv"], f["s_wo"] = c(by_row(i["L1_attn_Wv"].T)), c(by_row(i["L1_attn_Wo"].T))
    cs, sn = rope_tables(np.arange(S), HK)
    f["s_cos"], f["s_sin"] = c(np.tile(cs.T, (P // HK, 1))), c(np.tile(sn.T, (P // HK, 1)))
    f["s_causal"] = np.where(np.arange(S)[None, :] > np.arange(P)[:, None] % S, NEG, 0.0).astype(np.float32)
    return f


STAGES = [stage_mla, stage_mamba, stage_moe0, stage_cross, stage_self, stage_moe1]
SCRATCH = {"key_table": ([KROWS + B, KVC + RD], F32), "bc_rows": ([NG, 2 * NST, GT], F32),
           "slot_tok0": ([SLOTS0, 1], I32), "slot_tok1": ([SLOTS1, 1], I32), "xn0": ([T, D], F32), "xn1": ([T, D], F32),
           "y0": ([SLOTS0, D], F32), "y1": ([SLOTS1, D], F32)}


def kernel(**inputs):
    import concourse.bacc as bacc
    from concourse.bass_utils import run_bass_kernel_spmd

    nc = bacc.Bacc("TRN2", target_bir_lowering=False, num_devices=1)
    arrays = layout({k: np.asarray(v) for k, v in inputs.items()})
    d = {n: nc.dram_tensor(f"in_{n}", a.shape, mybir.dt.from_np(a.dtype), kind="ExternalInput").ap()
         for n, a in arrays.items()}
    for n, (shape, dt) in SCRATCH.items():
        d[n] = nc.dram_tensor(f"scratch_{n}", shape, dt).ap()
    out = nc.dram_tensor("out_x", [T, D], F32, kind="ExternalOutput").ap()
    build(nc, d, out, STAGES)
    r = run_bass_kernel_spmd(nc, [{f"in_{n}": a for n, a in arrays.items()}], core_ids=[0])
    return r.results[0]["out_x"].reshape(B, S, D)
```
